# Optimizing a Trainium2 kernel written in Bass

```python
import numpy as np
import jax
import jax.numpy as jnp

def _softmax(x, axis=-1):
    return jax.nn.softmax(x, axis=axis)

def _gelu(x):
    return jax.nn.gelu(x, approximate=True)

def _silu(x):
    return jax.nn.silu(x)

def _sigmoid(x):
    return jax.nn.sigmoid(x)

def _layernorm(x, axis=-1, eps=1e-05):
    m = jnp.mean(x, axis=axis, keepdims=True)
    v = jnp.var(x, axis=axis, keepdims=True)
    return (x - m) / jnp.sqrt(v + eps)

def _scatter_add(tgt, idx, src, axis=0):
    return tgt.at[idx].add(src)

def _segment_sum(src, seg, n):
    return jax.ops.segment_sum(src, seg, n)
kernel_name = 'mk_gps_d2_gnn_r32_fbbe38'

def setup_inputs(seed: int=0):
    np.random.seed(seed)
    _w = jnp.asarray

    def _rec_inputs():
        import jax
        import jax.numpy as jnp
        _gk = jax.random.key(seed)
        x = -0.0002928 + 1 * jax.random.normal(jax.random.fold_in(_gk, 1), (256, 512), jnp.float32)
        _s = jax.random.randint(jax.random.fold_in(_gk, 2), (2048,), 0, 256, jnp.int32)
        _d = jax.random.randint(jax.random.fold_in(_gk, 3), (2048,), 0, 256, jnp.int32)
        _loop = jnp.arange(256, dtype=jnp.int32)
        src = jnp.concatenate([_s, _d, _loop])
        dst = jnp.concatenate([_d, _s, _loop])
        _o = jnp.argsort(dst, stable=True)
        src = src[_o]
        dst = dst[_o]
        edge_weight = jax.random.uniform(jax.random.fold_in(_gk, 12), (4352,), jnp.float32, 0.0, 0.999999)
        return (x, src, dst, edge_weight)
    x, src, dst, edge_weight = _rec_inputs()

    def _L0_gnn_setup():
        import jax, jax.numpy as jnp
        import numpy as np
        N = 256
        C_IN = 512
        C_OUT = 512
        E_RAND = 8192
        key = jax.random.key(seed)
        k1, k2, k3, k4 = jax.random.split(key, 4)
        node_feats = jax.random.normal(k1, (N, C_IN), dtype=jnp.float32)
        rand_edges = jax.random.randint(k2, (2, E_RAND), 0, N, dtype=jnp.int64)
        self_loops = jnp.tile(jnp.arange(N, dtype=jnp.int64)[None, :], (2, 1))
        edge_index = jnp.concatenate([rand_edges, self_loops], axis=1)
        W = jax.random.normal(k3, (C_OUT, C_IN), dtype=jnp.float32) * (1.0 / np.sqrt(C_IN))
        b = jax.random.normal(k4, (C_OUT,), dtype=jnp.float32) * 0.01
        return {'node_feats': node_feats, 'edge_index': edge_index, 'W': W, 'b': b}
    _L0_gnn_all = _L0_gnn_setup()
    _L0_gnn_in = {k: v for k, v in _L0_gnn_all.items() if k in ('W', 'b')}
    del _L0_gnn_all

    def _L0_mix_setup():
        import jax, jax.numpy as jnp
        import numpy as np
        B, S, H = (4, 256, 512)
        NH, HD = (8, 64)
        FD = HD // 2
        key = jax.random.key(seed)
        k1, k2, k3, k4 = jax.random.split(key, 4)
        x = jax.random.normal(k1, (B, S, H), dtype=jnp.float32)
        W_qkv = jax.random.normal(k2, (H, 3 * H), dtype=jnp.float32) * (1.0 / np.sqrt(H))
        random_matrix = jax.random.normal(k3, (HD, FD), dtype=jnp.float32) * (1.0 / np.sqrt(HD))
        W_out = jax.random.normal(k4, (H, H), dtype=jnp.float32) * (1.0 / np.sqrt(H))
        b_out = jnp.zeros((H,), dtype=jnp.float32)
        return {'x': x, 'W_qkv': W_qkv, 'random_matrix': random_matrix, 'W_out': W_out, 'b_out': b_out}
    _L0_mix_all = _L0_mix_setup()
    _L0_mix_in = {k: v for k, v in _L0_mix_all.items() if k in ('W_qkv', 'random_matrix', 'W_out', 'b_out')}
    del _L0_mix_all

    def _L0_ffn_setup():
        import jax, jax.numpy as jnp
        import numpy as np
        B, S, D, H, E = (4, 1024, 512, 64, 8)
        key = jax.random.key(seed)
        ks = jax.random.split(key, 7)
        scale = 1.0 / np.sqrt(D)
        return {'x': jax.random.normal(ks[0], (B, S, D), dtype=jnp.float32), 'Wg': jax.random.normal(ks[1], (D, E), dtype=jnp.float32) * scale, 'bg': jnp.zeros((E,), dtype=jnp.float32), 'W1': jax.random.normal(ks[2], (E, D, H), dtype=jnp.float32) * scale, 'b1': jnp.zeros((E, H), dtype=jnp.float32), 'W2': jax.random.normal(ks[3], (E, H, D), dtype=jnp.float32) * (1.0 / np.sqrt(H)), 'b2': jnp.zeros((E, D), dtype=jnp.float32)}
    _L0_ffn_all = _L0_ffn_setup()
    _L0_ffn_in = {k: v for k, v in _L0_ffn_all.items() if k in ('Wg', 'bg', 'W1', 'b1', 'W2', 'b2')}
    del _L0_ffn_all

    def _L1_gnn_setup():
        import jax, jax.numpy as jnp
        import numpy as np
        N_NODES = 50000
        N_EDGES = 50000
        IN_F = 512
        OUT_F = 512
        key = jax.random.key(seed)
        k1, k2, k3, k4, k5 = jax.random.split(key, 5)
        input = jax.random.normal(k1, (N_NODES, IN_F), dtype=jnp.float32)
        edge_index = jax.random.randint(k2, (2, N_EDGES), 0, N_NODES, dtype=jnp.int64)
        edge_vals = jax.random.uniform(k3, (N_EDGES,), dtype=jnp.float32)
        stdv = 1.0 / np.sqrt(OUT_F)
        weight = jax.random.uniform(k4, (IN_F, OUT_F), dtype=jnp.float32, minval=-stdv, maxval=stdv)
        bias = jax.random.uniform(k5, (OUT_F,), dtype=jnp.float32, minval=-stdv, maxval=stdv)
        return {'input': input, 'edge_index': edge_index, 'edge_vals': edge_vals, 'weight': weight, 'bias': bias}
    _L1_gnn_all = _L1_gnn_setup()
    _L1_gnn_in = {k: v for k, v in _L1_gnn_all.items() if k in ('weight', 'bias')}
    del _L1_gnn_all

    def _L1_mix_setup():
        import math
        import jax, jax.numpy as jnp
        import numpy as np
        B, T, D, M = (4, 256, 512, 256)

        def _prm_exp(x, w):
            xd = 0.5 * jnp.sum(x * x, axis=-1, keepdims=True)
            wtx = jnp.einsum('btd,md->btm', x, w)
            return jnp.exp(wtx - xd) / math.sqrt(w.shape[0])
        key = jax.random.key(seed)
        ks = jax.random.split(key, 5)
        x = jax.random.normal(ks[0], (B, T, D), dtype=jnp.float32)
        w_qkv = jax.random.normal(ks[1], (3 * D, D), dtype=jnp.float32) * 0.02
        b_qkv = jnp.zeros((3 * D,), dtype=jnp.float32)
        w_proj = jax.random.normal(ks[2], (D, D), dtype=jnp.float32) * 0.02
        b_proj = jnp.zeros((D,), dtype=jnp.float32)
        a = jax.random.normal(ks[3], (D, M), dtype=jnp.float32)
        qmat, _ = jnp.linalg.qr(a)
        w_feat = qmat.T * math.sqrt(M)
        return dict(x=x, w_qkv=w_qkv, b_qkv=b_qkv, w_proj=w_proj, b_proj=b_proj, w_feat=w_feat)
    _L1_mix_all = _L1_mix_setup()
    _L1_mix_in = {k: v for k, v in _L1_mix_all.items() if k in ('w_qkv', 'b_qkv', 'w_proj', 'b_proj', 'w_feat')}
    del _L1_mix_all

    def _L1_ffn_setup():
        import jax, jax.numpy as jnp
        import numpy as np
        D, E, DR, K, DFF, DSH = (512, 64, 64, 2, 64, 1024)
        TEMP = 0.7
        SHARED_SCALE = 0.25
        EPS = 1e-05

        def _ln(x, g, b):
            m = jnp.mean(x, axis=-1, keepdims=True)
            v = jnp.mean(jnp.square(x - m), axis=-1, keepdims=True)
            return (x - m) * jax.lax.rsqrt(v + EPS) * g + b
        key = jax.random.key(seed)
        ks = jax.random.split(key, 16)
        s = 0.02
        return {'x': jax.random.normal(ks[0], (1, 512, D), dtype=jnp.float32), 'ln1_g': jnp.ones((D,), jnp.float32), 'ln1_b': jnp.zeros((D,), jnp.float32), 'Wr': jax.random.normal(ks[1], (D, DR), jnp.float32) * s, 'codebook': jax.random.normal(ks[2], (E, DR), jnp.float32), 'W1': jax.random.normal(ks[3], (E, D, DFF), jnp.float32) * s, 'b1': jnp.zeros((E, DFF), jnp.float32), 'W2': jax.random.normal(ks[4], (E, DFF, D), jnp.float32) * s, 'b2': jnp.zeros((E, D), jnp.float32), 'Ws1': jax.random.normal(ks[5], (D, DSH), jnp.float32) * s, 'bs1': jnp.zeros((DSH,), jnp.float32), 'Ws2': jax.random.normal(ks[6], (DSH, D), jnp.float32) * s, 'bs2': jnp.zeros((D,), jnp.float32), 'ffln_g': jnp.ones((D,), jnp.float32), 'ffln_b': jnp.zeros((D,), jnp.float32), 'Wf1': jax.random.normal(ks[7], (D, DFF), jnp.float32) * s, 'bf1': jnp.zeros((DFF,), jnp.float32), 'Wf2': jax.random.normal(ks[8], (DFF, D), jnp.float32) * s, 'bf2': jnp.zeros((D,), jnp.float32)}
    _L1_ffn_all = _L1_ffn_setup()
    _L1_ffn_in = {k: v for k, v in _L1_ffn_all.items() if k in ('ln1_g', 'ln1_b', 'Wr', 'codebook', 'W1', 'b1', 'W2', 'b2', 'Ws1', 'bs1', 'Ws2', 'bs2', 'ffln_g', 'ffln_b', 'Wf1', 'bf1', 'Wf2', 'bf2')}
    del _L1_ffn_all
    return {'x': x, 'src': src, 'dst': dst, 'edge_weight': edge_weight, 'L0_gnn_W': _L0_gnn_in['W'], 'L0_gnn_b': _L0_gnn_in['b'], 'L0_mix_W_qkv': _L0_mix_in['W_qkv'], 'L0_mix_random_matrix': _L0_mix_in['random_matrix'], 'L0_mix_W_out': _L0_mix_in['W_out'], 'L0_mix_b_out': _L0_mix_in['b_out'], 'L0_ffn_Wg': _L0_ffn_in['Wg'], 'L0_ffn_bg': _L0_ffn_in['bg'], 'L0_ffn_W1': _L0_ffn_in['W1'], 'L0_ffn_b1': _L0_ffn_in['b1'], 'L0_ffn_W2': _L0_ffn_in['W2'], 'L0_ffn_b2': _L0_ffn_in['b2'], 'L1_gnn_weight': _L1_gnn_in['weight'], 'L1_gnn_bias': _L1_gnn_in['bias'], 'L1_mix_w_qkv': _L1_mix_in['w_qkv'], 'L1_mix_b_qkv': _L1_mix_in['b_qkv'], 'L1_mix_w_proj': _L1_mix_in['w_proj'], 'L1_mix_b_proj': _L1_mix_in['b_proj'], 'L1_mix_w_feat': _L1_mix_in['w_feat'], 'L1_ffn_ln1_g': _L1_ffn_in['ln1_g'], 'L1_ffn_ln1_b': _L1_ffn_in['ln1_b'], 'L1_ffn_Wr': _L1_ffn_in['Wr'], 'L1_ffn_codebook': _L1_ffn_in['codebook'], 'L1_ffn_W1': _L1_ffn_in['W1'], 'L1_ffn_b1': _L1_ffn_in['b1'], 'L1_ffn_W2': _L1_ffn_in['W2'], 'L1_ffn_b2': _L1_ffn_in['b2'], 'L1_ffn_Ws1': _L1_ffn_in['Ws1'], 'L1_ffn_bs1': _L1_ffn_in['bs1'], 'L1_ffn_Ws2': _L1_ffn_in['Ws2'], 'L1_ffn_bs2': _L1_ffn_in['bs2'], 'L1_ffn_ffln_g': _L1_ffn_in['ffln_g'], 'L1_ffn_ffln_b': _L1_ffn_in['ffln_b'], 'L1_ffn_Wf1': _L1_ffn_in['Wf1'], 'L1_ffn_bf1': _L1_ffn_in['bf1'], 'L1_ffn_Wf2': _L1_ffn_in['Wf2'], 'L1_ffn_bf2': _L1_ffn_in['bf2']}

def reference(x, src, dst, edge_weight, L0_gnn_W, L0_gnn_b, L0_mix_W_qkv, L0_mix_random_matrix, L0_mix_W_out, L0_mix_b_out, L0_ffn_Wg, L0_ffn_bg, L0_ffn_W1, L0_ffn_b1, L0_ffn_W2, L0_ffn_b2, L1_gnn_weight, L1_gnn_bias, L1_mix_w_qkv, L1_mix_b_qkv, L1_mix_w_proj, L1_mix_b_proj, L1_mix_w_feat, L1_ffn_ln1_g, L1_ffn_ln1_b, L1_ffn_Wr, L1_ffn_codebook, L1_ffn_W1, L1_ffn_b1, L1_ffn_W2, L1_ffn_b2, L1_ffn_Ws1, L1_ffn_bs1, L1_ffn_Ws2, L1_ffn_bs2, L1_ffn_ffln_g, L1_ffn_ffln_b, L1_ffn_Wf1, L1_ffn_bf1, L1_ffn_Wf2, L1_ffn_bf2):
    import jax
    import jax.numpy as jnp

    def _L0_gnn_ref(node_feats, edge_index, W, b):
        import jax, jax.numpy as jnp
        import numpy as np
        N = 256
        C_IN = 512
        C_OUT = 512
        E_RAND = 8192
        src, dst = (edge_index[0], edge_index[1])
        adj = jnp.zeros((N, N), dtype=node_feats.dtype).at[src, dst].add(1.0)
        num_neighbours = adj.sum(axis=-1, keepdims=True)
        proj = node_feats @ W.T + b
        out = adj @ proj / num_neighbours
        return out

    def _L0_mix_ref(x, W_qkv, random_matrix, W_out, b_out):
        import jax, jax.numpy as jnp
        import numpy as np
        B, S, H = (4, 256, 512)
        NH, HD = (8, 64)
        FD = HD // 2
        b, s, h = x.shape
        qkv = (x @ W_qkv).reshape(b, s, 3, NH, HD)
        q, k, v = (qkv[:, :, 0], qkv[:, :, 1], qkv[:, :, 2])
        q_prime = jax.nn.elu(q @ random_matrix) + 1.0
        k_prime = jax.nn.elu(k @ random_matrix) + 1.0
        kv = jnp.einsum('bshd,bshf->bhdf', k_prime, v)
        z = jnp.einsum('bshd,bhdf->bshf', q_prime, kv)
        normalizer = jnp.einsum('bshd,bhd->bsh', q_prime, k_prime.sum(axis=1))
        z = z / (normalizer[..., None] + 1e-06)
        z = z.reshape(b, s, h)
        return z @ W_out + b_out

    def _L0_ffn_ref(x, Wg, bg, W1, b1, W2, b2):
        import jax, jax.numpy as jnp
        import numpy as np
        B, S, D, H, E = (4, 1024, 512, 64, 8)
        b, s, d = x.shape
        xf = x.reshape(-1, d)
        logits = xf @ Wg + bg
        scores = jax.nn.softmax(logits, axis=-1)
        top_s, top_i = jax.lax.top_k(scores, 1)
        idx = top_i[:, 0]
        sc = top_s[:, 0]
        n_experts = Wg.shape[1]
        out = jnp.zeros_like(xf)
        for e in range(n_experts):
            h = jax.nn.relu(xf @ W1[e] + b1[e]) @ W2[e] + b2[e]
            out = jnp.where((idx == e)[:, None], h, out)
        out = out * sc[:, None]
        return out.reshape(b, s, d)

    def _L1_gnn_ref(input, edge_index, edge_vals, weight, bias):
        import jax, jax.numpy as jnp
        import numpy as np
        N_NODES = 50000
        N_EDGES = 50000
        IN_F = 512
        OUT_F = 512
        support = jnp.matmul(input, weight)
        dst, src = (edge_index[0], edge_index[1])
        messages = support[src] * edge_vals[:, None]
        output = jax.ops.segment_sum(messages, dst, num_segments=input.shape[0])
        return output + bias

    def _L1_mix_ref(x, w_qkv, b_qkv, w_proj, b_proj, w_feat):
        import math
        import jax, jax.numpy as jnp
        import numpy as np
        B, T, D, M = (4, 256, 512, 256)

        def _prm_exp(x, w):
            xd = 0.5 * jnp.sum(x * x, axis=-1, keepdims=True)
            wtx = jnp.einsum('btd,md->btm', x, w)
            return jnp.exp(wtx - xd) / math.sqrt(w.shape[0])
        qkv = x @ w_qkv.T + b_qkv
        k, q, v = jnp.split(qkv, 3, axis=-1)
        kp = _prm_exp(k, w_feat)
        qp = _prm_exp(q, w_feat)
        denom = jnp.einsum('btm,bm->bt', qp, kp.sum(axis=1))[..., None]
        kptv = jnp.einsum('btd,btm->bdm', v, kp)
        y = jnp.einsum('btm,bdm->btd', qp, kptv) / (denom + 1e-08)
        y = y @ w_proj.T + b_proj
        return y

    def _L1_ffn_ref(x, ln1_g, ln1_b, Wr, codebook, W1, b1, W2, b2, Ws1, bs1, Ws2, bs2, ffln_g, ffln_b, Wf1, bf1, Wf2, bf2):
        import jax, jax.numpy as jnp
        import numpy as np
        D, E, DR, K, DFF, DSH = (512, 64, 64, 2, 64, 1024)
        TEMP = 0.7
        SHARED_SCALE = 0.25
        EPS = 1e-05

        def _ln(x, g, b):
            m = jnp.mean(x, axis=-1, keepdims=True)
            v = jnp.mean(jnp.square(x - m), axis=-1, keepdims=True)
            return (x - m) * jax.lax.rsqrt(v + EPS) * g + b
        B, S, _ = x.shape
        T = B * S
        h = _ln(x, ln1_g, ln1_b).reshape(T, D)
        r = h @ Wr
        logits = r @ codebook.T / TEMP
        probs = jax.nn.softmax(logits, axis=-1)
        vals, idx = jax.lax.top_k(probs, K)
        w = vals / jnp.sum(vals, axis=-1, keepdims=True)
        combine = jnp.zeros((T, E), x.dtype).at[jnp.arange(T)[:, None], idx].set(w)
        eh = jax.nn.silu(jnp.einsum('td,edf->tef', h, W1) + b1)
        eo = jnp.einsum('tef,efd->ted', eh, W2) + b2
        moe = jnp.einsum('te,ted->td', combine, eo)
        shared = (jax.nn.silu(h @ Ws1 + bs1) @ Ws2 + bs2) * SHARED_SCALE
        hmoe = (moe + shared).reshape(B, S, D)
        f = _ln(hmoe, ffln_g, ffln_b)
        f = jax.nn.silu(f @ Wf1 + bf1) @ Wf2 + bf2
        return x + hmoe + f
    edge_index = jnp.stack([src, dst])
    xn = _layernorm(x, axis=-1)
    x = x + _L0_gnn_ref(xn, edge_index, L0_gnn_W, L0_gnn_b) + _L0_mix_ref(xn[None], L0_mix_W_qkv, L0_mix_random_matrix, L0_mix_W_out, L0_mix_b_out)[0]
    x = x + _L0_ffn_ref(_layernorm(x, axis=-1)[None], L0_ffn_Wg, L0_ffn_bg, L0_ffn_W1, L0_ffn_b1, L0_ffn_W2, L0_ffn_b2)[0]
    xn = _layernorm(x, axis=-1)
    x = x + _L1_gnn_ref(xn, edge_index, edge_weight, L1_gnn_weight, L1_gnn_bias) + _L1_mix_ref(xn[None], L1_mix_w_qkv, L1_mix_b_qkv, L1_mix_w_proj, L1_mix_b_proj, L1_mix_w_feat)[0]
    x = x + _L1_ffn_ref(_layernorm(x, axis=-1)[None], L1_ffn_ln1_g, L1_ffn_ln1_b, L1_ffn_Wr, L1_ffn_codebook, L1_ffn_W1, L1_ffn_b1, L1_ffn_W2, L1_ffn_b2, L1_ffn_Ws1, L1_ffn_bs1, L1_ffn_Ws2, L1_ffn_bs2, L1_ffn_ffln_g, L1_ffn_ffln_b, L1_ffn_Wf1, L1_ffn_bf1, L1_ffn_Wf2, L1_ffn_bf2)[0]
    return x

_drawn_inputs = setup_inputs


def setup_inputs(seed=0):
    import zlib

    import numpy as np

    out = dict(_drawn_inputs(seed))
    spreads = {'L0_mix_b_out': (0.0, 0.1),
     'L0_ffn_bg': (0.0, 0.1),
     'L0_ffn_b1': (0.0, 0.293),
     'L0_ffn_b2': (0.0, 0.1),
     'L1_mix_b_qkv': (0.0, 0.1),
     'L1_mix_b_proj': (0.0, 0.1),
     'L1_ffn_ln1_g': (1.0, 0.6),
     'L1_ffn_ln1_b': (0.0, 0.713),
     'L1_ffn_b1': (0.0, 0.8),
     'L1_ffn_b2': (0.0, 0.279),
     'L1_ffn_bs1': (0.0, 0.8),
     'L1_ffn_bs2': (0.0, 0.8),
     'L1_ffn_ffln_g': (1.0, 0.6),
     'L1_ffn_ffln_b': (0.0, 0.8),
     'L1_ffn_bf1': (0.0, 0.8),
     'L1_ffn_bf2': (0.0, 0.292)}
    factors = {'L1_gnn_bias': 4.206,
     'L1_ffn_W1': 4.601,
     'L1_ffn_W2': 4.326,
     'L1_ffn_Ws1': 3.958,
     'L1_ffn_Ws2': 3.812,
     'L1_ffn_Wf1': 4.289,
     'L1_ffn_Wf2': 4.097}
    for name, (base, spread) in spreads.items():
        noise = np.random.default_rng([zlib.crc32(name.encode()), seed]).standard_normal(out[name].shape)
        drawn = base * np.exp(spread * noise) if base else spread * noise
        out[name] = jnp.asarray(drawn.astype(out[name].dtype))
    for name, factor in factors.items():
        out[name] = (out[name] * factor).astype(out[name].dtype)
    return out
```

```python
from contextlib import ExitStack

import numpy as np

import concourse.bass as bass
from concourse import mybir

ALU = mybir.AluOpType
ACT = mybir.ActivationFunctionType
F32 = mybir.dt.float32
F32R = mybir.dt.float32r
F16 = mybir.dt.float16
I32 = mybir.dt.int32
U32 = mybir.dt.uint32

P = 128
T = 256
D = 512
NT = T // P
KT = D // P
EDGES = 4352
ET = EDGES // P
HEADS = 8
HD = D // HEADS
FD = HD // 2
E0 = 8
E1 = 64
DFF = 64
M1 = 256
SHARED_GROUPS = 2
GROUPS = SHARED_GROUPS + E1 * DFF // D
LN_EPS = 1e-5
NORM_EPS = 1e-6
DENOM_EPS = 1e-8
TEMP = 0.7
SHARED_SCALE = 0.25
LO_SCALE = 4096.0

SLOTS = 4
RAWS = 3

FOLD_Q, FOLD_K, V0, GNN0, OUT0, UP0, DOWN0, GNN1, K1, Q1, V1, PROJ1, FFN1 = range(13)
STATIC_AT = K1


def ffn1_blocks():
    order = [("up", 0)]
    for g in range(GROUPS):
        if g + 1 < GROUPS:
            order.append(("up", g + 1))
        order.append(("down", g))
    return order


FFN1_ORDER = ffn1_blocks()
BLOCKS = FFN1 + len(FFN1_ORDER)


def raw_index(i):
    return i + (1 if i >= STATIC_AT else 0)


RAW_STATIC = STATIC_AT
N_RAW = BLOCKS + 1

COL_B1_0, COL_LN_G, COL_LN_B, COL_FF_G, COL_FF_B, COL_BK, COL_BQ, COL_B1 = 0, 4, 8, 12, 16, 20, 24, 28
COL_BF1 = COL_B1 + 4 * GROUPS
COLS = COL_BF1 + 1
SM_R, SM_WG = 0, HD
SMALL = HD + KT * E0
ST_FEAT, ST_RF, ST_WF2 = 0, KT * M1, KT * (M1 + P)
ROW_GNN0, ROW_OUT0 = 3, 4
ROW_GNN1, ROW_PROJ1, ROW_V1, ROW_SH, ROW_F2 = 0, 1, 2, 3, 4


NORMS = (("ln0", 2), ("z", 2), ("ln1", 2), ("ln2", 2), ("ln3", 2), ("ln4", 2), ("ln5", 2))
LN = tuple(n for n in NORMS if n[0] != "z")
CUTS = (("ln0", 2), ("adj", 2), ("fold", 4), ("q", 1), ("k", 1), ("v", 2), ("pr", 2), ("kv", 1), ("z", 2), ("ln1", 2),
        ("ln2", 2), ("sup", 2), ("k1", 2), ("q1", 2), ("kp", 1), ("v1", 2), ("qp", 1), ("kv1", 2), ("y1", 2),
        ("ln4", 2), ("ln5", 2), ("f1", 1))
SERIES = {
    "bn": LN, "mv": LN, "var": tuple((n, 1) for n, _ in LN), "rstd": tuple((n, 1) for n, _ in LN), "xn": NORMS,
    "turned": tuple(n for n in NORMS if n[0] != "ln3"), "hi": CUTS, "lo": CUTS, "affine": (("ln4", 4), ("ln5", 4)),
    "f": (("q", 1), ("k", 1), ("g", 2), ("kv", 2), ("k1", 4), ("q1", 4), ("v1", 2)),
    "done": (("fold", 4), ("q", 1), ("k", 1), ("v", 2), ("g", 2), ("kv", 1), ("z", 2), ("o", 2), ("deg", 1),
             ("agg0", 2), ("lg0", 1), ("s", 2), ("k1", 2), ("q1", 2), ("v1", 2), ("agg1", 2), ("kv1", 2),
             ("ksum1", 1), ("den1", 1), ("p1", 2), ("r", 1), ("lg1", 1), ("f1", 1), ("f2", 2)),
}


def series(name):
    stage, _, what = name.rpartition("_")
    before = 0
    for other, times in SERIES.get(what, ()):
        if other == stage:
            return f"all_{what}", before
        before += times
    return name, 0


def nth(name, n):
    return series(name)[1] + n


def last_use(i):
    if i < FFN1:
        return (("fold_done", 2), ("fold_done", 4), ("v_done", 2), ("g_done", 2), ("o_done", 2), ("ffn0_up", 2),
                ("ffn0_down", 2), ("s_done", 2), ("k1_done", 2), ("q1_done", 2), ("v1_done", 2), ("p1_done", 2))[i]
    kind, g = FFN1_ORDER[i - FFN1]
    return f"ffn1_{kind}", 2 * g + 2


def gnn_kernel(nc, x, src, dst, ew, stream, cols, small, bg, rows0, rows1, codebook, b2_0, b2_1, out):
    with ExitStack() as ctx:
        def sb(name, shape, dt=F32):
            return ctx.enter_context(nc.sbuf_tensor(name, shape, dt))

        sems = {}

        def sem(name):
            name = series(name)[0]
            if name not in sems:
                sems[name] = ctx.enter_context(nc.semaphore(name))
            return sems[name]

        bank = [ctx.enter_context(nc.psum_tensor(f"bank{i}", [P, 512], F32)) for i in range(8)]

        raw = sb("raw", [P, RAWS, 2048])
        w_hi = [sb(f"w_hi{i}", [P, 2048], F32R) for i in range(SLOTS)]
        w_lo = [sb(f"w_lo{i}", [P, 2048], F32R) for i in range(SLOTS)]
        st_hi = sb("static_hi", [P, 2048], F32R)
        st_lo = sb("static_lo", [P, 2048], F32R)
        xs = sb("xs", [P, NT, D])
        base = sb("base", [P, NT, D])
        xn = sb("xn", [P, NT, D])
        xT_hi = sb("xT_hi", [P, 1024], F32R)
        xT_lo = sb("xT_lo", [P, 1024], F32R)
        v_hi = sb("v_hi", [P, 1024], F32R)
        v_lo = sb("v_lo", [P, 1024], F32R)
        pr_hi = sb("proj_hi", [P, 1024], F32R)
        pr_lo = sb("proj_lo", [P, 1024], F32R)
        wide_hi = sb("wide_hi", [P, 2048], F32R)
        wide_lo = sb("wide_lo", [P, 2048], F32R)
        qf_hi = sb("qf_hi", [P, 512], F32R)
        qf_lo = sb("qf_lo", [P, 512], F32R)
        kf_hi = sb("kf_hi", [P, 512], F32R)
        kf_lo = sb("kf_lo", [P, 512], F32R)
        fa = sb("fa", [P, 1024])
        fb = sb("fb", [P, 1024])
        adj_hi = sb("adj_hi", [P, 2, 512], F32R)
        adj_lo = sb("adj_lo", [P, 2, 512], F32R)
        sel = sb("sel", [P, E1 * DFF], F16)
        rows = sb("rows", [P, 5, D])
        colsb = sb("colsb", [P, COLS])
        smr = sb("small_raw", [P, SMALL])
        sm_hi = sb("small_hi", [P, SMALL], F32R)
        sm_lo = sb("small_lo", [P, SMALL], F32R)
        b2s = sb("b2s", [E1, D])
        cbs = sb("cbs", [64, E1])
        bgs = sb("bgs", [P, E0])
        ident = sb("ident", [P, P])
        iota = sb("iota", [P, T])
        blockmask = sb("blockmask", [P, 256])
        edge_i = sb("edge_i", [P, 2, ET], I32)
        edge_f = sb("edge_f", [P, 2, ET])
        ewf = sb("ewf", [P, ET])
        ew_hi = sb("ew_hi", [P, ET], F32R)
        ew_lo = sb("ew_lo", [P, ET])
        ones = sb("ones", [P, 2], F32R)
        ones32 = sb("ones32", [P, 2])
        pcol = sb("pcol", [P, 4])
        mhalf = sb("mhalf", [P, 2])
        st = sb("bnst", [P, NT, 6])
        mv = sb("mv", [P, NT, 2])
        ve = sb("ve", [P, NT])
        rstd = sb("rstd", [P, NT])
        ks = sb("ks", [P, 2])
        ksb = sb("ksb", [P, 2, 4])
        ks_hi = sb("ks_hi", [P, 2, 4], F32R)
        ks_lo = sb("ks_lo", [P, 2, 4], F32R)
        nrm = sb("nrm", [P, 2, 8])
        rden = sb("rden", [P, 2, 8])
        lg = sb("logits", [P, NT, E1])
        pe_ = sb("expl", [P, NT, E0])
        top = sb("top", [P, NT, 8])
        topi = sb("topi", [P, NT, 8], U32)
        topf = sb("topf", [P, NT, 8])
        wk = sb("wk", [P, NT, 8])
        comb = sb("comb", [P, NT, P])
        comb2 = xn[:, 1, 0:NT * P].rearrange("p (n e) -> p n e", n=NT)
        combT = blockmask
        combT16 = iota[:, 0:T // 2].bitcast(F16)
        rT = xn[0:64, 0, 0:T]
        f1_hi, f1_lo = pr_hi, pr_lo
        iota2 = smr[:, 0:64].bitcast(F16)
        deg = sb("deg", [P, NT])
        degr = sb("degr", [P, NT])

        block = ctx.enter_context(nc.Block())

        def flat(t):
            return t[:, :, :].rearrange("p a b -> p (a b)")

        def f32(ap):
            return ap.bitcast(F32)

        @block.sync
        def _(sp):
            sp.dma_start(edge_i[:, 0, :], src).then_inc(sem("src_in"), 16)
            sp.dma_start(edge_i[:, 1, :], dst).then_inc(sem("dst_in"), 16)
            sp.dma_start(ewf[:, :], ew).then_inc(sem("ew_in"), 16)
            sp.dma_start(xs[:, :, :], x.rearrange("(n p) d -> p n d", p=P)).then_inc(sem("x_in"), 16)

            def load(r):
                if r >= RAWS:
                    sp.wait_ge(sem("raw_used"), r - RAWS + 1)
                sp.dma_start(raw[:, r % RAWS, :], stream[r]).then_inc(sem(f"raw_in{r % RAWS}"), 16)

            load(0)
            sp.dma_start(smr[:, :], small).then_inc(sem("small_in"), 16)
            sp.dma_start(bgs[:, :], bg[0, :].partition_broadcast(P)).then_inc(sem("bg_in"), 16)
            load(1)
            sp.dma_start(colsb[:, :], cols).then_inc(sem("cols_in"), 16)
            sp.dma_start(rows[:, 3:5, :], rows0.partition_broadcast(P)).then_inc(sem("rows0_in"), 16)
            load(2)
            sp.dma_start(b2s[0:E0, :], b2_0).then_inc(sem("b2_0_in"), 16)
            sp.dma_start(cbs[:, :], codebook).then_inc(sem("codebook_in"), 16)
            sp.dma_start(rows[:, 0:3, :], rows1[0:3, :].partition_broadcast(P)).then_inc(sem("rows1_in"), 16)
            for r in range(3, N_RAW):
                load(r)
                if r == 13:
                    sp.wait_ge(sem("ffn0_out"), 2)
                    sp.dma_start(b2s[:, :], b2_1).then_inc(sem("b2_1_in"), 16)
                    sp.dma_start(rows[:, 3:5, :], rows1[3:5, :].partition_broadcast(P)).then_inc(sem("rows2_in"), 16)
            for tt in range(NT):
                sp.wait_ge(sem("y_done"), nth("y_done", tt + 1))
                sp.dma_start(out[tt * P:(tt + 1) * P, :], xs[:, tt, :]).then_inc(sem("stored"), 16)
            sp.wait_ge(sem("stored"), 16 * NT)

        @block.gpsimd
        def _(pool):
            pool.memset(ident[:, :], 0.0).then_inc(sem("zeroed"), 1)
            pool.iota(iota[:, :], [[1, T]], 0, 0, allow_small_or_imprecise_dtypes=True).then_inc(sem("iota_made"), 1)
            pool.wait_ge(sem("zeroed"), 1)
            pool.affine_select(out=ident[:, :], in_=ident[:, :], compare_op=ALU.not_equal, fill=1.0, base=0,
                               pattern=[[-1, P]], channel_multiplier=1).then_inc(sem("ident_made"), 1)
            pool.memset(mhalf[:, :], -0.5).then_inc(sem("mhalf_made"), 1)

            def rsqrt(tag):
                pool.wait_ge(sem("mhalf_made"), 1)
                pool.wait_ge(sem(f"{tag}_var"), nth(f"{tag}_var", 1))
                pool.tensor_tensor(rstd[:, :], ve[:, :], mhalf[:, :], ALU.pow).then_inc(sem(f"{tag}_rstd"), 1)

            rsqrt("ln0")
            pool.iota(pcol[:, 0:1], [[0, 1]], 0, 1, allow_small_or_imprecise_dtypes=True).then_inc(sem("pidx_made"), 1)
            pool.iota(blockmask[:, :], [[1, 4], [0, HD]], 0, 0,
                      allow_small_or_imprecise_dtypes=True).then_inc(sem("heads_made"), 1)
            pool.iota(sel[:, :], [[1, E1], [0, DFF]], 0, 0,
                      allow_small_or_imprecise_dtypes=True).then_inc(sem("experts_made"), 1)

            pool.wait_ge(sem("x_in"), 16)
            pool.wait_ge(sem("rows0_in"), 16)
            for tt in range(NT):
                pool.tensor_tensor(base[:, tt, :], xs[:, tt, :], rows[:, ROW_OUT0, :],
                                   ALU.add).then_inc(sem("base0"), 1)

            def base1():
                pool.wait_ge(sem("rows1_in"), 16)
                for n, row in enumerate((ROW_GNN1, ROW_PROJ1)):
                    for tt in range(NT):
                        if n == 0:
                            pool.wait_ge(sem("x2"), tt + 1)
                        else:
                            pool.wait_ge(sem("base1"), tt + 1)
                        pool.tensor_tensor(base[:, tt, :], (base if n else xs)[:, tt, :], rows[:, row, :],
                                           ALU.add).then_inc(sem("base1"), 1)

            def base2():
                pool.wait_ge(sem("rows2_in"), 16)
                for tt in range(NT):
                    pool.wait_ge(sem("ln3_xn"), nth("ln3_xn", tt + 1))
                    pool.tensor_tensor(base[:, tt, :], xs[:, tt, :], fa[:, tt * D:(tt + 1) * D],
                                       ALU.add).then_inc(sem("base2"), 1)
                for tt in range(NT):
                    pool.wait_ge(sem("base2"), tt + 1)
                    pool.tensor_tensor(base[:, tt, :], base[:, tt, :], rows[:, ROW_F2, :],
                                       ALU.add).then_inc(sem("base2"), 1)

            def low(i):
                pool.wait_ge(sem("hi_cut"), i + 1)
                pool.tensor_tensor(w_lo[i % SLOTS][:, :], raw[:, raw_index(i) % RAWS, :],
                                   f32(w_hi[i % SLOTS][:, :]), ALU.subtract).then_inc(sem("raw_used"), 1)

            def low_static():
                pool.wait_ge(sem("static_hi_cut"), 1)
                pool.tensor_tensor(st_lo[:, :], raw[:, RAW_STATIC % RAWS, :], f32(st_hi[:, :]),
                                   ALU.subtract).then_inc(sem("raw_used"), 1)

            for i in range(BLOCKS):
                if i == STATIC_AT:
                    low_static()
                if i == 8:
                    pool.wait_ge(sem("small_cut"), 1)
                    pool.iota(iota2[:, :], [[0, 2], [1, E1]], 0, 0,
                              allow_small_or_imprecise_dtypes=True).then_inc(sem("iota2_made"), 1)
                    rsqrt("ln1")
                if i == 10:
                    rsqrt("ln2")
                    base1()
                if i == 15:
                    rsqrt("ln3")
                    rsqrt("ln4")
                    base2()
                low(i)
            rsqrt("ln5")
            for tt in range(NT):
                pool.wait_ge(sem("hmoe"), tt + 1)
                pool.wait_ge(sem("base2"), 4)
                pool.tensor_tensor(base[:, tt, :], base[:, tt, :], fa[:, tt * D:(tt + 1) * D],
                                   ALU.add).then_inc(sem("base3"), 1)

        def weights_ready(eng, i):
            eng.wait_ge(sem("raw_used"), raw_index(i) + 1)

        @block.tensor
        def _(pe):
            def mm3(o, a_hi, a_lo, b_hi, b_lo, first, last):
                pe.matmul(o, a_hi, b_hi, start=first, stop=False)
                pe.matmul(o, a_hi, b_lo, start=False, stop=False)
                return pe.matmul(o, a_lo, b_hi, start=False, stop=last)

            def turn(tag):
                for tt in range(NT):
                    pe.wait_ge(sem(f"{tag}_xn"), nth(f"{tag}_xn", tt + 1))
                    for kt in range(KT):
                        ins = pe.transpose(bank[6 + kt // 2][:, (kt % 2) * T + tt * P:(kt % 2) * T + (tt + 1) * P],
                                           xn[:, tt, kt * P:(kt + 1) * P], ident[:, :])
                        if tt == NT - 1 and kt % 2 == 1:
                            ins.then_inc(sem(f"{tag}_turned"), 1)

            def tokens_out(tag, banks, i, wait=None):
                weights_ready(pe, i)
                if wait:
                    pe.wait_ge(sem(wait[0]), nth(*wait))
                for tt in range(NT):
                    for kt in range(KT):
                        a = slice(kt * T + tt * P, kt * T + (tt + 1) * P)
                        b = slice(kt * D, (kt + 1) * D)
                        ins = mm3(bank[banks[tt]][:, :], xT_hi[:, a], xT_lo[:, a],
                                  w_hi[i % SLOTS][:, b], w_lo[i % SLOTS][:, b], kt == 0, kt == KT - 1)
                    ins.then_inc(sem(tag), 1)

            pe.wait_ge(sem("ident_made"), 1)
            turn("ln0")

            for j in range(ET):
                pe.wait_ge(sem("hot"), j + 1)
                hot = (v_hi, v_lo)[j % 2]
                for h in range(2):
                    lhs = hot[:, h * P:(h + 1) * P]
                    if j:
                        pe.matmul(bank[h][:, T:2 * T], lhs, hot[:, 3 * T:4 * T], start=False, stop=False)
                    ins = pe.matmul(bank[h][:, :], lhs, hot[:, T:3 * T], start=(j == 0), stop=(j == ET - 1))
                    if j == 0:
                        ins = pe.matmul(bank[h][:, T:2 * T], lhs, hot[:, 3 * T:4 * T], start=False, stop=False)
                ins.then_inc(sem("hot_used"), 1)

            pe.wait_ge(sem("small_cut"), 1)
            for n, i in enumerate((FOLD_Q, FOLD_K)):
                weights_ready(pe, i)
                for m in range(KT):
                    for kt in range(KT):
                        a = slice(kt * D + m * P, kt * D + (m + 1) * P)
                        o = bank[2 + 2 * n + m // 2][:, (m % 2) * T + kt * HD:(m % 2) * T + (kt + 1) * HD]
                        ins = mm3(o, w_hi[i % SLOTS][:, a], w_lo[i % SLOTS][:, a],
                                  sm_hi[:, SM_R:SM_R + HD], sm_lo[:, SM_R:SM_R + HD], True, True)
                    if m % 2 == 1:
                        ins.then_inc(sem("fold_done"), 1)

            pe.wait_ge(sem("fold_lo"), nth("fold_lo", 4))
            pe.wait_ge(sem("ln0_lo"), nth("ln0_lo", 2))
            for m in range(2):
                for kt in range(KT):
                    a = slice(kt * 512 + m * P, kt * 512 + (m + 1) * P)
                    b = slice(kt * T, (kt + 1) * T)
                    ins = mm3(bank[2][:, m * T:(m + 1) * T], wide_hi[:, a], wide_lo[:, a], xT_hi[:, b], xT_lo[:, b],
                              kt == 0, kt == KT - 1)
            ins.then_inc(sem("q_done"), 1)
            for tt in range(NT):
                for kt in range(KT):
                    a = slice(kt * T + tt * P, kt * T + (tt + 1) * P)
                    b = slice(kt * 512 + T, kt * 512 + 2 * T)
                    ins = mm3(bank[3][:, tt * T:(tt + 1) * T], xT_hi[:, a], xT_lo[:, a], wide_hi[:, b], wide_lo[:, b],
                              kt == 0, kt == KT - 1)
            ins.then_inc(sem("k_done"), 1)
            tokens_out("v_done", (4, 5), V0)
            tokens_out("g_done", (0, 1), GNN0, ("adj_lo", 2))

            pe.wait_ge(sem("k_lo"), nth("k_lo", 1))
            pe.wait_ge(sem("q_lo"), nth("q_lo", 1))
            pe.wait_ge(sem("v_lo"), nth("v_lo", 2))
            pe.wait_ge(sem("ones_made"), 1)
            for m in range(2):
                for tt in range(NT):
                    a = slice(tt * T + m * P, tt * T + (m + 1) * P)
                    b = slice(tt * D + m * 256, tt * D + (m + 1) * 256)
                    mm3(bank[2][:, m * 256:(m + 1) * 256], kf_hi[:, a], kf_lo[:, a], v_hi[:, b], v_lo[:, b],
                        tt == 0, tt == NT - 1)
                for tt in range(NT):
                    a = slice(tt * T + m * P, tt * T + (m + 1) * P)
                    pe.matmul(bank[3][:, 2 * m:2 * m + 2], kf_hi[:, a], ones[:, :], start=(tt == 0), stop=False)
                    ins = pe.matmul(bank[3][:, 2 * m:2 * m + 2], kf_lo[:, a], ones[:, :], start=False,
                                    stop=(tt == NT - 1))
            ins.then_inc(sem("kv_done"), 1)

            pe.wait_ge(sem("kv_lo"), nth("kv_lo", 1))
            for tt in range(NT):
                for m in range(2):
                    a = slice(m * T + tt * P, m * T + (tt + 1) * P)
                    b = slice(m * 256, (m + 1) * 256)
                    mm3(bank[4 + tt][:, b], qf_hi[:, a], qf_lo[:, a], xT_hi[:, b], xT_lo[:, b], True, True)
                for m in range(2):
                    a = slice(m * T + tt * P, m * T + (tt + 1) * P)
                    ins = mm3(bank[3][:, 64 + 8 * tt + 4 * m:68 + 8 * tt + 4 * m], qf_hi[:, a], qf_lo[:, a],
                              ks_hi[:, m, :], ks_lo[:, m, :], True, True)
                ins.then_inc(sem("z_done"), 1)
            turn("z")
            pe.wait_ge(sem("z_lo"), nth("z_lo", 2))
            weights_ready(pe, OUT0)
            pe.wait_ge(sem("pr_lo"), nth("pr_lo", 2))
            for tt in range(NT):
                for kt in range(KT):
                    a = slice(kt * T + tt * P, kt * T + (tt + 1) * P)
                    b = slice(kt * D, (kt + 1) * D)
                    ins = mm3(bank[tt][:, :], v_hi[:, a], v_lo[:, a], w_hi[OUT0 % SLOTS][:, b],
                              w_lo[OUT0 % SLOTS][:, b], kt == 0, kt == KT - 1)
                ins.then_inc(sem("o_done"), 1)

            def aggregate(tag, banks, part):
                for tt in range(NT):
                    for h in range(2):
                        a = slice(part * T + tt * P, part * T + (tt + 1) * P)
                        b = slice(h * D, (h + 1) * D)
                        ins = mm3(bank[banks[tt]][:, :], adj_hi[:, h, a], adj_lo[:, h, a], pr_hi[:, b], pr_lo[:, b],
                                  h == 0, h == 1)
                    ins.then_inc(sem(tag), 1)

            pe.wait_ge(sem("z_xn"), nth("z_xn", 2))
            for tt in range(NT):
                for h in range(2):
                    a = slice(tt * P, (tt + 1) * P)
                    pe.matmul(bank[4][:, 2 * tt:2 * tt + 2], adj_hi[:, h, a], ones[:, :], start=(h == 0), stop=False)
                    ins = pe.matmul(bank[4][:, 2 * tt:2 * tt + 2], adj_lo[:, h, a], ones[:, :], start=False,
                                    stop=(h == 1))
            ins.then_inc(sem("deg_done"), 1)
            aggregate("agg0_done", (2, 3), 0)

            def up(tag, i, routed, g, m0):
                weights_ready(pe, i)
                for j in range(2):
                    if g:
                        pe.wait_ge(sem(f"{tag}_act"), nth(f"{tag}_act", 4 * g - 2 + 2 * j))
                    for mm in range(2):
                        for kt in range(KT):
                            a = slice(kt * D + (2 * j + mm) * P, kt * D + (2 * j + mm + 1) * P)
                            b = slice(kt * T, (kt + 1) * T)
                            ins = mm3(bank[2 + j][:, mm * T:(mm + 1) * T], w_hi[i % SLOTS][:, a],
                                      w_lo[i % SLOTS][:, a], xT_hi[:, b], xT_lo[:, b], kt == 0, kt == KT - 1)
                    ins.then_inc(sem(f"{tag}_up"), 1)
                    if routed:
                        if g > SHARED_GROUPS:
                            pe.wait_ge(sem(f"{tag}_scaled"), nth(f"{tag}_scaled", 2 * g - 1 + j))
                        for mm in range(2):
                            m = m0 + 2 * j + mm
                            ins = pe.matmul(bank[6 + j][:, mm * T:(mm + 1) * T], sel[:, m * P:(m + 1) * P],
                                            combT16[:, :], start=True, stop=True)
                        ins.then_inc(sem(f"{tag}_spread"), 1)

            def down(tag, i, g, first, last):
                weights_ready(pe, i)
                for j in range(2):
                    pe.wait_ge(sem(f"{tag}_act_lo"), nth(f"{tag}_act_lo", 2 * g + j + 1))
                    for mm in range(2):
                        for tt in range(NT):
                            a = slice((g % 2) * 1024 + j * 512 + mm * T + tt * P,
                                      (g % 2) * 1024 + j * 512 + mm * T + (tt + 1) * P)
                            b = slice((2 * j + mm) * D, (2 * j + mm + 1) * D)
                            s = last and j == 1 and mm == 1
                            ins = mm3(bank[tt][:, :], wide_hi[:, a], wide_lo[:, a], w_hi[i % SLOTS][:, b],
                                      w_lo[i % SLOTS][:, b], first and j == 0 and mm == 0, s)
                    ins.then_inc(sem(f"{tag}_down"), 1)

            turn("ln1")
            pe.wait_ge(sem("ln1_lo"), nth("ln1_lo", 2))
            for tt in range(NT):
                for kt in range(KT):
                    a = slice(kt * T + tt * P, kt * T + (tt + 1) * P)
                    b = slice(SM_WG + kt * E0, SM_WG + (kt + 1) * E0)
                    ins = mm3(bank[4][:, 8 + tt * 8:16 + tt * 8], xT_hi[:, a], xT_lo[:, a], sm_hi[:, b], sm_lo[:, b],
                              kt == 0, kt == KT - 1)
            ins.then_inc(sem("lg0_done"), 1)
            for tt in range(NT):
                pe.wait_ge(sem("comb0"), tt + 1)
                ins = pe.transpose(bank[5][:, tt * P:(tt + 1) * P], comb[:, tt, :], ident[:, :])
            ins.then_inc(sem("comb0_turned"), 1)
            pe.wait_ge(sem("comb0_16"), 1)
            pe.wait_ge(sem("sel_made"), 1)
            up("ffn0", UP0, True, 0, 0)
            pe.wait_ge(sem("b2_0_in"), 16)
            down("ffn0", DOWN0, 0, True, False)
            for tt in range(NT):
                pe.matmul(bank[tt][:, :], combT[0:E0, tt * P:(tt + 1) * P], b2s[0:E0, :], start=False,
                          stop=True).then_inc(sem("ffn0_out"), 1)

            turn("ln2")
            pe.wait_ge(sem("ln2_lo"), nth("ln2_lo", 2))
            tokens_out("s_done", (0, 1), GNN1)

            def turned_out(tag, banks, i):
                weights_ready(pe, i)
                for m in range(KT):
                    for kt in range(KT):
                        a = slice(kt * D + m * P, kt * D + (m + 1) * P)
                        b = slice(kt * T, (kt + 1) * T)
                        ins = mm3(bank[banks[m // 2]][:, (m % 2) * T:(m % 2 + 1) * T], w_hi[i % SLOTS][:, a],
                                  w_lo[i % SLOTS][:, a], xT_hi[:, b], xT_lo[:, b], kt == 0, kt == KT - 1)
                    if m % 2 == 1:
                        ins.then_inc(sem(tag), 1)

            turned_out("k1_done", (2, 3), K1)
            turned_out("q1_done", (4, 5), Q1)

            def features(n, name, b):
                pe.wait_ge(sem(f"{name}_lo"), nth(f"{name}_lo", 2))
                for tt in range(NT):
                    for kt in range(KT):
                        a = slice(n * 1024 + kt * T + tt * P, n * 1024 + kt * T + (tt + 1) * P)
                        f = slice(ST_FEAT + kt * M1, ST_FEAT + (kt + 1) * M1)
                        ins = mm3(bank[b][:, tt * M1:(tt + 1) * M1], wide_hi[:, a], wide_lo[:, a], st_hi[:, f],
                                  st_lo[:, f], kt == 0, kt == KT - 1)
                ins.then_inc(sem(f"{name}_feat"), 1)

            def norms(name, sq, c):
                pe.wait_ge(sem(f"{name}_sq"), nth(f"{name}_sq", 2))
                for tt in range(NT):
                    for kt in range(KT):
                        ins = pe.matmul(bank[7][:, c + tt:c + tt + 1], sq[:, kt * T + tt * P:kt * T + (tt + 1) * P],
                                        ones32[:, 0:1], start=(kt == 0), stop=(kt == KT - 1))
                ins.then_inc(sem(f"{name}_norm"), 1)

            pe.wait_ge(sem("raw_used"), RAW_STATIC + 1)
            norms("k1", flat(xn), 0)
            features(0, "k1", 6)
            pe.wait_ge(sem("k1_nb"), 1)
            norms("q1", fa, 8)
            features(1, "q1", 2)
            pe.wait_ge(sem("q1_lo"), nth("q1_lo", 2))
            tokens_out("v1_done", (4, 5), V1)
            pe.wait_ge(sem("sup_lo"), nth("sup_lo", 2))
            aggregate("agg1_done", (0, 1), 1)
            for tt in range(NT):
                pe.wait_ge(sem("qp"), tt + 1)
                for m in range(2):
                    ins = pe.transpose(bank[3][:, m * T + tt * P:m * T + (tt + 1) * P],
                                       fb[:, tt * M1 + m * P:tt * M1 + (m + 1) * P], ident[:, :])
            ins.then_inc(sem("qp_turned"), 1)
            pe.wait_ge(sem("q1_nb"), 1)
            pe.wait_ge(sem("kp_lo"), nth("kp_lo", 1))
            pe.wait_ge(sem("v1_lo"), nth("v1_lo", 2))
            for m in range(2):
                for tt in range(NT):
                    a = slice(tt * M1 + m * P, tt * M1 + (m + 1) * P)
                    b = slice(tt * D, (tt + 1) * D)
                    ins = mm3(bank[(6, 2)[m]][:, :], kf_hi[:, a], kf_lo[:, a], v_hi[:, b], v_lo[:, b], tt == 0,
                              tt == NT - 1)
                ins.then_inc(sem("kv1_done"), 1)
                for tt in range(NT):
                    a = slice(tt * M1 + m * P, tt * M1 + (m + 1) * P)
                    pe.matmul(bank[7][:, 16 + 2 * m:18 + 2 * m], kf_hi[:, a], ones[:, :], start=(tt == 0), stop=False)
                    ins = pe.matmul(bank[7][:, 16 + 2 * m:18 + 2 * m], kf_lo[:, a], ones[:, :], start=False,
                                    stop=(tt == NT - 1))
            ins.then_inc(sem("ksum1_done"), 1)
            pe.wait_ge(sem("qp_lo"), nth("qp_lo", 1))
            pe.wait_ge(sem("kv1_lo"), nth("kv1_lo", 2))
            for kt in range(KT):
                for m in range(2):
                    a = slice(m * D + kt * P, m * D + (kt + 1) * P)
                    b = slice(m * T, (m + 1) * T)
                    ins = mm3(bank[4 + kt // 2][:, (kt % 2) * T:(kt % 2 + 1) * T], xT_hi[:, a], xT_lo[:, a],
                              qf_hi[:, b], qf_lo[:, b], m == 0, m == 1)
                if kt % 2 == 1:
                    ins.then_inc(sem("y1_turned"), 1)
            pe.wait_ge(sem("ks1_lo"), nth("ks1_lo", 1))
            for tt in range(NT):
                for m in range(2):
                    a = slice(m * T + tt * P, m * T + (tt + 1) * P)
                    ins = mm3(bank[7][:, 24 + 2 * tt:26 + 2 * tt], qf_hi[:, a], qf_lo[:, a], ks_hi[:, m, 0:2],
                              ks_lo[:, m, 0:2], m == 0, m == 1)
            ins.then_inc(sem("den1_done"), 1)
            weights_ready(pe, PROJ1)
            pe.wait_ge(sem("y1_lo"), nth("y1_lo", 2))
            for tt in range(NT):
                for kt in range(KT):
                    a = slice(kt * T + tt * P, kt * T + (tt + 1) * P)
                    b = slice(kt * D, (kt + 1) * D)
                    ins = mm3(bank[(2, 6)[tt]][:, :], v_hi[:, a], v_lo[:, a], w_hi[PROJ1 % SLOTS][:, b],
                              w_lo[PROJ1 % SLOTS][:, b], kt == 0, kt == KT - 1)
                ins.then_inc(sem("p1_done"), 1)

            def router_and_f(tag):
                for kt in range(KT):
                    a = slice(ST_RF + kt * P, ST_RF + (kt + 1) * P)
                    b = slice(kt * T, (kt + 1) * T)
                    ins = mm3(bank[4][:, 0:T], st_hi[:, a], st_lo[:, a], xT_hi[:, b], xT_lo[:, b], kt == 0,
                              kt == KT - 1)
                ins.then_inc(sem(tag), 1)

            turn("ln4")
            pe.wait_ge(sem("ln4_lo"), nth("ln4_lo", 2))
            router_and_f("r_done")
            pe.wait_ge(sem("codebook_in"), 16)
            pe.wait_ge(sem("rT"), 1)
            for tt in range(NT):
                ins = pe.matmul(bank[5][:, tt * E1:(tt + 1) * E1], rT[:, tt * P:(tt + 1) * P], cbs[:, :], start=True,
                                stop=True)
            ins.then_inc(sem("lg1_done"), 1)
            for n, (kind, g) in enumerate(FFN1_ORDER):
                routed = g >= SHARED_GROUPS
                if kind == "up":
                    if g == SHARED_GROUPS:
                        for tt in range(NT):
                            pe.wait_ge(sem("comb1"), tt + 1)
                            ins = pe.transpose(bank[4][:, tt * P:(tt + 1) * P], comb[:, tt, :], ident[:, :])
                        ins.then_inc(sem("comb1_turned"), 1)
                        pe.wait_ge(sem("comb1_16"), 1)
                    up("ffn1", FFN1 + n, routed, g, 4 * (g - SHARED_GROUPS))
                else:
                    down("ffn1", FFN1 + n, g, g == 0, False)
            pe.wait_ge(sem("b2_1_in"), 16)
            for tt in range(NT):
                pe.matmul(bank[tt][:, :], combT[0:E1, tt * P:(tt + 1) * P], b2s[:, :], start=False,
                          stop=True).then_inc(sem("ffn1_out"), 1)
            turn("ln5")
            pe.wait_ge(sem("ln5_lo"), nth("ln5_lo", 2))
            router_and_f("f1_done")
            pe.wait_ge(sem("f1_lo"), nth("f1_lo", 1))
            for tt in range(NT):
                a = slice(tt * P, (tt + 1) * P)
                f = slice(ST_WF2, ST_WF2 + D)
                mm3(bank[2 + tt][:, :], f1_hi[64:P, a], f1_lo[64:P, a], st_hi[64:P, f], st_lo[64:P, f], True,
                    True).then_inc(sem("f2_done"), 1)

        @block.scalar
        def _(act):
            def high_block(i):
                r = raw_index(i)
                act.wait_ge(sem(f"raw_in{r % RAWS}"), nth(f"raw_in{r % RAWS}", 16 * (r // RAWS + 1)))
                if i >= SLOTS:
                    event, n = last_use(i - SLOTS)
                    act.wait_ge(sem(event), nth(event, n))
                act.activation(w_hi[i % SLOTS][:, :], raw[:, r % RAWS, :], ACT.Copy).then_inc(sem("hi_cut"), 1)

            def high_static():
                r = RAW_STATIC
                act.wait_ge(sem(f"raw_in{r % RAWS}"), nth(f"raw_in{r % RAWS}", 16 * (r // RAWS + 1)))
                act.activation(st_hi[:, :], raw[:, r % RAWS, :], ACT.Copy).then_inc(sem("static_hi_cut"), 1)

            def high(tag, o, i, wait, n, scale=1.0):
                act.wait_ge(sem(wait), nth(wait, n))
                act.activation(o, i, ACT.Copy, scale=scale).then_inc(sem(f"{tag}_hi"), 1)

            def high_turned(tag, o):
                for h in range(2):
                    high(tag, o[:, h * 512:(h + 1) * 512], bank[6 + h][:, :], f"{tag}_turned", h + 1)

            high_turned("ln0", xT_hi)
            for i in range(SLOTS):
                high_block(i)
            for h in range(2):
                high("adj", adj_hi[:, h, :], bank[h][:, :], "hot_used", ET)
            for n in range(2):
                for h in range(2):
                    high("fold", wide_hi[:, :].rearrange("p (m c) -> p m c", m=KT)[:, 2 * h:2 * h + 2,
                                                                                 n * T:(n + 1) * T],
                         bank[2 + 2 * n + h][:, :].rearrange("p (m c) -> p m c", m=2), "fold_done", 2 * n + h + 1)
                high_block(SLOTS + n)

            def elu_exp(name, i, o):
                act.wait_ge(sem(f"{name}_min"), nth(f"{name}_min", 1))
                act.activation(o, i, ACT.Exp).then_inc(sem(f"{name}_exp"), 1)

            elu_exp("q", fa[:, 0:512], fa[:, 512:1024])
            elu_exp("k", fb[:, 512:1024], xn[:, 0, :])
            high("q", qf_hi[:, :], fb[:, 0:512], "q_f", 1)
            high("k", kf_hi[:, :], xn[:, 1, :], "k_f", 1)
            for tt in range(NT):
                high("v", v_hi[:, tt * D:(tt + 1) * D], bank[4 + tt][:, :], "v_done", tt + 1)
            high_block(6)
            for tt in range(NT):
                high("pr", pr_hi[:, tt * D:(tt + 1) * D], fa[:, tt * D:(tt + 1) * D], "g_f", tt + 1)
            high_block(7)
            high("kv", xT_hi[:, 0:512], fb[:, 0:512], "kv_f", 2)
            high_turned("z", v_hi)
            high_static()
            high_block(8)
            high_turned("ln1", xT_hi)

            for tt in range(NT):
                act.wait_ge(sem("negmax0"), tt + 1)
                act.activation(pe_[:, tt, 0:E0], lg[:, tt, 0:E0], ACT.Exp, bias=wk[:, tt, 0:1],
                               accum_out=wk[:, tt, 1:2]).then_inc(sem("sum0"), 1)

            def hidden(tag, func, g, col):
                for j in range(2):
                    act.wait_ge(sem(f"{tag}_up"), nth(f"{tag}_up", 2 * g + j + 1))
                    if g:
                        act.wait_ge(sem(f"{tag}_scaled"), nth(f"{tag}_scaled", 2 * g - 1 + j))
                    for mm in range(2):
                        c = col + 4 * g + 2 * j + mm
                        act.activation(fa[:, j * 512 + mm * T:j * 512 + (mm + 1) * T],
                                       bank[2 + j][:, mm * T:(mm + 1) * T], func,
                                       bias=colsb[:, c:c + 1]).then_inc(sem(f"{tag}_act"), 1)

            act.wait_ge(sem("cols_in"), 16)
            hidden("ffn0", ACT.Relu, 0, COL_B1_0)
            high_block(9)
            high_turned("ln2", xT_hi)
            high_block(10)
            for tt in range(NT):
                high("sup", pr_hi[:, tt * D:(tt + 1) * D], bank[tt][:, :], "s_done", tt + 1)
            high_block(11)
            for name, n, f, sq in (("k1", 0, fa, flat(xn)), ("q1", 1, fb, fa)):
                for h in range(2):
                    a = slice(h * 512, (h + 1) * 512)
                    high(name, wide_hi[:, n * 1024 + h * 512:n * 1024 + (h + 1) * 512], f[:, a], f"{name}_f",
                         2 * h + 2)
                    if n:
                        act.wait_ge(sem("k1_sq"), 2)
                        act.wait_ge(sem("k1_lo"), nth("k1_lo", 2))
                    act.activation(sq[:, a], f[:, a], ACT.Square).then_inc(sem(f"{name}_sq"), 1)
                high_block(12 + n)
            act.wait_ge(sem("k1_nb"), 1)
            act.wait_ge(sem("q1_lo"), nth("q1_lo", 2))
            act.wait_ge(sem("q1_sq"), 2)
            for tt in range(NT):
                act.wait_ge(sem("k1_feat"), 1)
                act.activation(fb[:, 512 + tt * M1:512 + (tt + 1) * M1], bank[6][:, tt * M1:(tt + 1) * M1], ACT.Exp,
                               bias=nrm[:, 0, tt:tt + 1]).then_inc(sem("kp"), 1)
            high("kp", kf_hi[:, :], fb[:, 512:1024], "kp", 2, M1 ** -0.5)
            act.wait_ge(sem("q1_nb"), 1)
            act.wait_ge(sem("q1_feat"), 1)
            for tt in range(NT):
                act.activation(fb[:, tt * M1:(tt + 1) * M1], bank[2][:, tt * M1:(tt + 1) * M1], ACT.Exp,
                               bias=nrm[:, 1, tt:tt + 1]).then_inc(sem("qp"), 1)
            for tt in range(NT):
                high("v1", v_hi[:, tt * D:(tt + 1) * D], xn[:, tt, :], "v1_f", tt + 1)
            high("qp", qf_hi[:, :], bank[3][:, :], "qp_turned", 1, M1 ** -0.5)
            high_block(14)
            for m in range(2):
                high("kv1", xT_hi[:, m * D:(m + 1) * D], bank[(6, 2)[m]][:, :], "kv1_done", m + 1)
            for h in range(2):
                high("y1", v_hi[:, h * 512:(h + 1) * 512], bank[4 + h][:, :], "y1_turned", h + 1)
            high_block(15)
            for h in range(2):
                high("ln4", xT_hi[:, h * 512:(h + 1) * 512], fb[:, h * 512:(h + 1) * 512], "ln4_affine", 2 * h + 2)
            act.wait_ge(sem("r_done"), nth("r_done", 1))
            act.activation(rT[:, :], bank[4][0:64, 0:T], ACT.Copy).then_inc(sem("rT"), 1)
            for tt in range(NT):
                act.wait_ge(sem("negmax1"), tt + 1)
                act.activation(wk[:, tt, 2:4], top[:, tt, 0:2], ACT.Exp, bias=wk[:, tt, 0:1],
                               accum_out=wk[:, tt, 1:2]).then_inc(sem("sum1"), 1)
            act.wait_ge(sem("base2"), 2)
            ups = 0
            for n, (kind, g) in enumerate(FFN1_ORDER):
                if kind == "up":
                    hidden("ffn1", ACT.Silu, g, COL_B1)
                if FFN1 + n + SLOTS < BLOCKS:
                    high_block(FFN1 + n + SLOTS)
            for h in range(2):
                high("ln5", xT_hi[:, h * 512:(h + 1) * 512], fb[:, h * 512:(h + 1) * 512], "ln5_affine", 2 * h + 2)
            act.wait_ge(sem("f1_done"), nth("f1_done", 1))
            act.activation(fb[64:P, 0:T], bank[4][64:P, 0:T], ACT.Silu,
                           bias=colsb[64:P, COL_BF1:COL_BF1 + 1]).then_inc(sem("f1_f"), 1)
            high("f1", f1_hi[64:P, 0:T], fb[64:P, 0:T], "f1_f", 1)

        @block.vector
        def _(dve):
            def stats(tag, tiles, wait):
                for tt in range(NT):
                    dve.wait_ge(sem(wait[0]), nth(wait[0], wait[1] if wait[1] == 16 else tt + 1))
                    dve.bn_stats(st[:, tt, :], tiles[tt]).then_inc(sem(f"{tag}_bn"), 1)
                    dve.wait_ge(sem(f"{tag}_bn"), nth(f"{tag}_bn", tt + 1))
                    dve.bn_aggr(mv[:, tt, :], st[:, tt, :]).then_inc(sem(f"{tag}_mv"), 1)
                dve.wait_ge(sem(f"{tag}_mv"), nth(f"{tag}_mv", NT))
                dve.tensor_scalar(ve[:, :], mv[:, :, 1], LN_EPS, None, ALU.add).then_inc(sem(f"{tag}_var"), 1)

            def normalize(tag, tiles, outs):
                dve.wait_ge(sem(f"{tag}_rstd"), nth(f"{tag}_rstd", 1))
                for tt in range(NT):
                    dve.tensor_scalar(outs[tt], tiles[tt], mv[:, tt, 0:1], rstd[:, tt:tt + 1], ALU.subtract,
                                      ALU.mult).then_inc(sem(f"{tag}_xn"), 1)

            def low(tag, o, i, hi, n=1):
                dve.wait_ge(sem(f"{tag}_hi"), nth(f"{tag}_hi", n))
                dve.tensor_tensor(o, i, f32(hi), ALU.subtract).then_inc(sem(f"{tag}_lo"), 1)

            def low_turned(tag, lo, hi):
                for h in range(2):
                    a = slice(h * 512, (h + 1) * 512)
                    low(tag, lo[:, a], bank[6 + h][:, :], hi[:, a], h + 1)

            x_tiles = [xs[:, tt, :] for tt in range(NT)]
            xn_tiles = [xn[:, tt, :] for tt in range(NT)]
            fa_tiles = [fa[:, tt * D:(tt + 1) * D] for tt in range(NT)]

            dve.memset(ones32[:, :], 1.0).then_inc(sem("ones32_made"), 1)
            dve.wait_ge(sem("ones32_made"), 1)
            dve.tensor_copy(ones[:, :], ones32[:, :]).then_inc(sem("ones_made"), 1)
            for q in range(4):
                dve.memset(pcol[32 * q:32 * q + 32, 1:2], float(q))
            dve.memset(pcol[0:64, 3:4], 1.0)
            dve.memset(pcol[64:P, 3:4], 1.0 / LO_SCALE).then_inc(sem("pcol_made"), 1)
            stats("ln0", x_tiles, ("x_in", 16))
            dve.wait_ge(sem("src_in"), 16)
            dve.wait_ge(sem("dst_in"), 16)
            dve.wait_ge(sem("ew_in"), 16)
            dve.tensor_copy(edge_f[:, :, :], edge_i[:, :, :]).then_inc(sem("edges"), 1)
            dve.tensor_copy(ew_hi[:, :], ewf[:, :]).then_inc(sem("ew_cut"), 1)
            dve.wait_ge(sem("ew_cut"), 1)
            dve.tensor_tensor(ew_lo[:, :], ewf[:, :], f32(ew_hi[:, :]), ALU.subtract).then_inc(sem("ew_cut"), 1)
            normalize("ln0", x_tiles, xn_tiles)
            dve.wait_ge(sem("edges"), 1)
            dve.wait_ge(sem("ew_cut"), 2)
            dve.wait_ge(sem("iota_made"), 1)
            for j in range(ET):
                if j >= 2:
                    dve.wait_ge(sem("hot_used"), j - 1)
                hot = (v_hi, v_lo)[j % 2]
                s, d = edge_f[:, 0, j:j + 1], edge_f[:, 1, j:j + 1]
                dve.tensor_scalar(hot[:, 0:T], iota[:, :], d, None, ALU.is_equal)
                dve.tensor_scalar(hot[:, T:2 * T], iota[:, :], s, None, ALU.is_equal)
                dve.tensor_scalar(hot[:, 2 * T:3 * T], iota[:, :], s, f32(ew_hi[:, j:j + 1]), ALU.is_equal, ALU.mult)
                dve.tensor_scalar(hot[:, 3 * T:4 * T], iota[:, :], s, ew_lo[:, j:j + 1], ALU.is_equal,
                                  ALU.mult).then_inc(sem("hot"), 1)
                if j == 3:
                    low_turned("ln0", xT_lo, xT_hi)
                if j == 4:
                    dve.wait_ge(sem("small_in"), 16)
                    dve.tensor_copy(sm_hi[:, :], smr[:, :]).then_inc(sem("small_hi"), 1)
                    dve.wait_ge(sem("small_hi"), nth("small_hi", 1))
                    dve.tensor_tensor(sm_lo[:, :], smr[:, :], f32(sm_hi[:, :]), ALU.subtract)\
                       .then_inc(sem("small_cut"), 1)
            for h in range(2):
                low("adj", adj_lo[:, h, :], bank[h][:, :], adj_hi[:, h, :], h + 1)

            def folded(t, n, h):
                return t[:, :].rearrange("p (m c) -> p m c", m=KT)[:, 2 * h:2 * h + 2, n * T:(n + 1) * T]

            for n in range(2):
                for h in range(2):
                    low("fold", folded(wide_lo, n, h), bank[2 + 2 * n + h][:, :].rearrange("p (m c) -> p m c", m=2),
                        folded(wide_hi, n, h), 2 * n + h + 1)

            dve.wait_ge(sem("q_done"), nth("q_done", 1))
            dve.tensor_scalar(fa[:, 0:512], bank[2][:, :], 0.0, None, ALU.min).then_inc(sem("q_min"), 1)
            dve.wait_ge(sem("k_done"), nth("k_done", 1))
            dve.tensor_scalar(fb[:, 512:1024], bank[3][:, :], 0.0, None, ALU.min).then_inc(sem("k_min"), 1)
            dve.wait_ge(sem("q_exp"), 1)
            dve.scalar_tensor_tensor(out=fb[:, 0:512], in0=bank[2][:, :], scalar=0.0, in1=fa[:, 512:1024],
                                     op0=ALU.max, op1=ALU.add).then_inc(sem("q_f"), 1)
            dve.wait_ge(sem("k_exp"), 1)
            dve.scalar_tensor_tensor(out=xn[:, 1, :], in0=bank[3][:, :], scalar=0.0, in1=xn[:, 0, :],
                                     op0=ALU.max, op1=ALU.add).then_inc(sem("k_f"), 1)
            low("q", qf_lo[:, :], fb[:, 0:512], qf_hi[:, :])
            low("k", kf_lo[:, :], xn[:, 1, :], kf_hi[:, :])
            dve.wait_ge(sem("heads_made"), 1)
            dve.wait_ge(sem("pcol_made"), 1)
            dve.tensor_scalar(blockmask[:, :], blockmask[:, :], pcol[:, 1:2], None,
                              ALU.is_equal).then_inc(sem("blockmask"), 1)
            for tt in range(NT):
                low("v", v_lo[:, tt * D:(tt + 1) * D], bank[4 + tt][:, :], v_hi[:, tt * D:(tt + 1) * D], tt + 1)
            dve.wait_ge(sem("rows0_in"), 16)
            dve.wait_ge(sem("q_f"), nth("q_f", 1))
            for tt in range(NT):
                dve.wait_ge(sem("g_done"), nth("g_done", tt + 1))
                dve.tensor_tensor(fa_tiles[tt], bank[tt][:, :], rows[:, ROW_GNN0, :], ALU.add).then_inc(sem("g_f"), 1)
            for tt in range(NT):
                low("pr", pr_lo[:, tt * D:(tt + 1) * D], fa_tiles[tt], pr_hi[:, tt * D:(tt + 1) * D], tt + 1)
            dve.wait_ge(sem("kv_done"), nth("kv_done", 1))
            dve.wait_ge(sem("blockmask"), 1)
            dve.wait_ge(sem("q_lo"), nth("q_lo", 1))
            for m in range(2):
                dve.tensor_tensor(fb[:, m * 256:(m + 1) * 256], bank[2][:, m * 256:(m + 1) * 256], blockmask[:, :],
                                  ALU.mult).then_inc(sem("kv_f"), 1)
            dve.tensor_copy(ks[:, :], bank[3][:, 0:4:2]).then_inc(sem("ks"), 1)
            dve.wait_ge(sem("ks"), 1)
            for m in range(2):
                dve.tensor_scalar(ksb[:, m, :], blockmask[:, 0:256:HD], ks[:, m:m + 1], None,
                                  ALU.mult).then_inc(sem("ksb"), 1)
            dve.wait_ge(sem("ksb"), 2)
            dve.tensor_copy(ks_hi[:, :, :], ksb[:, :, :]).then_inc(sem("ks_hi"), 1)
            dve.wait_ge(sem("ks_hi"), nth("ks_hi", 1))
            dve.tensor_tensor(ks_lo[:, :, :], ksb[:, :, :], f32(ks_hi[:, :, :]), ALU.subtract)
            low("kv", xT_lo[:, 0:512], fb[:, 0:512], xT_hi[:, 0:512])
            dve.wait_ge(sem("k_lo"), nth("k_lo", 1))
            for tt in range(NT):
                dve.wait_ge(sem("z_done"), nth("z_done", 2))
                dve.tensor_scalar(nrm[:, tt, :], bank[3][:, 64 + 8 * tt:72 + 8 * tt], NORM_EPS, None,
                                  ALU.add).then_inc(sem("nrm"), 1)
                dve.wait_ge(sem("nrm"), tt + 1)
                dve.reciprocal(rden[:, tt, :], nrm[:, tt, :]).then_inc(sem("rden"), 1)
                dve.wait_ge(sem("rden"), tt + 1)
                dve.tensor_tensor(xn[:, tt, :].rearrange("p (h f) -> p h f", h=HEADS),
                                  bank[4 + tt][:, :].rearrange("p (h f) -> p h f", h=HEADS),
                                  rden[:, tt, :].unsqueeze(2).to_broadcast([P, HEADS, HD]),
                                  ALU.mult).then_inc(sem("z_xn"), 1)
            low_turned("z", v_lo, v_hi)
            for tt in range(NT):
                dve.wait_ge(sem("o_done"), nth("o_done", tt + 1))
                dve.wait_ge(sem("base0"), tt + 1)
                dve.tensor_tensor(base[:, tt, :], bank[tt][:, :], base[:, tt, :], ALU.add).then_inc(sem("mixed0"), 1)
            dve.wait_ge(sem("deg_done"), nth("deg_done", 1))
            dve.tensor_copy(deg[:, :], bank[4][:, 0:4:2]).then_inc(sem("deg"), 1)
            dve.wait_ge(sem("deg"), 1)
            dve.reciprocal(degr[:, :], deg[:, :]).then_inc(sem("degr"), 1)
            dve.wait_ge(sem("degr"), 1)
            for tt in range(NT):
                dve.wait_ge(sem("agg0_done"), nth("agg0_done", tt + 1))
                dve.wait_ge(sem("mixed0"), tt + 1)
                dve.scalar_tensor_tensor(out=xs[:, tt, :], in0=bank[2 + tt][:, :], scalar=degr[:, tt:tt + 1],
                                         in1=base[:, tt, :], op0=ALU.mult, op1=ALU.add).then_inc(sem("x1"), 1)
            stats("ln1", x_tiles, ("x1", 1))
            normalize("ln1", x_tiles, xn_tiles)
            low_turned("ln1", xT_lo, xT_hi)

            def select(n, tt, k):
                w = (E0, E1)[n]
                dve.max(top[:, tt, :], lg[:, tt, 0:w]).then_inc(sem(f"top{n}"), 1)
                dve.wait_ge(sem(f"top{n}"), nth(f"top{n}", tt + 1))
                dve.tensor_scalar(wk[:, tt, 0:1], top[:, tt, 0:1], -1.0, None, ALU.mult).then_inc(sem(f"negmax{n}"), 1)
                dve.max_index(topi[:, tt, :], top[:, tt, :], lg[:, tt, 0:w]).then_inc(sem(f"topi{n}"), 1)
                dve.wait_ge(sem(f"topi{n}"), nth(f"topi{n}", tt + 1))
                dve.tensor_copy(topf[:, tt, 0:k], topi[:, tt, 0:k]).then_inc(sem(f"topf{n}"), 1)

            def spread_halves(n, b):
                dve.wait_ge(sem(f"comb{n}_turned"), nth(f"comb{n}_turned", 1))
                dve.tensor_copy(combT16[:, :], b[:, 0:T]).then_inc(sem(f"comb{n}_hi"), 1)
                dve.tensor_copy(combT[0:64, :], b[0:64, 0:T])
                dve.wait_ge(sem(f"comb{n}_hi"), nth(f"comb{n}_hi", 1))
                dve.tensor_tensor(combT[64:P, :], b[64:P, 0:T], combT16[64:P, :], ALU.subtract)\
                   .then_inc(sem(f"comb{n}_lo"), 1)
                dve.wait_ge(sem(f"comb{n}_lo"), nth(f"comb{n}_lo", 1))
                dve.tensor_scalar(combT16[64:P, :], combT[64:P, :], LO_SCALE, None, ALU.mult)\
                   .then_inc(sem(f"comb{n}_16"), 1)

            dve.wait_ge(sem("bg_in"), 16)
            dve.wait_ge(sem("lg0_done"), nth("lg0_done", 1))
            dve.tensor_tensor(lg[:, :, 0:E0], bank[4][:, 8:24].rearrange("p (t e) -> p t e", t=NT),
                              bgs[:, :].unsqueeze(1).to_broadcast([P, NT, E0]), ALU.add).then_inc(sem("lg0"), 1)
            dve.wait_ge(sem("lg0"), 1)
            dve.wait_ge(sem("iota2_made"), 1)
            for tt in range(NT):
                select(0, tt, 1)
            for tt in range(NT):
                dve.wait_ge(sem("sum0"), tt + 1)
                dve.reciprocal(wk[:, tt, 2:3], wk[:, tt, 1:2]).then_inc(sem("score0"), 1)
                dve.wait_ge(sem("score0"), tt + 1)
                dve.wait_ge(sem("topf0"), tt + 1)
                dve.tensor_scalar(comb[:, tt, :], iota2[:, :], topf[:, tt, 0:1], wk[:, tt, 2:3], ALU.is_equal,
                                  ALU.mult).then_inc(sem("comb0"), 1)
            spread_halves(0, bank[5])
            dve.wait_ge(sem("pidx_made"), 1)
            dve.tensor_copy(pcol[0:64, 2:3], pcol[0:64, 0:1])
            dve.wait_ge(sem("experts_made"), 1)
            dve.tensor_scalar(pcol[64:P, 2:3], pcol[64:P, 0:1], -64.0, None, ALU.add).then_inc(sem("pmod"), 1)
            dve.wait_ge(sem("pmod"), 1)
            dve.tensor_scalar(sel[:, :], sel[:, :], pcol[:, 2:3], pcol[:, 3:4], ALU.is_equal,
                              ALU.mult).then_inc(sem("sel_made"), 1)

            def hidden(tag, g, routed):
                for j in range(2):
                    a = slice(j * 512, (j + 1) * 512)
                    o = slice((g % 2) * 1024 + j * 512, (g % 2) * 1024 + (j + 1) * 512)
                    dve.wait_ge(sem(f"{tag}_act"), nth(f"{tag}_act", 4 * g + 2 * j + 2))
                    if g:
                        dve.wait_ge(sem(f"{tag}_act_lo"), nth(f"{tag}_act_lo", 2 * g - 1 + j))
                    if routed:
                        n = g - (SHARED_GROUPS if tag == "ffn1" else 0)
                        dve.wait_ge(sem(f"{tag}_spread"), nth(f"{tag}_spread", 2 * n + j + 1))
                        dve.tensor_tensor(fb[:, a], fa[:, a], bank[6 + j][:, :], ALU.mult)\
                           .then_inc(sem(f"{tag}_scaled"), 1)
                    else:
                        dve.tensor_scalar(fb[:, a], fa[:, a], SHARED_SCALE, None, ALU.mult)\
                           .then_inc(sem(f"{tag}_scaled"), 1)
                    dve.wait_ge(sem(f"{tag}_scaled"), nth(f"{tag}_scaled", 2 * g + j + 1))
                    if g >= 2:
                        dve.wait_ge(sem(f"{tag}_down"), nth(f"{tag}_down", 2 * (g - 2) + j + 1))
                    dve.tensor_copy(wide_hi[:, o], fb[:, a]).then_inc(sem(f"{tag}_act_hi"), 1)
                    dve.wait_ge(sem(f"{tag}_act_hi"), nth(f"{tag}_act_hi", 2 * g + j + 1))
                    dve.tensor_tensor(wide_lo[:, o], fb[:, a], f32(wide_hi[:, o]), ALU.subtract)\
                       .then_inc(sem(f"{tag}_act_lo"), 1)

            hidden("ffn0", 0, True)
            for tt in range(NT):
                dve.wait_ge(sem("ffn0_out"), tt + 1)
                dve.tensor_tensor(xs[:, tt, :], bank[tt][:, :], xs[:, tt, :], ALU.add).then_inc(sem("x2"), 1)
            stats("ln2", x_tiles, ("x2", 1))
            normalize("ln2", x_tiles, xn_tiles)
            low_turned("ln2", xT_lo, xT_hi)
            for tt in range(NT):
                low("sup", pr_lo[:, tt * D:(tt + 1) * D], bank[tt][:, :], pr_hi[:, tt * D:(tt + 1) * D], tt + 1)
            dve.wait_ge(sem("cols_in"), 16)
            for name, n, f, col in (("k1", 0, fa, COL_BK), ("q1", 1, fb, COL_BQ)):
                for h in range(2):
                    dve.wait_ge(sem(f"{name}_done"), nth(f"{name}_done", h + 1))
                    for mm in range(2):
                        m = 2 * h + mm
                        dve.tensor_scalar(f[:, m * T:(m + 1) * T], bank[2 + 2 * n + h][:, mm * T:(mm + 1) * T],
                                          colsb[:, col + m:col + m + 1], None, ALU.add).then_inc(sem(f"{name}_f"), 1)
                for h in range(2):
                    a = slice(h * 512, (h + 1) * 512)
                    o = slice(n * 1024 + h * 512, n * 1024 + (h + 1) * 512)
                    low(name, wide_lo[:, o], f[:, a], wide_hi[:, o], h + 1)
            for n, name in enumerate(("k1", "q1")):
                dve.wait_ge(sem(f"{name}_norm"), nth(f"{name}_norm", 1))
                dve.tensor_scalar(nrm[:, n, 0:2], bank[7][:, 8 * n:8 * n + 2], -0.5, None,
                                  ALU.mult).then_inc(sem(f"{name}_nb"), 1)

            def low_scaled(tag, lo, i, hi):
                dve.wait_ge(sem(f"{tag}_hi"), nth(f"{tag}_hi", 1))
                dve.scalar_tensor_tensor(out=lo, in0=i, scalar=M1 ** -0.5, in1=f32(hi), op0=ALU.mult,
                                         op1=ALU.subtract).then_inc(sem(f"{tag}_lo"), 1)

            low_scaled("kp", kf_lo[:, :], fb[:, 512:1024], kf_hi[:, :])
            dve.wait_ge(sem("rows1_in"), 16)
            for tt in range(NT):
                dve.wait_ge(sem("v1_done"), nth("v1_done", tt + 1))
                dve.tensor_tensor(xn[:, tt, :], bank[4 + tt][:, :], rows[:, ROW_V1, :], ALU.add)\
                   .then_inc(sem("v1_f"), 1)
            for tt in range(NT):
                a = slice(tt * D, (tt + 1) * D)
                low("v1", v_lo[:, a], xn[:, tt, :], v_hi[:, a], tt + 1)
            low_scaled("qp", qf_lo[:, :], bank[3][:, :], qf_hi[:, :])
            for m in range(2):
                a = slice(m * D, (m + 1) * D)
                low("kv1", xT_lo[:, a], bank[(6, 2)[m]][:, :], xT_hi[:, a], m + 1)
            dve.wait_ge(sem("ksum1_done"), nth("ksum1_done", 1))
            sums = bank[7][:, 16:20].rearrange("p (m c) -> p m c", m=2)
            dve.tensor_copy(ks_hi[:, :, 0:2], sums).then_inc(sem("ks1_hi"), 1)
            dve.wait_ge(sem("ks1_hi"), nth("ks1_hi", 1))
            dve.tensor_tensor(ks_lo[:, :, 0:2], sums, f32(ks_hi[:, :, 0:2]), ALU.subtract).then_inc(sem("ks1_lo"), 1)
            for h in range(2):
                a = slice(h * 512, (h + 1) * 512)
                low("y1", v_lo[:, a], bank[4 + h][:, :], v_hi[:, a], h + 1)
            dve.wait_ge(sem("den1_done"), nth("den1_done", 1))
            dve.tensor_scalar(deg[:, :], bank[7][:, 24:28:2], DENOM_EPS, None, ALU.add).then_inc(sem("den1"), 1)
            dve.wait_ge(sem("den1"), 1)
            dve.reciprocal(degr[:, :], deg[:, :]).then_inc(sem("denr1"), 1)
            for tt in range(NT):
                dve.wait_ge(sem("agg1_done"), nth("agg1_done", tt + 1))
                dve.wait_ge(sem("base1"), 4)
                dve.tensor_tensor(base[:, tt, :], bank[tt][:, :], base[:, tt, :], ALU.add).then_inc(sem("mixed1"), 1)
            dve.wait_ge(sem("denr1"), 1)
            for tt in range(NT):
                dve.wait_ge(sem("p1_done"), nth("p1_done", tt + 1))
                dve.wait_ge(sem("mixed1"), tt + 1)
                dve.scalar_tensor_tensor(out=xs[:, tt, :], in0=bank[(2, 6)[tt]][:, :], scalar=degr[:, tt:tt + 1],
                                         in1=base[:, tt, :], op0=ALU.mult, op1=ALU.add).then_inc(sem("x3"), 1)
            stats("ln3", x_tiles, ("x3", 1))
            normalize("ln3", x_tiles, fa_tiles)
            stats("ln4", fa_tiles, ("ln3_xn", 1))
            normalize("ln4", fa_tiles, xn_tiles)

            def affine(tag, g, b):
                for kt in range(KT):
                    dve.wait_ge(sem(f"{tag}_turned"), nth(f"{tag}_turned", kt // 2 + 1))
                    dve.tensor_scalar(fb[:, kt * T:(kt + 1) * T], bank[6 + kt // 2][:, (kt % 2) * T:(kt % 2 + 1) * T],
                                      colsb[:, g + kt:g + kt + 1], colsb[:, b + kt:b + kt + 1], ALU.mult,
                                      ALU.add).then_inc(sem(f"{tag}_affine"), 1)
                for h in range(2):
                    a = slice(h * 512, (h + 1) * 512)
                    low(tag, xT_lo[:, a], fb[:, a], xT_hi[:, a], h + 1)

            affine("ln4", COL_LN_G, COL_LN_B)
            dve.wait_ge(sem("lg1_done"), nth("lg1_done", 1))
            dve.tensor_scalar(lg[:, :, :], bank[5][:, 0:NT * E1].rearrange("p (t e) -> p t e", t=NT), 1.0 / TEMP,
                              None, ALU.mult).then_inc(sem("lg1"), 1)
            dve.wait_ge(sem("lg1"), 1)
            for tt in range(NT):
                select(1, tt, 2)
            for tt in range(NT):
                dve.wait_ge(sem("sum1"), tt + 1)
                dve.reciprocal(wk[:, tt, 4:5], wk[:, tt, 1:2]).then_inc(sem("score1"), 1)
                dve.wait_ge(sem("score1"), tt + 1)
                dve.tensor_scalar(wk[:, tt, 5:7], wk[:, tt, 2:4], wk[:, tt, 4:5], None, ALU.mult)\
                   .then_inc(sem("weights1"), 1)
                dve.wait_ge(sem("weights1"), tt + 1)
                dve.wait_ge(sem("topf1"), tt + 1)
                for k, c in enumerate((comb, comb2)):
                    dve.tensor_scalar(c[:, tt, :], iota2[:, :], topf[:, tt, k:k + 1], wk[:, tt, 5 + k:6 + k],
                                      ALU.is_equal, ALU.mult).then_inc(sem("picked"), 1)
                dve.wait_ge(sem("picked"), 2 * tt + 2)
                dve.tensor_tensor(comb[:, tt, :], comb[:, tt, :], comb2[:, tt, :], ALU.add).then_inc(sem("comb1"), 1)
            hidden("ffn1", 0, False)
            spread_halves(1, bank[4])
            for g in range(1, GROUPS):
                hidden("ffn1", g, g >= SHARED_GROUPS)
            for tt in range(NT):
                dve.wait_ge(sem("ffn1_out"), tt + 1)
                dve.scalar_tensor_tensor(out=fa_tiles[tt], in0=rows[:, ROW_SH, :], scalar=SHARED_SCALE,
                                         in1=bank[tt][:, :], op0=ALU.mult, op1=ALU.add).then_inc(sem("hmoe"), 1)
            stats("ln5", fa_tiles, ("hmoe", 1))
            normalize("ln5", fa_tiles, xn_tiles)
            affine("ln5", COL_FF_G, COL_FF_B)
            low("f1", f1_lo[64:P, 0:T], fb[64:P, 0:T], f1_hi[64:P, 0:T])
            for tt in range(NT):
                dve.wait_ge(sem("f2_done"), nth("f2_done", tt + 1))
                dve.wait_ge(sem("base3"), tt + 1)
                dve.tensor_tensor(xs[:, tt, :], bank[2 + tt][:, :], base[:, tt, :], ALU.add).then_inc(sem("y_done"), 1)


def blocks_of(m):
    return m.reshape(KT, P, -1).transpose(1, 0, 2).reshape(P, -1)


def kernel(**inputs):
    import concourse.bacc as bacc
    from concourse.bass_utils import run_bass_kernel_spmd

    w = {k: np.asarray(v) for k, v in inputs.items()}
    qkv0, qkv1 = w["L0_mix_W_qkv"], w["L1_mix_w_qkv"]
    blocks = [
        qkv0[:, 0:D].T, qkv0[:, D:2 * D].T, qkv0[:, 2 * D:], w["L0_gnn_W"].T, w["L0_mix_W_out"],
        w["L0_ffn_W1"].transpose(1, 0, 2).reshape(D, D), w["L0_ffn_W2"].reshape(D, D), w["L1_gnn_weight"],
        qkv1[0:D].T, qkv1[D:2 * D].T, qkv1[2 * D:].T, w["L1_mix_w_proj"].T,
    ]
    ws1, ws2, w1, w2 = w["L1_ffn_Ws1"], w["L1_ffn_Ws2"], w["L1_ffn_W1"], w["L1_ffn_W2"]
    for kind, g in FFN1_ORDER:
        if g < SHARED_GROUPS:
            blocks.append(ws1[:, g * D:(g + 1) * D] if kind == "up" else ws2[g * D:(g + 1) * D])
        else:
            e = slice((g - SHARED_GROUPS) * D // DFF, (g - SHARED_GROUPS + 1) * D // DFF)
            blocks.append(w1[e].transpose(1, 0, 2).reshape(D, D) if kind == "up" else w2[e].reshape(D, D))
    static = np.zeros((P, 2048), np.float32)
    static[:, ST_FEAT:ST_RF] = blocks_of(w["L1_mix_w_feat"].T)
    static[:, ST_RF:ST_WF2] = blocks_of(np.concatenate([w["L1_ffn_Wr"], w["L1_ffn_Wf1"]], 1))
    static[64:P, ST_WF2:ST_WF2 + D] = w["L1_ffn_Wf2"]
    packed = [blocks_of(b) for b in blocks]
    packed.insert(STATIC_AT, static)
    cols = np.zeros((P, COLS), np.float32)
    for at, v in ((COL_B1_0, w["L0_ffn_b1"]), (COL_LN_G, w["L1_ffn_ln1_g"]), (COL_LN_B, w["L1_ffn_ln1_b"]),
                  (COL_FF_G, w["L1_ffn_ffln_g"]), (COL_FF_B, w["L1_ffn_ffln_b"]), (COL_BK, w["L1_mix_b_qkv"][0:D]),
                  (COL_BQ, w["L1_mix_b_qkv"][D:2 * D]), (COL_B1, w["L1_ffn_bs1"]), (COL_B1 + 8, w["L1_ffn_b1"])):
        v = v.reshape(-1, P).T
        cols[:, at:at + v.shape[1]] = v
    cols[64:P, COL_BF1] = w["L1_ffn_bf1"]
    small = np.zeros((P, SMALL), np.float32)
    small[0:HD, 0:FD] = small[HD:P, FD:HD] = w["L0_mix_random_matrix"]
    small[:, SM_WG:] = blocks_of(w["L0_ffn_Wg"])
    arrays = {
        "x": w["x"], "src": w["src"].reshape(P, ET), "dst": w["dst"].reshape(P, ET),
        "ew": w["edge_weight"].reshape(P, ET), "stream": np.stack(packed), "cols": cols, "small": small,
        "bg": w["L0_ffn_bg"].reshape(1, E0),
        "rows0": np.stack([w["L0_gnn_b"], w["L0_mix_b_out"]]),
        "rows1": np.stack([w["L1_gnn_bias"], w["L1_mix_b_proj"], w["L1_mix_b_qkv"][2 * D:], w["L1_ffn_bs2"],
                           w["L1_ffn_bf2"]]),
        "codebook": w["L1_ffn_codebook"].T, "b2_0": w["L0_ffn_b2"], "b2_1": w["L1_ffn_b2"],
    }
    arrays = {k: np.ascontiguousarray(v) for k, v in arrays.items()}
    nc = bacc.Bacc("TRN2", target_bir_lowering=False, num_devices=1)
    aps = {k: nc.dram_tensor(k, v.shape, mybir.dt.from_np(v.dtype), kind="ExternalInput").ap()
           for k, v in arrays.items()}
    out = nc.dram_tensor("out", (T, D), F32, kind="ExternalOutput").ap()
    gnn_kernel(nc, out=out, **aps)
    r = run_bass_kernel_spmd(nc, [arrays], core_ids=[0])
    return r.results[0]["out"]
```

```python
from contextlib import ExitStack

import numpy as np

import concourse.bass as bass
from concourse import mybir

ALU = mybir.AluOpType
ACT = mybir.ActivationFunctionType
F32 = mybir.dt.float32
F32R = mybir.dt.float32r
F16 = mybir.dt.float16
I32 = mybir.dt.int32
U32 = mybir.dt.uint32

P = 128
T = 256
D = 512
NT = T // P
KT = D // P
EDGES = 4352
ET = EDGES // P
HEADS = 8
HD = D // HEADS
FD = HD // 2
E0 = 8
E1 = 64
DFF = 64
M1 = 256
SHARED_GROUPS = 2
GROUPS = SHARED_GROUPS + E1 * DFF // D
LN_EPS = 1e-5
NORM_EPS = 1e-6
DENOM_EPS = 1e-8
TEMP = 0.7
SHARED_SCALE = 0.25
LO_SCALE = 4096.0

HOTS = 4
TURN_AT, FOLD_AT, QUERY_AT, KEY_AT, VALUE_AT = 1, 3, 12, 15, 17
GNN_AT = VALUE_AT + NT * KT
SLOTS = 4
RAWS = 3

UNSPLIT = 2
V0, GNN0, OUT0, UP0, DOWN0, GNN1, K1, Q1, V1, PROJ1, FFN1 = range(11)
STATIC_AT = K1


def ffn1_blocks():
    order = [("up", 0)]
    for g in range(GROUPS):
        if g + 1 < GROUPS:
            order.append(("up", g + 1))
        order.append(("down", g))
    return order


FFN1_ORDER = ffn1_blocks()
BLOCKS = FFN1 + len(FFN1_ORDER)


def raw_index(i):
    return UNSPLIT + i + (1 if i >= STATIC_AT else 0)


RAW_STATIC = UNSPLIT + STATIC_AT
N_RAW = UNSPLIT + BLOCKS + 1

COL_B1_0, COL_LN_G, COL_LN_B, COL_FF_G, COL_FF_B, COL_BK, COL_BQ, COL_B1 = 0, 4, 8, 12, 16, 20, 24, 28
COL_BF1 = COL_B1 + 4 * GROUPS
COLS = COL_BF1 + 1
SM_R, SM_WG = 0, HD
SMALL = HD + KT * E0
ST_FEAT, ST_RF = 0, KT * M1
ROW_GNN0, ROW_OUT0 = 3, 4
ROW_GNN1, ROW_PROJ1, ROW_V1, ROW_SH, ROW_F2 = 0, 1, 2, 3, 4


NORMS = (("ln0", 2), ("z", 2), ("ln1", 2), ("ln2", 2), ("ln4", 2), ("ln3", 2), ("ln5", 2))
LN = (("ln0", 2), ("ln1", 2), ("ln2", 2), ("ln3", 2), ("ln5", 2))
CUTS = (("ln0", 2), ("fold", 4), ("q", 1), ("k", 1), ("v", 2), ("adj", 2), ("pr", 2), ("kv", 1), ("z", 2), ("ln1", 2),
        ("ln2", 2), ("sup", 2), ("k1", 2), ("q1", 2), ("kp", 1), ("v1", 2), ("qp", 1), ("kv1", 2), ("y1", 2),
        ("ln4", 2), ("ln5", 2))
SERIES = {
    "bn": LN, "mv": LN, "var": LN, "rstd": LN, "xn": NORMS,
    "turned": tuple(n for n in NORMS if n[0] != "ln3"), "hi": CUTS, "lo": CUTS, "affine": (("ln4", 4), ("ln5", 4)), "affine2": (("ln4", 4), ("ln5", 4)),
    "f": (("q", 1), ("k", 1), ("kv", 2), ("k1", 4), ("q1", 4), ("v1", 2)),
    "done": (("fold", 4), ("q", 1), ("k", 1), ("v", 2), ("g", 2), ("kv", 1), ("agg0", 2), ("z", 2), ("o", 2),
             ("lg0", 1), ("s", 2), ("k1", 2), ("q1", 2), ("v1", 2), ("kv1", 2),
             ("ksum1", 1), ("den1", 1), ("p1", 2), ("r", 1), ("lg1", 1)),
}


def series(name):
    stage, _, what = name.rpartition("_")
    before = 0
    for other, times in SERIES.get(what, ()):
        if other == stage:
            return f"all_{what}", before
        before += times
    return name, 0


def nth(name, n):
    return series(name)[1] + n


def last_use(i):
    if i < FFN1:
        return (("v_done", 2), ("g_done", 2), ("o_done", 2), ("ffn0_up", 2),
                ("ffn0_out", 2), ("s_done", 2), ("k1_done", 2), ("q1_done", 2), ("v1_done", 2), ("p1_done", 2))[i]
    kind, g = FFN1_ORDER[i - FFN1]
    return f"ffn1_{kind}", 2 * g + 2


def gnn_kernel(nc, x, src, dst, ew, stream, cols, small, bg, rows0, rows1, codebook, b2_0, b2_1, wf2, out):
    with ExitStack() as ctx:
        def sb(name, shape, dt=F32):
            return ctx.enter_context(nc.sbuf_tensor(name, shape, dt))

        sems = {}

        def sem(name):
            name = series(name)[0]
            if name not in sems:
                sems[name] = ctx.enter_context(nc.semaphore(name))
            return sems[name]

        bank = [ctx.enter_context(nc.psum_tensor(f"bank{i}", [P, 512], F32)) for i in range(8)]

        raw = sb("raw", [P, RAWS, 2048])
        w_hi = [sb(f"w_hi{i}", [P, 2048], F32R) for i in range(SLOTS)]
        w_lo = [sb(f"w_lo{i}", [P, 2048], F32R) for i in range(SLOTS)]
        st_hi = sb("static_hi", [P, 2048], F32R)
        st_lo = sb("static_lo", [P, 2048], F32R)
        xs = sb("xs", [P, NT, D])
        base = sb("base", [P, NT, D])
        xn = sb("xn", [P, NT, D])
        xT_hi = sb("xT_hi", [P, 1024], F32R)
        xT_lo = sb("xT_lo", [P, 1024], F32R)
        v_hi = sb("v_hi", [P, 1024], F32R)
        v_lo = sb("v_lo", [P, 1024], F32R)
        pr_hi = sb("proj_hi", [P, 1024], F32R)
        pr_lo = sb("proj_lo", [P, 1024], F32R)
        wide_hi = sb("wide_hi", [P, 2048], F32R)
        wide_lo = sb("wide_lo", [P, 2048], F32R)
        qf_hi = sb("qf_hi", [P, 512], F32R)
        qf_lo = sb("qf_lo", [P, 512], F32R)
        kf_hi = sb("kf_hi", [P, 512], F32R)
        kf_lo = sb("kf_lo", [P, 512], F32R)
        fa = sb("fa", [P, 1024])
        fb = sb("fb", [P, 1024])
        adj_hi = sb("adj_hi", [P, 2, 512], F32R)
        adj_lo = sb("adj_lo", [P, 2, 512], F32R)
        sel = sb("sel", [P, E1 * DFF], F16)
        rows = sb("rows", [P, 5, D])
        colsb = sb("colsb", [P, COLS])
        smr = sb("small_raw", [P, SMALL])
        b2s = sb("b2s", [P, D])
        cbs = sb("cbs", [64, E1])
        bgs = sb("bgs", [P, E0])
        ident = sb("ident", [P, P])
        iota = sb("iota", [P, T])
        blockmask = sb("blockmask", [P, 256])
        edge_i = sb("edge_i", [P, 2, ET], I32)
        edge_f = sb("edge_f", [P, 2, ET])
        ewf = sb("ewf", [P, ET])
        ew_hi = sb("ew_hi", [P, ET], F32R)
        ew_lo = sb("ew_lo", [P, ET])
        ones = sb("ones", [P, 2], F32R)
        ones32 = sb("ones32", [P, 2])
        pcol = sb("pcol", [P, 4])
        mhalf = sb("mhalf", [P, 2])
        warm = sb("warm", [P, 2])
        st = sb("bnst", [P, NT, 6])
        mv = sb("mv", [P, NT, 2])
        ve = sb("ve", [P, NT])
        rstd = sb("rstd", [P, NT])
        ve2 = sb("ve2", [P, NT])
        rstd2 = sb("rstd2", [P, NT])
        ks = sb("ks", [P, 2])
        ksb = sb("ksb", [P, 2, 4])
        ks_hi = sb("ks_hi", [P, 2, 4], F32R)
        ks_lo = sb("ks_lo", [P, 2, 4], F32R)
        nrm = sb("nrm", [P, 2, 8])
        rden = sb("rden", [P, 2, 8])
        lg = sb("logits", [P, NT, E1])
        pe_ = sb("expl", [P, NT, E0])
        top = sb("top", [P, NT, 8])
        topi = sb("topi", [P, NT, 8], U32)
        topf = sb("topf", [P, NT, 8])
        wk = sb("wk", [P, NT, 8])
        comb = sb("comb", [P, NT, P])
        comb2 = xn[:, 1, 0:NT * P].rearrange("p (n e) -> p n e", n=NT)
        combT = blockmask
        combT16 = iota[:, 0:T // 2].bitcast(F16)
        rT = xn[0:64, 0, 0:T]
        iota2 = smr[:, 0:64].bitcast(F16)
        deg = sb("deg", [P, NT])
        degr = sb("degr", [P, NT])

        block = ctx.enter_context(nc.Block())

        hots = (adj_hi[:, :, :].rearrange("p a b -> p (a b)"), adj_lo[:, :, :].rearrange("p a b -> p (a b)"),
                pr_hi[:, :], pr_lo[:, :])

        def flat(t):
            return t[:, :, :].rearrange("p a b -> p (a b)")

        def f32(ap):
            return ap.bitcast(F32)

        def tile_of(t, tt):
            return t[:, :].rearrange("p (k t) -> p k t", k=KT)[:, :, tt * P:(tt + 1) * P]

        def tile_of_bank(b):
            return bank[b][:, :].rearrange("p (k t) -> p k t", k=KT)

        def folded(t, n, h):
            return t[:, :].rearrange("p (m c) -> p m c", m=KT)[:, 2 * h:2 * h + 2, n * T:(n + 1) * T]

        @block.sync
        def _(sp):
            sp.dma_start(edge_i[:, 0, :], src).then_inc(sem("src_in"), 16)
            for tt in range(NT):
                sp.dma_start(xs[:, tt, :], x[tt * P:(tt + 1) * P, :]).then_inc(sem(f"x{tt}_in"), 16)

            def load(r):
                if r >= RAWS + UNSPLIT:
                    sp.wait_ge(sem("raw_used"), r - RAWS - UNSPLIT + 1)
                elif r >= RAWS:
                    sp.wait_ge(sem("fold_done"), nth("fold_done", 2 * (r - RAWS) + 2))
                sp.dma_start(raw[:, r % RAWS, :], stream[r]).then_inc(sem(f"raw_in{r % RAWS}"), 16)

            sp.dma_start(smr[:, :], small).then_inc(sem("small_in"), 16)
            load(0)
            sp.dma_start(bgs[:, :], bg[0, :].partition_broadcast(P)).then_inc(sem("bg_in"), 16)
            load(1)
            sp.dma_start(colsb[:, :], cols).then_inc(sem("cols_in"), 16)
            sp.dma_start(rows[:, 3:5, :], rows0.partition_broadcast(P)).then_inc(sem("rows0_in"), 16)
            load(2)
            sp.dma_start(b2s[0:E0, :], b2_0).then_inc(sem("b2_0_in"), 16)
            sp.dma_start(b2s[64:P, :], wf2).then_inc(sem("wf2_in"), 16)
            sp.dma_start(cbs[:, :], codebook).then_inc(sem("codebook_in"), 16)
            sp.dma_start(rows[:, 0:3, :], rows1[0:3, :].partition_broadcast(P)).then_inc(sem("rows1_in"), 16)
            for r in range(3, N_RAW):
                load(r)
                if r == 13:
                    sp.wait_ge(sem("ffn0_out"), 2)
                    sp.dma_start(b2s[0:E1, :], b2_1).then_inc(sem("b2_1_in"), 16)
                    sp.dma_start(rows[:, 3:5, :], rows1[3:5, :].partition_broadcast(P)).then_inc(sem("rows2_in"), 16)
            for tt in range(NT):
                sp.wait_ge(sem("y_done"), nth("y_done", tt + 1))
                sp.dma_start(out[tt * P:(tt + 1) * P, :], xs[:, tt, :]).then_inc(sem("stored"), 16)
            sp.wait_ge(sem("stored"), 16 * NT)

        @block.gpsimd
        def _(pool):
            pool.memset(mhalf[:, :], -0.5).then_inc(sem("mhalf_made"), 1)
            pool.memset(ident[:, :], 0.0).then_inc(sem("zeroed"), 1)
            pool.iota(iota[:, :], [[1, T]], 0, 0, allow_small_or_imprecise_dtypes=True).then_inc(sem("iota_made"), 1)
            pool.wait_ge(sem("zeroed"), 1)
            pool.affine_select(out=ident[:, :], in_=ident[:, :], compare_op=ALU.not_equal, fill=1.0, base=0,
                               pattern=[[-1, P]], channel_multiplier=1).then_inc(sem("ident_made"), 1)

            def rsqrt(tag):
                pool.wait_ge(sem("mhalf_made"), 1)
                for tt in range(NT):
                    pool.wait_ge(sem(f"{tag}_var"), nth(f"{tag}_var", tt + 1))
                    pool.tensor_tensor(rstd[:, tt:tt + 1], ve[:, tt:tt + 1], mhalf[:, 0:1],
                                       ALU.pow).then_inc(sem(f"{tag}_rstd"), 1)

            rsqrt("ln0")
            pool.iota(pcol[:, 0:1], [[0, 1]], 0, 1, allow_small_or_imprecise_dtypes=True).then_inc(sem("pidx_made"), 1)
            pool.iota(blockmask[:, :], [[1, 4], [0, HD]], 0, 0,
                      allow_small_or_imprecise_dtypes=True).then_inc(sem("heads_made"), 1)
            pool.iota(sel[:, :], [[1, E1], [0, DFF]], 0, 0,
                      allow_small_or_imprecise_dtypes=True).then_inc(sem("experts_made"), 1)

            pool.wait_ge(sem("rows0_in"), 16)
            for tt in range(NT):
                pool.wait_ge(sem(f"x{tt}_in"), 16)
                pool.tensor_tensor(base[:, tt, :], xs[:, tt, :], rows[:, ROW_OUT0, :],
                                   ALU.add).then_inc(sem("base0"), 1)
            for tt in range(NT):
                pool.wait_ge(sem("base0"), tt + 1)
                pool.tensor_tensor(base[:, tt, :], base[:, tt, :], rows[:, ROW_GNN0, :],
                                   ALU.add).then_inc(sem("base0"), 1)

            def base1():
                pool.wait_ge(sem("rows1_in"), 16)
                for n, row in enumerate((ROW_GNN1, ROW_PROJ1)):
                    for tt in range(NT):
                        if n == 0:
                            pool.wait_ge(sem("x2"), tt + 1)
                        else:
                            pool.wait_ge(sem("base1"), tt + 1)
                        pool.tensor_tensor(base[:, tt, :], (base if n else xs)[:, tt, :], rows[:, row, :],
                                           ALU.add).then_inc(sem("base1"), 1)

            def base2():
                pool.wait_ge(sem("rows2_in"), 16)
                for tt in range(NT):
                    pool.wait_ge(sem("ln3_xn"), nth("ln3_xn", tt + 1))
                    pool.tensor_tensor(base[:, tt, :], xs[:, tt, :], fa[:, tt * D:(tt + 1) * D],
                                       ALU.add).then_inc(sem("base2"), 1)
                for tt in range(NT):
                    pool.wait_ge(sem("base2"), tt + 1)
                    pool.tensor_tensor(base[:, tt, :], base[:, tt, :], rows[:, ROW_F2, :],
                                       ALU.add).then_inc(sem("base2"), 1)

            def low(i):
                pool.wait_ge(sem("hi_cut"), i + 1)
                pool.tensor_tensor(w_lo[i % SLOTS][:, :], raw[:, raw_index(i) % RAWS, :],
                                   f32(w_hi[i % SLOTS][:, :]), ALU.subtract).then_inc(sem("raw_used"), 1)

            def low_static():
                pool.wait_ge(sem("static_hi_cut"), 1)
                pool.tensor_tensor(st_lo[:, :], raw[:, RAW_STATIC % RAWS, :], f32(st_hi[:, :]),
                                   ALU.subtract).then_inc(sem("raw_used"), 1)

            for i in range(BLOCKS):
                if i == 3:
                    pool.wait_ge(sem("fold_done"), nth("fold_done", 4))
                    pool.iota(iota2[:, :], [[0, 2], [1, E1]], 0, 0,
                              allow_small_or_imprecise_dtypes=True).then_inc(sem("iota2_made"), 1)
                if i == 6:
                    rsqrt("ln1")
                if i == STATIC_AT:
                    low_static()
                if i == 7:
                    rsqrt("ln2")
                    base1()
                if i == 13:
                    for tt in range(NT):
                        pool.wait_ge(sem("normed_var"), tt + 1)
                        pool.tensor_tensor(rstd2[:, tt:tt + 1], ve2[:, tt:tt + 1], mhalf[:, 0:1],
                                           ALU.pow).then_inc(sem("normed_rstd"), 1)
                    rsqrt("ln3")
                    base2()
                low(i)
            rsqrt("ln5")
            for tt in range(NT):
                pool.wait_ge(sem("hmoe"), tt + 1)
                pool.wait_ge(sem("base2"), 4)
                pool.tensor_tensor(base[:, tt, :], base[:, tt, :], fa[:, tt * D:(tt + 1) * D],
                                   ALU.add).then_inc(sem("base3"), 1)

        def weights_ready(eng, i):
            eng.wait_ge(sem("raw_used"), raw_index(i) - UNSPLIT + 1)

        @block.tensor
        def _(pe):
            def mm3(o, a_hi, a_lo, b_hi, b_lo, first, last):
                pe.matmul(o, a_hi, b_hi, start=first, stop=False)
                pe.matmul(o, a_hi, b_lo, start=False, stop=False)
                return pe.matmul(o, a_lo, b_hi, start=False, stop=last)

            def grouped(o, parts, late, event, n, last=True):
                for k, (a_hi, a_lo, b_hi, b_lo) in enumerate(parts):
                    pe.matmul(o, a_hi, b_hi, start=(k == 0), stop=False)
                    if late == "a":
                        pe.matmul(o, a_hi, b_lo, start=False, stop=False)
                    else:
                        pe.matmul(o, a_lo, b_hi, start=False, stop=False)
                pe.wait_ge(sem(event), nth(event, n))
                for k, (a_hi, a_lo, b_hi, b_lo) in enumerate(parts):
                    x, y = (a_lo, b_hi) if late == "a" else (a_hi, b_lo)
                    ins = pe.matmul(o, x, y, start=False, stop=(last and k == len(parts) - 1))
                return ins

            def keep_clock(n, b, operand):
                for _ in range(n):
                    pe.matmul(bank[b][:, :], operand[:, 0:P], operand[:, 0:512], start=True, stop=True)

            def turn(tag, tt, halved=False):
                pe.wait_ge(sem(f"{tag}_xn"), nth(f"{tag}_xn", tt + 1))
                for kt in range(KT):
                    b = bank[(4 if halved and kt >= KT // 2 else 6) + tt]
                    ins = pe.transpose(b[:, kt * P:(kt + 1) * P], xn[:, tt, kt * P:(kt + 1) * P], ident[:, :])
                ins.then_inc(sem(f"{tag}_turned"), 1)

            def tokens_out(tag, banks, i, tt, kts=range(KT)):
                weights_ready(pe, i)
                for kt in kts:
                    a = slice(kt * T + tt * P, kt * T + (tt + 1) * P)
                    b = slice(kt * D, (kt + 1) * D)
                    ins = mm3(bank[banks[tt]][:, :], xT_hi[:, a], xT_lo[:, a], w_hi[i % SLOTS][:, b],
                              w_lo[i % SLOTS][:, b], kt == 0, kt == KT - 1)
                    if kt == KT - 1:
                        ins.then_inc(sem(tag), 1)

            pe.wait_ge(sem("ident_made"), 1)

            def edges(j):
                pe.wait_ge(sem("hot"), j + 1)
                pe.wait_ge(sem("hot_w"), j + 1)
                hot = hots[j % HOTS]
                for h in range(2):
                    lhs = hot[:, h * P:(h + 1) * P]
                    if j:
                        pe.matmul(bank[h][:, T:2 * T], lhs, hot[:, 3 * T:4 * T], start=False, stop=False)
                    ins = pe.matmul(bank[h][:, :], lhs, hot[:, T:3 * T], start=(j == 0), stop=(j == ET - 1))
                    if j == 0:
                        ins = pe.matmul(bank[h][:, T:2 * T], lhs, hot[:, 3 * T:4 * T], start=False, stop=False)
                ins.then_inc(sem("hot_used"), 1)

            def fold(n, m):
                pe.wait_ge(sem("small_in"), 16)
                pe.wait_ge(sem(f"raw_in{n}"), 16)
                for kt in range(KT):
                    a = slice(kt * D + m * P, kt * D + (m + 1) * P)
                    o = bank[2 + 2 * n + m // 2][:, (m % 2) * T + kt * HD:(m % 2) * T + (kt + 1) * HD]
                    ins = pe.matmul(o, raw[:, n, a], smr[:, SM_R:SM_R + HD], start=True, stop=True)
                if m % 2 == 1:
                    ins.then_inc(sem("fold_done"), 1)

            def query(m):
                pe.wait_ge(sem("ln0_lo"), nth("ln0_lo", 2))
                pe.wait_ge(sem("fold_lo"), nth("fold_lo", 2))
                for kt in range(KT):
                    a = slice(kt * 512 + m * P, kt * 512 + (m + 1) * P)
                    b = slice(kt * T, (kt + 1) * T)
                    ins = mm3(bank[2][:, m * T:(m + 1) * T], wide_hi[:, a], wide_lo[:, a], xT_hi[:, b], xT_lo[:, b],
                              kt == 0, kt == KT - 1)
                if m == 1:
                    ins.then_inc(sem("q_done"), 1)

            def key(tt):
                pe.wait_ge(sem("fold_lo"), nth("fold_lo", 4))
                for kt in range(KT):
                    a = slice(kt * T + tt * P, kt * T + (tt + 1) * P)
                    b = slice(kt * 512 + T, kt * 512 + 2 * T)
                    ins = mm3(bank[3][:, tt * T:(tt + 1) * T], xT_hi[:, a], xT_lo[:, a], wide_hi[:, b],
                              wide_lo[:, b], kt == 0, kt == KT - 1)
                if tt == 1:
                    ins.then_inc(sem("k_done"), 1)

            def tokens_after(tag, o, i, tt, t_hi, t_lo, split):
                weights_ready(pe, i)
                pe.wait_ge(sem(f"{split}_hi"), nth(f"{split}_hi", tt + 1))
                parts = [(t_hi[:, kt * T + tt * P:kt * T + (tt + 1) * P], t_lo[:, kt * T + tt * P:kt * T + (tt + 1) * P],
                          w_hi[i % SLOTS][:, kt * D:(kt + 1) * D], w_lo[i % SLOTS][:, kt * D:(kt + 1) * D])
                         for kt in range(KT)]
                grouped(o, parts, "a", f"{split}_lo", tt + 1).then_inc(sem(tag), 1)

            for j in range(ET):
                edges(j)
                if j in (TURN_AT, TURN_AT + 1):
                    turn("ln0", j - TURN_AT)
                if FOLD_AT <= j < FOLD_AT + 2 * KT:
                    fold((j - FOLD_AT) // KT, (j - FOLD_AT) % KT)
                if j in (QUERY_AT, QUERY_AT + 1):
                    query(j - QUERY_AT)
                if j in (KEY_AT, KEY_AT + 1):
                    key(j - KEY_AT)
                if VALUE_AT <= j < VALUE_AT + NT * KT:
                    tokens_out("v_done", (4, 5), V0, (j - VALUE_AT) // KT, ((j - VALUE_AT) % KT,))
                if GNN_AT <= j < GNN_AT + NT * KT:
                    tokens_out("g_done", (6, 7), GNN0, (j - GNN_AT) // KT, ((j - GNN_AT) % KT,))

            pe.wait_ge(sem("k_lo"), nth("k_lo", 1))
            pe.wait_ge(sem("q_lo"), nth("q_lo", 1))
            pe.wait_ge(sem("v_lo"), nth("v_lo", 2))
            pe.wait_ge(sem("ones_made"), 1)
            for m in range(2):
                for tt in range(NT):
                    a = slice(tt * T + m * P, tt * T + (m + 1) * P)
                    b = slice(tt * D + m * 256, tt * D + (m + 1) * 256)
                    mm3(bank[2][:, m * 256:(m + 1) * 256], kf_hi[:, a], kf_lo[:, a], v_hi[:, b], v_lo[:, b],
                        tt == 0, tt == NT - 1)
                for tt in range(NT):
                    a = slice(tt * T + m * P, tt * T + (m + 1) * P)
                    pe.matmul(bank[3][:, 2 * m:2 * m + 2], kf_hi[:, a], ones[:, :], start=(tt == 0), stop=False)
                    pe.matmul(bank[3][:, 2 * m:2 * m + 2], kf_lo[:, a], ones[:, :], start=False,
                              stop=(tt == NT - 1))
            pe.wait_ge(sem("adj_lo"), nth("adj_lo", 2))
            for tt in range(NT):
                for h in range(2):
                    a = slice(tt * P, (tt + 1) * P)
                    pe.matmul(bank[3][:, 8 + 2 * tt:10 + 2 * tt], adj_hi[:, h, a], ones[:, :], start=(h == 0),
                              stop=False)
                    ins = pe.matmul(bank[3][:, 8 + 2 * tt:10 + 2 * tt], adj_lo[:, h, a], ones[:, :], start=False,
                                    stop=(h == 1))
            ins.then_inc(sem("kv_done"), 1)

            def aggregate(tag, part, tt):
                for h in range(2):
                    a = slice(part * T + tt * P, part * T + (tt + 1) * P)
                    b = slice(h * D, (h + 1) * D)
                    ins = mm3(bank[tt][:, :], adj_hi[:, h, a], adj_lo[:, h, a], pr_hi[:, b], pr_lo[:, b],
                              h == 0, h == 1)
                ins.then_inc(sem(tag), 1)

            pe.wait_ge(sem("pr_lo"), nth("pr_lo", 2))
            for tt in range(NT):
                aggregate("agg0_done", 0, tt)

            pe.wait_ge(sem("kv_lo"), nth("kv_lo", 1))
            for tt in range(NT):
                for m in range(2):
                    a = slice(m * T + tt * P, m * T + (tt + 1) * P)
                    ins = mm3(bank[3][:, 64 + 8 * tt + 4 * m:68 + 8 * tt + 4 * m], qf_hi[:, a], qf_lo[:, a],
                              ks_hi[:, m, :], ks_lo[:, m, :], True, True)
            ins.then_inc(sem("norms_done"), 1)
            for tt in range(NT):
                for m in range(2):
                    a = slice(m * T + tt * P, m * T + (tt + 1) * P)
                    b = slice(m * 256, (m + 1) * 256)
                    ins = mm3(bank[4 + tt][:, b], qf_hi[:, a], qf_lo[:, a], xT_hi[:, b], xT_lo[:, b], True, True)
                ins.then_inc(sem("z_done"), 1)
            weights_ready(pe, OUT0)
            for tt in range(NT):
                turn("z", tt)
            for tt in range(NT):
                tokens_after("o_done", bank[2 + tt][:, :], OUT0, tt, v_hi, v_lo, "z")

            def spread(tag, g, j, m0):
                if g > SHARED_GROUPS:
                    pe.wait_ge(sem(f"{tag}_scaled"), nth(f"{tag}_scaled", 2 * g - 1 + j))
                for mm in range(2):
                    m = m0 + 2 * j + mm
                    ins = pe.matmul(bank[6 + j][:, mm * T:(mm + 1) * T], sel[:, m * P:(m + 1) * P],
                                    combT16[:, :], start=True, stop=True)
                ins.then_inc(sem(f"{tag}_spread"), 1)

            def up_part(tag, i, g, j, mm):
                for kt in range(KT):
                    a = slice(kt * D + (2 * j + mm) * P, kt * D + (2 * j + mm + 1) * P)
                    b = slice(kt * T, (kt + 1) * T)
                    ins = mm3(bank[2 + j][:, mm * T:(mm + 1) * T], w_hi[i % SLOTS][:, a],
                              w_lo[i % SLOTS][:, a], xT_hi[:, b], xT_lo[:, b], kt == 0, kt == KT - 1)
                if mm == 1:
                    ins.then_inc(sem(f"{tag}_up"), 1)

            def up_half(tag, i, g, j):
                weights_ready(pe, i)
                if g:
                    pe.wait_ge(sem(f"{tag}_act"), nth(f"{tag}_act", 4 * g - 2 + 2 * j))
                for mm in range(2):
                    up_part(tag, i, g, j, mm)

            def up(tag, i, routed, g, m0):
                for j in range(2):
                    up_half(tag, i, g, j)
                    if routed:
                        spread(tag, g, j, m0)

            def down_part(i, g, tt, m, first):
                a = slice((g % 2) * 1024 + m * T + tt * P, (g % 2) * 1024 + m * T + (tt + 1) * P)
                b = slice(m * D, (m + 1) * D)
                return mm3(bank[tt][:, :], wide_hi[:, a], wide_lo[:, a], w_hi[i % SLOTS][:, b],
                           w_lo[i % SLOTS][:, b], first and m == 0, False)

            def down(tag, i, g):
                weights_ready(pe, i)
                for j in range(2):
                    pe.wait_ge(sem(f"{tag}_act_lo"), nth(f"{tag}_act_lo", 2 * g + j + 1))
                    for m in (2 * j, 2 * j + 1):
                        for tt in range(NT):
                            ins = down_part(i, g, tt, m, g == 0)
                    ins.then_inc(sem(f"{tag}_down"), 1)

            def last_down(tag, i, g, b2_in, experts):
                weights_ready(pe, i)
                pe.wait_ge(sem(b2_in), 16)
                for tt in range(NT):
                    for m in range(KT):
                        if tt == 0 and m % 2 == 0:
                            pe.wait_ge(sem(f"{tag}_act_lo"), nth(f"{tag}_act_lo", 2 * g + m // 2 + 1))
                        down_part(i, g, tt, m, g == 0)
                    if tt == 0:
                        pe.wait_ge(sem(f"comb{tag[-1]}_T"), 1)
                    pe.matmul(bank[tt][:, :], combT[0:experts, tt * P:(tt + 1) * P], b2s[0:experts, :], start=False,
                              stop=True).then_inc(sem(f"{tag}_out"), 1)

            pe.wait_ge(sem("mixed0"), 1)
            for tt in range(NT):
                turn("ln1", tt)
                keep_clock(4, 0, adj_hi[:, 0, :])
                pe.wait_ge(sem("ln1_full"), tt + 1)
                for kt in range(KT):
                    a = slice(kt * T + tt * P, kt * T + (tt + 1) * P)
                    b = slice(SM_WG + kt * E0, SM_WG + (kt + 1) * E0)
                    ins = pe.matmul(bank[4][:, 8 + tt * 8:16 + tt * 8], fb[:, a], smr[:, b], start=(kt == 0),
                                    stop=(kt == KT - 1))
            ins.then_inc(sem("lg0_done"), 1)
            pe.wait_ge(sem("ln1_lo"), nth("ln1_lo", 2))
            pe.wait_ge(sem("x1"), 2)
            up_half("ffn0", UP0, 0, 0)
            for tt in range(NT):
                pe.wait_ge(sem("comb0"), tt + 1)
                ins = pe.transpose(bank[5][:, tt * P:(tt + 1) * P], comb[:, tt, :], ident[:, :])
            ins.then_inc(sem("comb0_turned"), 1)
            up_part("ffn0", UP0, 0, 1, 0)
            pe.wait_ge(sem("comb0_16"), 1)
            pe.wait_ge(sem("sel_made"), 1)
            spread("ffn0", 0, 0, 0)
            up_part("ffn0", UP0, 0, 1, 1)
            spread("ffn0", 0, 1, 0)
            last_down("ffn0", DOWN0, 0, "b2_0_in", E0)

            pe.wait_ge(sem("x2"), 1)
            for tt in range(NT):
                turn("ln2", tt)
                tokens_after("s_done", bank[tt][:, :], GNN1, tt, xT_hi, xT_lo, "ln2")

            def turned_out(tag, banks, i):
                weights_ready(pe, i)
                for m in range(KT):
                    for kt in range(KT):
                        a = slice(kt * D + m * P, kt * D + (m + 1) * P)
                        b = slice(kt * T, (kt + 1) * T)
                        ins = mm3(bank[banks[m // 2]][:, (m % 2) * T:(m % 2 + 1) * T], w_hi[i % SLOTS][:, a],
                                  w_lo[i % SLOTS][:, a], xT_hi[:, b], xT_lo[:, b], kt == 0, kt == KT - 1)
                    if m % 2 == 1:
                        ins.then_inc(sem(tag), 1)

            turned_out("k1_done", (2, 3), K1)
            turned_out("q1_done", (4, 5), Q1)

            def features(n, name, b):
                pe.wait_ge(sem(f"{name}_lo"), nth(f"{name}_lo", 2))
                for tt in range(NT):
                    for kt in range(KT):
                        a = slice(n * 1024 + kt * T + tt * P, n * 1024 + kt * T + (tt + 1) * P)
                        f = slice(ST_FEAT + kt * M1, ST_FEAT + (kt + 1) * M1)
                        ins = mm3(bank[b][:, tt * M1:(tt + 1) * M1], wide_hi[:, a], wide_lo[:, a], st_hi[:, f],
                                  st_lo[:, f], kt == 0, kt == KT - 1)
                ins.then_inc(sem(f"{name}_feat"), 1)

            def norms(name, sq, c):
                pe.wait_ge(sem(f"{name}_sum"), 2)
                for tt in range(NT):
                    ins = pe.matmul(bank[7][:, c + tt:c + tt + 1], sq[:, tt * P:(tt + 1) * P], ones32[:, 0:1],
                                    start=True, stop=True)
                ins.then_inc(sem(f"{name}_norm"), 1)

            pe.wait_ge(sem("raw_used"), RAW_STATIC - UNSPLIT + 1)
            features(0, "k1", 6)
            norms("k1", flat(xn), 0)
            features(1, "q1", 2)
            pe.wait_ge(sem("k1_nb"), 1)
            norms("q1", fa, 8)
            for tt in range(NT):
                tokens_out("v1_done", (4, 5), V1, tt)
            pe.wait_ge(sem("sup_lo"), nth("sup_lo", 2))
            aggregate("agg1_done", 1, 0)
            for tt in range(NT):
                pe.wait_ge(sem("qp"), tt + 1)
                for m in range(2):
                    ins = pe.transpose(bank[3][:, m * T + tt * P:m * T + (tt + 1) * P],
                                       fb[:, tt * M1 + m * P:tt * M1 + (m + 1) * P], ident[:, :])
            ins.then_inc(sem("qp_turned"), 1)
            pe.wait_ge(sem("q1_nb"), 1)
            pe.wait_ge(sem("kp_lo"), nth("kp_lo", 1))
            pe.wait_ge(sem("v1_lo"), nth("v1_lo", 2))
            for m in range(2):
                for tt in range(NT):
                    a = slice(tt * M1 + m * P, tt * M1 + (m + 1) * P)
                    b = slice(tt * D, (tt + 1) * D)
                    ins = mm3(bank[(6, 2)[m]][:, :], kf_hi[:, a], kf_lo[:, a], v_hi[:, b], v_lo[:, b], tt == 0,
                              tt == NT - 1)
                ins.then_inc(sem("kv1_done"), 1)
                for tt in range(NT):
                    a = slice(tt * M1 + m * P, tt * M1 + (m + 1) * P)
                    pe.matmul(bank[7][:, 16 + 2 * m:18 + 2 * m], kf_hi[:, a], ones[:, :], start=(tt == 0), stop=False)
                    ins = pe.matmul(bank[7][:, 16 + 2 * m:18 + 2 * m], kf_lo[:, a], ones[:, :], start=False,
                                    stop=(tt == NT - 1))
            ins.then_inc(sem("ksum1_done"), 1)
            aggregate("agg1_done", 1, 1)
            pe.wait_ge(sem("qp_lo"), nth("qp_lo", 1))
            pe.wait_ge(sem("kv1_lo"), nth("kv1_lo", 2))
            for kt in range(KT):
                for m in range(2):
                    a = slice(m * D + kt * P, m * D + (kt + 1) * P)
                    b = slice(m * T, (m + 1) * T)
                    ins = mm3(bank[4 + kt // 2][:, (kt % 2) * T:(kt % 2 + 1) * T], xT_hi[:, a], xT_lo[:, a],
                              qf_hi[:, b], qf_lo[:, b], m == 0, m == 1)
                if kt % 2 == 1:
                    ins.then_inc(sem("y1_turned"), 1)
            pe.wait_ge(sem("ks1_lo"), nth("ks1_lo", 1))
            for tt in range(NT):
                for m in range(2):
                    a = slice(m * T + tt * P, m * T + (tt + 1) * P)
                    ins = mm3(bank[7][:, 24 + 2 * tt:26 + 2 * tt], qf_hi[:, a], qf_lo[:, a], ks_hi[:, m, 0:2],
                              ks_lo[:, m, 0:2], m == 0, m == 1)
            ins.then_inc(sem("den1_done"), 1)
            weights_ready(pe, PROJ1)
            pe.wait_ge(sem("y1_hi"), nth("y1_hi", 2))
            for tt in range(NT):
                parts = [(v_hi[:, kt * T + tt * P:kt * T + (tt + 1) * P], v_lo[:, kt * T + tt * P:kt * T + (tt + 1) * P],
                          w_hi[PROJ1 % SLOTS][:, kt * D:(kt + 1) * D], w_lo[PROJ1 % SLOTS][:, kt * D:(kt + 1) * D])
                         for kt in range(KT)]
                grouped(bank[2 + tt][:, :], parts, "a", "y1_lo", 2).then_inc(sem("p1_done"), 1)

            def router_and_f(tag, b, t0, t1, split, n):
                pe.wait_ge(sem(f"{split}_hi"), nth(f"{split}_hi", n))
                parts = [(st_hi[:, ST_RF + kt * P:ST_RF + (kt + 1) * P], st_lo[:, ST_RF + kt * P:ST_RF + (kt + 1) * P],
                          xT_hi[:, kt * T + t0:kt * T + t1], xT_lo[:, kt * T + t0:kt * T + t1]) for kt in range(KT)]
                grouped(bank[b][:, t0:t1], parts, "b", f"{split}_lo", n).then_inc(sem(tag), 1)

            for tt in range(NT):
                turn("ln4", tt, True)
                keep_clock((10, 8)[tt], 0, st_hi[:, :])
            router_and_f("r_done", 4, 0, T, "ln4", 2)
            for n, (kind, g) in enumerate(FFN1_ORDER):
                routed = g >= SHARED_GROUPS
                if kind == "up":
                    if g == 0:
                        weights_ready(pe, FFN1 + n)
                        up_part("ffn1", FFN1 + n, g, 0, 0)
                        pe.wait_ge(sem("codebook_in"), 16)
                        pe.wait_ge(sem("rT"), 1)
                        for tt in range(NT):
                            ins = pe.matmul(bank[5][:, tt * E1:(tt + 1) * E1], rT[:, tt * P:(tt + 1) * P], cbs[:, :],
                                            start=True, stop=True)
                        ins.then_inc(sem("lg1_done"), 1)
                        up_part("ffn1", FFN1 + n, g, 0, 1)
                        up_half("ffn1", FFN1 + n, g, 1)
                        continue
                    if g == SHARED_GROUPS:
                        pe.wait_ge(sem("comb1_16"), 1)
                    up("ffn1", FFN1 + n, routed, g, 4 * (g - SHARED_GROUPS))
                    if g == SHARED_GROUPS - 1:
                        for tt in range(NT):
                            pe.wait_ge(sem("comb1"), tt + 1)
                            ins = pe.transpose(bank[4][:, tt * P:(tt + 1) * P], comb[:, tt, :], ident[:, :])
                        ins.then_inc(sem("comb1_turned"), 1)
                elif g < GROUPS - 1:
                    down("ffn1", FFN1 + n, g)
                else:
                    last_down("ffn1", FFN1 + n, g, "b2_1_in", E1)
            turn("ln5", 0, True)
            keep_clock(10, 0, st_hi[:, :])
            turn("ln5", 1, True)
            for tt in range(NT):
                router_and_f("f1_done", 2 + tt, tt * P, (tt + 1) * P, "ln5", tt + 1)
            pe.wait_ge(sem("wf2_in"), 16)
            for tt in range(NT):
                pe.wait_ge(sem("f1_silu"), tt + 1)
                pe.matmul(bank[6 + tt][:, :], fb[64:P, tt * P:(tt + 1) * P], b2s[64:P, :], start=True,
                          stop=True).then_inc(sem("f2_done"), 1)

        @block.scalar
        def _(act):
            act.dma_start(edge_i[:, 1, :], dst).then_inc(sem("dst_in"), 16)
            act.dma_start(ewf[:, :], ew).then_inc(sem("ew_in"), 16)
            act.wait_ge(sem("mhalf_made"), 1)
            act.activation(warm[:, :], mhalf[:, :], ACT.Exp)

            def high_block(i):
                r = raw_index(i)
                act.wait_ge(sem(f"raw_in{r % RAWS}"), nth(f"raw_in{r % RAWS}", 16 * (r // RAWS + 1)))
                if i >= SLOTS:
                    event, n = last_use(i - SLOTS)
                    act.wait_ge(sem(event), nth(event, n))
                act.activation(w_hi[i % SLOTS][:, :], raw[:, r % RAWS, :], ACT.Copy).then_inc(sem("hi_cut"), 1)

            def high_static():
                r = RAW_STATIC
                act.wait_ge(sem(f"raw_in{r % RAWS}"), nth(f"raw_in{r % RAWS}", 16 * (r // RAWS + 1)))
                act.activation(st_hi[:, :], raw[:, r % RAWS, :], ACT.Copy).then_inc(sem("static_hi_cut"), 1)

            def high(tag, o, i, wait, n, scale=1.0):
                act.wait_ge(sem(wait), nth(wait, n))
                act.activation(o, i, ACT.Copy, scale=scale).then_inc(sem(f"{tag}_hi"), 1)

            def high_turned(tag, o, tt):
                high(tag, tile_of(o, tt), tile_of_bank(6 + tt), f"{tag}_turned", tt + 1)

            def affine_high(tag, g, b, tt):
                act.wait_ge(sem(f"{tag}_turned"), nth(f"{tag}_turned", tt + 1))
                for kt in range(KT // 2, KT):
                    act.activation(fb[:, kt * T + tt * P:kt * T + (tt + 1) * P],
                                   bank[4 + tt][:, kt * P:(kt + 1) * P], ACT.Identity, scale=colsb[:, g + kt:g + kt + 1],
                                   bias=colsb[:, b + kt:b + kt + 1]).then_inc(sem(f"{tag}_affine2"), 1)
                act.wait_ge(sem(f"{tag}_affine2"), nth(f"{tag}_affine2", 2 * tt + 2))
                high(tag, tile_of(xT_hi, tt), tile_of(fb, tt), f"{tag}_affine", 2 * tt + 2)

            def high_fold(n, h):
                high("fold", folded(wide_hi, n, h), bank[2 + 2 * n + h][:, :].rearrange("p (m c) -> p m c", m=2),
                     "fold_done", 2 * n + h + 1)

            def elu_exp(name, i, o):
                act.wait_ge(sem(f"{name}_min"), nth(f"{name}_min", 1))
                act.activation(o, i, ACT.Exp).then_inc(sem(f"{name}_exp"), 1)

            act.wait_ge(sem("ew_cut"), 1)
            for j in range(ET):
                act.wait_ge(sem("hot_src"), j + 1)
                hot = hots[j % HOTS]
                act.activation(hot[:, 2 * T:3 * T], f32(hot[:, T:2 * T]), ACT.Copy,
                               scale=f32(ew_hi[:, j:j + 1])).then_inc(sem("hot_w"), 1)
                if j in (4, 5):
                    high_turned("ln0", xT_hi, j - 4)
                if j in (7, 9, 11, 13):
                    high_fold((j - 7) // 4, (j - 7) // 2 % 2)
                if j in (8, 15, 21, 26):
                    high_block((8, 15, 21, 26).index(j))
                if j == 17:
                    elu_exp("q", fa[:, 0:512], fa[:, 512:1024])
                if j == 19:
                    high("q", qf_hi[:, :], fb[:, 0:512], "q_f", 1)
                if j == 20:
                    elu_exp("k", fb[:, 512:1024], xn[:, 0, :])
                if j == 22:
                    high("k", kf_hi[:, :], xn[:, 1, :], "k_f", 1)
                if j in (24, 28):
                    tt = (j - 24) // 4
                    high("v", v_hi[:, tt * D:(tt + 1) * D], bank[4 + tt][:, :], "v_done", tt + 1)
                if j == 30:
                    high_block(4)
            for h in range(2):
                high("adj", adj_hi[:, h, :], bank[h][:, :], "hot_used", ET)
            for tt in range(NT):
                high("pr", pr_hi[:, tt * D:(tt + 1) * D], bank[6 + tt][:, :], "g_done", tt + 1)
            high("kv", xT_hi[:, 0:512], fb[:, 0:512], "kv_f", 2)
            high_block(5)
            high_static()
            for tt in range(NT):
                high_turned("z", v_hi, tt)
            for tt in range(NT):
                act.wait_ge(sem("ln1_turned"), nth("ln1_turned", tt + 1))
                act.activation(tile_of(fb, tt), tile_of_bank(6 + tt), ACT.Copy).then_inc(sem("ln1_full"), 1)
                high_turned("ln1", xT_hi, tt)

            for tt in range(NT):
                act.wait_ge(sem("negmax0"), tt + 1)
                act.activation(pe_[:, tt, 0:E0], lg[:, tt, 0:E0], ACT.Exp, bias=wk[:, tt, 0:1],
                               accum_out=wk[:, tt, 1:2]).then_inc(sem("sum0"), 1)

            def hidden(tag, func, g, col):
                for j in range(2):
                    act.wait_ge(sem(f"{tag}_up"), nth(f"{tag}_up", 2 * g + j + 1))
                    if g:
                        act.wait_ge(sem(f"{tag}_scaled"), nth(f"{tag}_scaled", 2 * g - 1 + j))
                    for mm in range(2):
                        c = col + 4 * g + 2 * j + mm
                        act.activation(fa[:, j * 512 + mm * T:j * 512 + (mm + 1) * T],
                                       bank[2 + j][:, mm * T:(mm + 1) * T], func,
                                       bias=colsb[:, c:c + 1]).then_inc(sem(f"{tag}_act"), 1)

            act.wait_ge(sem("cols_in"), 16)
            hidden("ffn0", ACT.Relu, 0, COL_B1_0)
            high_block(6)
            for tt in range(NT):
                high_turned("ln2", xT_hi, tt)
            high_block(7)
            high_block(8)
            for tt in range(NT):
                high("sup", pr_hi[:, tt * D:(tt + 1) * D], bank[tt][:, :], "s_done", tt + 1)
            for name, n, f, sq in (("k1", 0, fa, flat(xn)), ("q1", 1, fb, fa)):
                for h in range(2):
                    a = slice(h * 512, (h + 1) * 512)
                    high(name, wide_hi[:, n * 1024 + h * 512:n * 1024 + (h + 1) * 512], f[:, a], f"{name}_f",
                         2 * h + 2)
                    if n:
                        act.wait_ge(sem("k1_sq"), 2)
                        act.wait_ge(sem("k1_lo"), nth("k1_lo", 2))
                    act.activation(sq[:, a], f[:, a], ACT.Square).then_inc(sem(f"{name}_sq"), 1)
                high_block(9 + n)
            act.wait_ge(sem("k1_nb"), 1)
            act.wait_ge(sem("q1_lo"), nth("q1_lo", 2))
            act.wait_ge(sem("q1_sq"), 2)
            for tt in range(NT):
                act.wait_ge(sem("k1_feat"), 1)
                act.activation(fb[:, 512 + tt * M1:512 + (tt + 1) * M1], bank[6][:, tt * M1:(tt + 1) * M1], ACT.Exp,
                               bias=nrm[:, 0, tt:tt + 1]).then_inc(sem("kp"), 1)
            high("kp", kf_hi[:, :], fb[:, 512:1024], "kp", 2, M1 ** -0.5)
            high_block(11)
            act.wait_ge(sem("q1_nb"), 1)
            act.wait_ge(sem("q1_feat"), 1)
            for tt in range(NT):
                act.activation(fb[:, tt * M1:(tt + 1) * M1], bank[2][:, tt * M1:(tt + 1) * M1], ACT.Exp,
                               bias=nrm[:, 1, tt:tt + 1]).then_inc(sem("qp"), 1)
            for tt in range(NT):
                high("v1", v_hi[:, tt * D:(tt + 1) * D], xn[:, tt, :], "v1_f", tt + 1)
            high_block(12)
            high("qp", qf_hi[:, :], bank[3][:, :], "qp_turned", 1, M1 ** -0.5)
            for m in range(2):
                high("kv1", xT_hi[:, m * D:(m + 1) * D], bank[(6, 2)[m]][:, :], "kv1_done", m + 1)
            for h in range(2):
                high("y1", v_hi[:, h * 512:(h + 1) * 512], bank[4 + h][:, :], "y1_turned", h + 1)
            high_block(13)
            for tt in range(NT):
                affine_high("ln4", COL_LN_G, COL_LN_B, tt)
            act.wait_ge(sem("r_done"), nth("r_done", 1))
            act.activation(rT[:, :], bank[4][0:64, 0:T], ACT.Copy).then_inc(sem("rT"), 1)
            for tt in range(NT):
                act.wait_ge(sem("negmax1"), tt + 1)
                act.activation(wk[:, tt, 2:4], top[:, tt, 0:2], ACT.Exp, bias=wk[:, tt, 0:1],
                               accum_out=wk[:, tt, 1:2]).then_inc(sem("sum1"), 1)
            act.wait_ge(sem("base2"), 2)
            ups = 0
            for n, (kind, g) in enumerate(FFN1_ORDER):
                if kind == "up":
                    hidden("ffn1", ACT.Silu, g, COL_B1)
                if FFN1 + n + SLOTS < BLOCKS:
                    high_block(FFN1 + n + SLOTS)
            for tt in range(NT):
                affine_high("ln5", COL_FF_G, COL_FF_B, tt)
            for tt in range(NT):
                a = slice(tt * P, (tt + 1) * P)
                act.wait_ge(sem("f1_done"), tt + 1)
                act.activation(fb[64:P, a], bank[2 + tt][64:P, a], ACT.Silu,
                               bias=colsb[64:P, COL_BF1:COL_BF1 + 1]).then_inc(sem("f1_silu"), 1)

        @block.vector
        def _(dve):
            def stats(tag, tile, tt, event, n):
                dve.wait_ge(sem(event), nth(event, n))
                dve.bn_stats(st[:, tt, :], tile).then_inc(sem(f"{tag}_bn"), 1)
                dve.wait_ge(sem(f"{tag}_bn"), nth(f"{tag}_bn", tt + 1))
                dve.bn_aggr(mv[:, tt, :], st[:, tt, :]).then_inc(sem(f"{tag}_mv"), 1)
                dve.wait_ge(sem(f"{tag}_mv"), nth(f"{tag}_mv", tt + 1))
                if tag == "ln3":
                    dve.tensor_scalar(ve2[:, tt:tt + 1], mv[:, tt, 1:2], 1.0 + LN_EPS, LN_EPS * LN_EPS, ALU.mult,
                                      ALU.add).then_inc(sem("normed_var"), 1)
                dve.tensor_scalar(ve[:, tt:tt + 1], mv[:, tt, 1:2], LN_EPS, None, ALU.add)\
                   .then_inc(sem(f"{tag}_var"), 1)

            def normalize(tag, tile, tt, out):
                dve.wait_ge(sem(f"{tag}_rstd"), nth(f"{tag}_rstd", tt + 1))
                dve.tensor_scalar(out, tile, mv[:, tt, 0:1], rstd[:, tt:tt + 1], ALU.subtract,
                                  ALU.mult).then_inc(sem(f"{tag}_xn"), 1)

            def low(tag, o, i, hi, n=1):
                dve.wait_ge(sem(f"{tag}_hi"), nth(f"{tag}_hi", n))
                dve.tensor_tensor(o, i, f32(hi), ALU.subtract).then_inc(sem(f"{tag}_lo"), 1)

            def low_turned(tag, lo, hi, tt):
                low(tag, tile_of(lo, tt), tile_of_bank(6 + tt), tile_of(hi, tt), tt + 1)

            x_tiles = [xs[:, tt, :] for tt in range(NT)]
            xn_tiles = [xn[:, tt, :] for tt in range(NT)]
            fa_tiles = [fa[:, tt * D:(tt + 1) * D] for tt in range(NT)]

            dve.memset(ones32[:, :], 1.0).then_inc(sem("ones32_made"), 1)
            dve.wait_ge(sem("ones32_made"), 1)
            dve.tensor_copy(ones[:, :], ones32[:, :]).then_inc(sem("ones_made"), 1)
            for q in range(4):
                dve.memset(pcol[32 * q:32 * q + 32, 1:2], float(q))
            dve.memset(pcol[0:64, 3:4], 1.0)
            dve.memset(pcol[64:P, 3:4], 1.0 / LO_SCALE).then_inc(sem("pcol_made"), 1)
            dve.wait_ge(sem("src_in"), 16)
            dve.wait_ge(sem("dst_in"), 16)
            dve.tensor_copy(edge_f[:, :, :], edge_i[:, :, :]).then_inc(sem("edges"), 1)
            dve.wait_ge(sem("ew_in"), 16)
            dve.tensor_copy(ew_hi[:, :], ewf[:, :]).then_inc(sem("ew_cut"), 1)
            dve.wait_ge(sem("ew_cut"), 1)
            dve.tensor_tensor(ew_lo[:, :], ewf[:, :], f32(ew_hi[:, :]), ALU.subtract).then_inc(sem("ew_cut"), 1)
            dve.wait_ge(sem("edges"), 1)
            dve.wait_ge(sem("ew_cut"), 2)
            dve.wait_ge(sem("iota_made"), 1)

            def low_fold(n, h):
                low("fold", folded(wide_lo, n, h), bank[2 + 2 * n + h][:, :].rearrange("p (m c) -> p m c", m=2),
                    folded(wide_hi, n, h), 2 * n + h + 1)

            for j in range(ET):
                if j >= HOTS:
                    dve.wait_ge(sem("hot_used"), j - HOTS + 1)
                hot = hots[j % HOTS]
                s, d = edge_f[:, 0, j:j + 1], edge_f[:, 1, j:j + 1]
                dve.tensor_scalar(hot[:, T:2 * T], iota[:, :], s, None, ALU.is_equal).then_inc(sem("hot_src"), 1)
                dve.tensor_scalar(hot[:, 0:T], iota[:, :], d, None, ALU.is_equal)
                dve.tensor_scalar(hot[:, 3 * T:4 * T], iota[:, :], s, ew_lo[:, j:j + 1], ALU.is_equal,
                                  ALU.mult).then_inc(sem("hot"), 1)
                if j in (0, 1):
                    stats("ln0", x_tiles[j], j, f"x{j}_in", 16)
                if j in (1, 2):
                    normalize("ln0", x_tiles[j - 1], j - 1, xn_tiles[j - 1])
                if j in (5, 6):
                    low_turned("ln0", xT_lo, xT_hi, j - 5)
                if j in (7, 9, 11, 13):
                    low_fold((j - 7) // 4, (j - 7) // 2 % 2)
                if j == 16:
                    dve.wait_ge(sem("q_done"), nth("q_done", 1))
                    dve.tensor_scalar(fa[:, 0:512], bank[2][:, :], 0.0, None, ALU.min).then_inc(sem("q_min"), 1)
                if j == 18:
                    dve.wait_ge(sem("q_exp"), 1)
                    dve.scalar_tensor_tensor(out=fb[:, 0:512], in0=bank[2][:, :], scalar=0.0, in1=fa[:, 512:1024],
                                             op0=ALU.max, op1=ALU.add).then_inc(sem("q_f"), 1)
                if j == 19:
                    dve.wait_ge(sem("k_done"), nth("k_done", 1))
                    dve.tensor_scalar(fb[:, 512:1024], bank[3][:, :], 0.0, None, ALU.min).then_inc(sem("k_min"), 1)
                if j == 20:
                    low("q", qf_lo[:, :], fb[:, 0:512], qf_hi[:, :])
                if j == 21:
                    dve.wait_ge(sem("k_exp"), 1)
                    dve.scalar_tensor_tensor(out=xn[:, 1, :], in0=bank[3][:, :], scalar=0.0, in1=xn[:, 0, :],
                                             op0=ALU.max, op1=ALU.add).then_inc(sem("k_f"), 1)
                if j == 23:
                    low("k", kf_lo[:, :], xn[:, 1, :], kf_hi[:, :])
                if j in (25, 29):
                    tt = (j - 25) // 4
                    low("v", v_lo[:, tt * D:(tt + 1) * D], bank[4 + tt][:, :], v_hi[:, tt * D:(tt + 1) * D], tt + 1)
                if j == 26:
                    dve.wait_ge(sem("heads_made"), 1)
                    dve.wait_ge(sem("pcol_made"), 1)
                    dve.tensor_scalar(blockmask[:, :], blockmask[:, :], pcol[:, 1:2], None,
                                      ALU.is_equal).then_inc(sem("blockmask"), 1)
                if j == 30:
                    dve.wait_ge(sem("pidx_made"), 1)
                    dve.tensor_copy(pcol[0:64, 2:3], pcol[0:64, 0:1])
                    dve.wait_ge(sem("experts_made"), 1)
                    dve.tensor_scalar(pcol[64:P, 2:3], pcol[64:P, 0:1], -64.0, None, ALU.add).then_inc(sem("pmod"), 1)
                    dve.wait_ge(sem("pmod"), 1)
                    dve.tensor_scalar(sel[:, :], sel[:, :], pcol[:, 2:3], pcol[:, 3:4], ALU.is_equal,
                                      ALU.mult).then_inc(sem("sel_made"), 1)
            for h in range(2):
                low("adj", adj_lo[:, h, :], bank[h][:, :], adj_hi[:, h, :], h + 1)
            for tt in range(NT):
                low("pr", pr_lo[:, tt * D:(tt + 1) * D], bank[6 + tt][:, :], pr_hi[:, tt * D:(tt + 1) * D], tt + 1)
            dve.wait_ge(sem("kv_done"), nth("kv_done", 1))
            dve.wait_ge(sem("blockmask"), 1)
            dve.wait_ge(sem("q_lo"), nth("q_lo", 1))
            for m in range(2):
                dve.tensor_tensor(fb[:, m * 256:(m + 1) * 256], bank[2][:, m * 256:(m + 1) * 256], blockmask[:, :],
                                  ALU.mult).then_inc(sem("kv_f"), 1)
            dve.tensor_copy(ks[:, :], bank[3][:, 0:4:2]).then_inc(sem("ks"), 1)
            dve.tensor_copy(deg[:, :], bank[3][:, 8:12:2]).then_inc(sem("deg"), 1)
            dve.wait_ge(sem("ks"), 1)
            for m in range(2):
                dve.tensor_scalar(ksb[:, m, :], blockmask[:, 0:256:HD], ks[:, m:m + 1], None,
                                  ALU.mult).then_inc(sem("ksb"), 1)
            dve.wait_ge(sem("ksb"), 2)
            dve.tensor_copy(ks_hi[:, :, :], ksb[:, :, :]).then_inc(sem("ks_hi"), 1)
            dve.wait_ge(sem("deg"), 1)
            dve.reciprocal(degr[:, :], deg[:, :]).then_inc(sem("degr"), 1)
            dve.wait_ge(sem("ks_hi"), nth("ks_hi", 1))
            dve.tensor_tensor(ks_lo[:, :, :], ksb[:, :, :], f32(ks_hi[:, :, :]), ALU.subtract)
            low("kv", xT_lo[:, 0:512], fb[:, 0:512], xT_hi[:, 0:512])
            dve.wait_ge(sem("k_lo"), nth("k_lo", 1))
            dve.wait_ge(sem("norms_done"), 1)
            dve.tensor_scalar(nrm[:, :, :], bank[3][:, 64:80].rearrange("p (t h) -> p t h", t=NT), NORM_EPS, None,
                              ALU.add).then_inc(sem("nrm"), 1)
            dve.wait_ge(sem("nrm"), 1)
            dve.reciprocal(rden[:, :, :], nrm[:, :, :]).then_inc(sem("rden"), 1)
            dve.wait_ge(sem("rden"), 1)
            for tt in range(NT):
                dve.wait_ge(sem("z_done"), nth("z_done", tt + 1))
                dve.tensor_tensor(xn[:, tt, :].rearrange("p (h f) -> p h f", h=HEADS),
                                  bank[4 + tt][:, :].rearrange("p (h f) -> p h f", h=HEADS),
                                  rden[:, tt, :].unsqueeze(2).to_broadcast([P, HEADS, HD]),
                                  ALU.mult).then_inc(sem("z_xn"), 1)
            for tt in range(NT):
                low_turned("z", v_lo, v_hi, tt)
            dve.wait_ge(sem("degr"), 1)
            for tt in range(NT):
                dve.wait_ge(sem("agg0_done"), nth("agg0_done", tt + 1))
                dve.wait_ge(sem("base0"), NT + tt + 1)
                dve.scalar_tensor_tensor(out=base[:, tt, :], in0=bank[tt][:, :], scalar=degr[:, tt:tt + 1],
                                         in1=base[:, tt, :], op0=ALU.mult, op1=ALU.add).then_inc(sem("mixed0"), 1)
            for tt in range(NT):
                dve.wait_ge(sem("o_done"), nth("o_done", tt + 1))
                dve.wait_ge(sem("mixed0"), tt + 1)
                dve.tensor_tensor(xs[:, tt, :], bank[2 + tt][:, :], base[:, tt, :], ALU.add).then_inc(sem("x1"), 1)
                stats("ln1", x_tiles[tt], tt, "x1", tt + 1)
                if tt == 1:
                    low("ln1", tile_of(xT_lo, 0), tile_of(fb, 0), tile_of(xT_hi, 0), 1)
                normalize("ln1", x_tiles[tt], tt, xn_tiles[tt])
            low("ln1", tile_of(xT_lo, 1), tile_of(fb, 1), tile_of(xT_hi, 1), 2)

            def select(n, tt, k):
                w = (E0, E1)[n]
                dve.max(top[:, tt, :], lg[:, tt, 0:w]).then_inc(sem(f"top{n}"), 1)
                dve.wait_ge(sem(f"top{n}"), nth(f"top{n}", tt + 1))
                dve.tensor_scalar(wk[:, tt, 0:1], top[:, tt, 0:1], -1.0, None, ALU.mult).then_inc(sem(f"negmax{n}"), 1)
                dve.max_index(topi[:, tt, :], top[:, tt, :], lg[:, tt, 0:w]).then_inc(sem(f"topi{n}"), 1)
                dve.wait_ge(sem(f"topi{n}"), nth(f"topi{n}", tt + 1))
                dve.tensor_copy(topf[:, tt, 0:k], topi[:, tt, 0:k]).then_inc(sem(f"topf{n}"), 1)

            def spread_halves(n, b):
                dve.wait_ge(sem(f"comb{n}_turned"), nth(f"comb{n}_turned", 1))
                dve.tensor_scalar(combT16[64:P, :], b[64:P, 0:T], LO_SCALE, None, ALU.mult)\
                   .then_inc(sem(f"comb{n}_hi"), 1)
                dve.tensor_copy(combT16[0:64, :], b[0:64, 0:T])
                dve.wait_ge(sem(f"comb{n}_hi"), nth(f"comb{n}_hi", 1))
                dve.scalar_tensor_tensor(out=combT16[64:P, :], in0=b[64:P, 0:T], scalar=LO_SCALE,
                                         in1=combT16[64:P, :], op0=ALU.mult, op1=ALU.subtract)\
                   .then_inc(sem(f"comb{n}_16"), 1)
                dve.tensor_copy(combT[0:64, :], b[0:64, 0:T]).then_inc(sem(f"comb{n}_T"), 1)

            dve.wait_ge(sem("bg_in"), 16)
            dve.wait_ge(sem("lg0_done"), nth("lg0_done", 1))
            dve.tensor_tensor(lg[:, :, 0:E0], bank[4][:, 8:24].rearrange("p (t e) -> p t e", t=NT),
                              bgs[:, :].unsqueeze(1).to_broadcast([P, NT, E0]), ALU.add).then_inc(sem("lg0"), 1)
            dve.wait_ge(sem("lg0"), 1)
            dve.wait_ge(sem("iota2_made"), 1)
            for tt in range(NT):
                select(0, tt, 1)
            for tt in range(NT):
                dve.wait_ge(sem("sum0"), tt + 1)
                dve.reciprocal(wk[:, tt, 2:3], wk[:, tt, 1:2]).then_inc(sem("score0"), 1)
                dve.wait_ge(sem("score0"), tt + 1)
                dve.wait_ge(sem("topf0"), tt + 1)
                dve.tensor_scalar(comb[:, tt, :], iota2[:, :], topf[:, tt, 0:1], wk[:, tt, 2:3], ALU.is_equal,
                                  ALU.mult).then_inc(sem("comb0"), 1)
            spread_halves(0, bank[5])

            def hidden(tag, g, routed):
                for j in range(2):
                    a = slice(j * 512, (j + 1) * 512)
                    o = slice((g % 2) * 1024 + j * 512, (g % 2) * 1024 + (j + 1) * 512)
                    dve.wait_ge(sem(f"{tag}_act"), nth(f"{tag}_act", 4 * g + 2 * j + 2))
                    if g:
                        dve.wait_ge(sem(f"{tag}_act_lo"), nth(f"{tag}_act_lo", 2 * g - 1 + j))
                    if routed:
                        n = g - (SHARED_GROUPS if tag == "ffn1" else 0)
                        dve.wait_ge(sem(f"{tag}_spread"), nth(f"{tag}_spread", 2 * n + j + 1))
                        dve.tensor_tensor(fb[:, a], fa[:, a], bank[6 + j][:, :], ALU.mult)\
                           .then_inc(sem(f"{tag}_scaled"), 1)
                    else:
                        dve.tensor_scalar(fb[:, a], fa[:, a], SHARED_SCALE, None, ALU.mult)\
                           .then_inc(sem(f"{tag}_scaled"), 1)
                    dve.wait_ge(sem(f"{tag}_scaled"), nth(f"{tag}_scaled", 2 * g + j + 1))
                    if g >= 2:
                        dve.wait_ge(sem(f"{tag}_down"), nth(f"{tag}_down", 2 * (g - 2) + j + 1))
                    dve.tensor_copy(wide_hi[:, o], fb[:, a]).then_inc(sem(f"{tag}_act_hi"), 1)
                    dve.wait_ge(sem(f"{tag}_act_hi"), nth(f"{tag}_act_hi", 2 * g + j + 1))
                    dve.tensor_tensor(wide_lo[:, o], fb[:, a], f32(wide_hi[:, o]), ALU.subtract)\
                       .then_inc(sem(f"{tag}_act_lo"), 1)

            hidden("ffn0", 0, True)
            for tt in range(NT):
                dve.wait_ge(sem("ffn0_out"), tt + 1)
                dve.tensor_tensor(xs[:, tt, :], bank[tt][:, :], xs[:, tt, :], ALU.add).then_inc(sem("x2"), 1)
                stats("ln2", x_tiles[tt], tt, "x2", tt + 1)
                if tt == 1:
                    low_turned("ln2", xT_lo, xT_hi, 0)
                normalize("ln2", x_tiles[tt], tt, xn_tiles[tt])
            low_turned("ln2", xT_lo, xT_hi, 1)
            for tt in range(NT):
                low("sup", pr_lo[:, tt * D:(tt + 1) * D], bank[tt][:, :], pr_hi[:, tt * D:(tt + 1) * D], tt + 1)
            dve.wait_ge(sem("cols_in"), 16)
            def negative_norms(n, name):
                dve.wait_ge(sem(f"{name}_norm"), 1)
                dve.tensor_scalar(nrm[:, n, 0:2], bank[7][:, 8 * n:8 * n + 2], -0.5, None,
                                  ALU.mult).then_inc(sem(f"{name}_nb"), 1)

            for name, n, f, sq, col in (("k1", 0, fa, flat(xn), COL_BK), ("q1", 1, fb, fa, COL_BQ)):
                for h in range(2):
                    dve.wait_ge(sem(f"{name}_done"), nth(f"{name}_done", h + 1))
                    for mm in range(2):
                        m = 2 * h + mm
                        dve.tensor_scalar(f[:, m * T:(m + 1) * T], bank[2 + 2 * n + h][:, mm * T:(mm + 1) * T],
                                          colsb[:, col + m:col + m + 1], None, ALU.add).then_inc(sem(f"{name}_f"), 1)
                for h in range(2):
                    a = slice(h * 512, (h + 1) * 512)
                    o = slice(n * 1024 + h * 512, n * 1024 + (h + 1) * 512)
                    low(name, wide_lo[:, o], f[:, a], wide_hi[:, o], h + 1)
                dve.wait_ge(sem(f"{name}_sq"), 2)
                dve.tensor_tensor(sq[:, 0:512], sq[:, 0:512], sq[:, 512:1024], ALU.add).then_inc(sem(f"{name}_sum"), 1)
                dve.wait_ge(sem(f"{name}_sum"), 1)
                dve.tensor_tensor(sq[:, 0:T], sq[:, 0:T], sq[:, T:2 * T], ALU.add).then_inc(sem(f"{name}_sum"), 1)
                if n:
                    negative_norms(0, "k1")
            negative_norms(1, "q1")
            def low_scaled(tag, lo, i, hi):
                dve.wait_ge(sem(f"{tag}_hi"), nth(f"{tag}_hi", 1))
                dve.scalar_tensor_tensor(out=lo, in0=i, scalar=M1 ** -0.5, in1=f32(hi), op0=ALU.mult,
                                         op1=ALU.subtract).then_inc(sem(f"{tag}_lo"), 1)

            low_scaled("kp", kf_lo[:, :], fb[:, 512:1024], kf_hi[:, :])
            dve.wait_ge(sem("rows1_in"), 16)
            for tt in range(NT):
                dve.wait_ge(sem("v1_done"), nth("v1_done", tt + 1))
                dve.tensor_tensor(xn[:, tt, :], bank[4 + tt][:, :], rows[:, ROW_V1, :], ALU.add)\
                   .then_inc(sem("v1_f"), 1)
            for tt in range(NT):
                a = slice(tt * D, (tt + 1) * D)
                low("v1", v_lo[:, a], xn[:, tt, :], v_hi[:, a], tt + 1)
            low_scaled("qp", qf_lo[:, :], bank[3][:, :], qf_hi[:, :])
            for m in range(2):
                a = slice(m * D, (m + 1) * D)
                low("kv1", xT_lo[:, a], bank[(6, 2)[m]][:, :], xT_hi[:, a], m + 1)
            dve.wait_ge(sem("ksum1_done"), nth("ksum1_done", 1))
            sums = bank[7][:, 16:20].rearrange("p (m c) -> p m c", m=2)
            dve.tensor_copy(ks_hi[:, :, 0:2], sums).then_inc(sem("ks1_hi"), 1)
            dve.wait_ge(sem("ks1_hi"), nth("ks1_hi", 1))
            dve.tensor_tensor(ks_lo[:, :, 0:2], sums, f32(ks_hi[:, :, 0:2]), ALU.subtract).then_inc(sem("ks1_lo"), 1)
            for h in range(2):
                a = slice(h * 512, (h + 1) * 512)
                low("y1", v_lo[:, a], bank[4 + h][:, :], v_hi[:, a], h + 1)
            dve.wait_ge(sem("den1_done"), nth("den1_done", 1))
            dve.tensor_scalar(deg[:, :], bank[7][:, 24:28:2], DENOM_EPS, None, ALU.add).then_inc(sem("den1"), 1)
            dve.wait_ge(sem("den1"), 1)
            dve.reciprocal(degr[:, :], deg[:, :]).then_inc(sem("denr1"), 1)
            for tt in range(NT):
                dve.wait_ge(sem("agg1_done"), nth("agg1_done", tt + 1))
                dve.wait_ge(sem("base1"), 4)
                dve.tensor_tensor(base[:, tt, :], bank[tt][:, :], base[:, tt, :], ALU.add).then_inc(sem("mixed1"), 1)
            dve.wait_ge(sem("denr1"), 1)

            def affine(tag, g, b, tt):
                dve.wait_ge(sem(f"{tag}_turned"), nth(f"{tag}_turned", tt + 1))
                for kt in range(KT // 2):
                    dve.tensor_scalar(fb[:, kt * T + tt * P:kt * T + (tt + 1) * P],
                                      bank[6 + tt][:, kt * P:(kt + 1) * P], colsb[:, g + kt:g + kt + 1],
                                      colsb[:, b + kt:b + kt + 1], ALU.mult, ALU.add).then_inc(sem(f"{tag}_affine"), 1)

            for tt in range(NT):
                dve.wait_ge(sem("p1_done"), nth("p1_done", tt + 1))
                dve.wait_ge(sem("mixed1"), tt + 1)
                dve.scalar_tensor_tensor(out=xs[:, tt, :], in0=bank[2 + tt][:, :], scalar=degr[:, tt:tt + 1],
                                         in1=base[:, tt, :], op0=ALU.mult, op1=ALU.add).then_inc(sem("x3"), 1)
                stats("ln3", x_tiles[tt], tt, "x3", tt + 1)
                if tt == 1:
                    affine("ln4", COL_LN_G, COL_LN_B, 0)
                dve.wait_ge(sem("normed_rstd"), tt + 1)
                dve.tensor_scalar(xn[:, tt, :], xs[:, tt, :], mv[:, tt, 0:1], rstd2[:, tt:tt + 1], ALU.subtract,
                                  ALU.mult).then_inc(sem("ln4_xn"), 1)
            affine("ln4", COL_LN_G, COL_LN_B, 1)
            for tt in range(NT):
                low("ln4", tile_of(xT_lo, tt), tile_of(fb, tt), tile_of(xT_hi, tt), tt + 1)
            for tt in range(NT):
                normalize("ln3", x_tiles[tt], tt, fa_tiles[tt])
            dve.wait_ge(sem("lg1_done"), nth("lg1_done", 1))
            dve.tensor_scalar(lg[:, :, :], bank[5][:, 0:NT * E1].rearrange("p (t e) -> p t e", t=NT), 1.0 / TEMP,
                              None, ALU.mult).then_inc(sem("lg1"), 1)
            dve.wait_ge(sem("lg1"), 1)
            for tt in range(NT):
                select(1, tt, 2)
            for tt in range(NT):
                dve.wait_ge(sem("sum1"), tt + 1)
                dve.reciprocal(wk[:, tt, 4:5], wk[:, tt, 1:2]).then_inc(sem("score1"), 1)
                dve.wait_ge(sem("score1"), tt + 1)
                dve.tensor_scalar(wk[:, tt, 5:7], wk[:, tt, 2:4], wk[:, tt, 4:5], None, ALU.mult)\
                   .then_inc(sem("weights1"), 1)
                dve.wait_ge(sem("weights1"), tt + 1)
                dve.wait_ge(sem("topf1"), tt + 1)
                for k, c in enumerate((comb, comb2)):
                    dve.tensor_scalar(c[:, tt, :], iota2[:, :], topf[:, tt, k:k + 1], wk[:, tt, 5 + k:6 + k],
                                      ALU.is_equal, ALU.mult).then_inc(sem("picked"), 1)
                dve.wait_ge(sem("picked"), 2 * tt + 2)
                dve.tensor_tensor(comb[:, tt, :], comb[:, tt, :], comb2[:, tt, :], ALU.add).then_inc(sem("comb1"), 1)
            hidden("ffn1", 0, False)
            hidden("ffn1", 1, False)
            spread_halves(1, bank[4])
            for g in range(SHARED_GROUPS, GROUPS):
                hidden("ffn1", g, g >= SHARED_GROUPS)
            for tt in range(NT):
                dve.wait_ge(sem("ffn1_out"), tt + 1)
                dve.scalar_tensor_tensor(out=fa_tiles[tt], in0=rows[:, ROW_SH, :], scalar=SHARED_SCALE,
                                         in1=bank[tt][:, :], op0=ALU.mult, op1=ALU.add).then_inc(sem("hmoe"), 1)
                stats("ln5", fa_tiles[tt], tt, "hmoe", tt + 1)
                if tt == 1:
                    affine("ln5", COL_FF_G, COL_FF_B, 0)
                normalize("ln5", fa_tiles[tt], tt, xn_tiles[tt])
            low("ln5", tile_of(xT_lo, 0), tile_of(fb, 0), tile_of(xT_hi, 0), 1)
            affine("ln5", COL_FF_G, COL_FF_B, 1)
            low("ln5", tile_of(xT_lo, 1), tile_of(fb, 1), tile_of(xT_hi, 1), 2)
            for tt in range(NT):
                dve.wait_ge(sem("f2_done"), tt + 1)
                dve.wait_ge(sem("base3"), tt + 1)
                dve.tensor_tensor(xs[:, tt, :], bank[6 + tt][:, :], base[:, tt, :], ALU.add).then_inc(sem("y_done"), 1)


def blocks_of(m):
    return m.reshape(KT, P, -1).transpose(1, 0, 2).reshape(P, -1)


def kernel(**inputs):
    import concourse.bacc as bacc
    from concourse.bass_utils import run_bass_kernel_spmd

    w = {k: np.asarray(v) for k, v in inputs.items()}
    qkv0, qkv1 = w["L0_mix_W_qkv"], w["L1_mix_w_qkv"]
    blocks = [
        qkv0[:, 0:D].T, qkv0[:, D:2 * D].T, qkv0[:, 2 * D:], w["L0_gnn_W"].T, w["L0_mix_W_out"],
        w["L0_ffn_W1"].transpose(1, 0, 2).reshape(D, D), w["L0_ffn_W2"].reshape(D, D), w["L1_gnn_weight"],
        qkv1[0:D].T, qkv1[D:2 * D].T, qkv1[2 * D:].T, w["L1_mix_w_proj"].T,
    ]
    ws1, ws2, w1, w2 = w["L1_ffn_Ws1"], w["L1_ffn_Ws2"], w["L1_ffn_W1"], w["L1_ffn_W2"]
    for kind, g in FFN1_ORDER:
        if g < SHARED_GROUPS:
            blocks.append(ws1[:, g * D:(g + 1) * D] if kind == "up" else ws2[g * D:(g + 1) * D])
        else:
            e = slice((g - SHARED_GROUPS) * D // DFF, (g - SHARED_GROUPS + 1) * D // DFF)
            blocks.append(w1[e].transpose(1, 0, 2).reshape(D, D) if kind == "up" else w2[e].reshape(D, D))
    static = np.zeros((P, 2048), np.float32)
    static[:, ST_FEAT:ST_RF] = blocks_of(w["L1_mix_w_feat"].T)
    static[:, ST_RF:ST_RF + KT * P] = blocks_of(np.concatenate([w["L1_ffn_Wr"], w["L1_ffn_Wf1"]], 1))
    packed = [blocks_of(b) for b in blocks]
    packed.insert(RAW_STATIC, static)
    cols = np.zeros((P, COLS), np.float32)
    for at, v in ((COL_B1_0, w["L0_ffn_b1"]), (COL_LN_G, w["L1_ffn_ln1_g"]), (COL_LN_B, w["L1_ffn_ln1_b"]),
                  (COL_FF_G, w["L1_ffn_ffln_g"]), (COL_FF_B, w["L1_ffn_ffln_b"]), (COL_BK, w["L1_mix_b_qkv"][0:D]),
                  (COL_BQ, w["L1_mix_b_qkv"][D:2 * D]), (COL_B1, w["L1_ffn_bs1"]), (COL_B1 + 8, w["L1_ffn_b1"])):
        v = v.reshape(-1, P).T
        cols[:, at:at + v.shape[1]] = v
    cols[64:P, COL_BF1] = w["L1_ffn_bf1"]
    small = np.zeros((P, SMALL), np.float32)
    small[0:HD, 0:FD] = small[HD:P, FD:HD] = w["L0_mix_random_matrix"]
    small[:, SM_WG:] = blocks_of(w["L0_ffn_Wg"])
    arrays = {
        "x": w["x"], "src": w["src"].reshape(P, ET), "dst": w["dst"].reshape(P, ET),
        "ew": w["edge_weight"].reshape(P, ET), "stream": np.stack(packed), "cols": cols, "small": small,
        "bg": w["L0_ffn_bg"].reshape(1, E0),
        "rows0": np.stack([w["L0_gnn_b"], w["L0_mix_b_out"]]),
        "rows1": np.stack([w["L1_gnn_bias"], w["L1_mix_b_proj"], w["L1_mix_b_qkv"][2 * D:], w["L1_ffn_bs2"],
                           w["L1_ffn_bf2"]]),
        "codebook": w["L1_ffn_codebook"].T, "b2_0": w["L0_ffn_b2"], "b2_1": w["L1_ffn_b2"],
        "wf2": w["L1_ffn_Wf2"],
    }
    arrays = {k: np.ascontiguousarray(v) for k, v in arrays.items()}
    nc = bacc.Bacc("TRN2", target_bir_lowering=False, num_devices=1)
    aps = {k: nc.dram_tensor(k, v.shape, mybir.dt.from_np(v.dtype), kind="ExternalInput").ap()
           for k, v in arrays.items()}
    out = nc.dram_tensor("out", (T, D), F32, kind="ExternalOutput").ap()
    gnn_kernel(nc, out=out, **aps)
    r = run_bass_kernel_spmd(nc, [arrays], core_ids=[0])
    return r.results[0]["out"]
```

```python
from contextlib import ExitStack

import numpy as np

import concourse.bass as bass
from concourse import mybir

ALU = mybir.AluOpType
ACT = mybir.ActivationFunctionType
F32 = mybir.dt.float32
F32R = mybir.dt.float32r
F16 = mybir.dt.float16
I32 = mybir.dt.int32
U32 = mybir.dt.uint32

P = 128
T = 256
D = 512
NT = T // P
KT = D // P
EDGES = 4352
ET = EDGES // P
HEADS = 8
HD = D // HEADS
FD = HD // 2
E0 = 8
E1 = 64
DFF = 64
M1 = 256
SHARED_GROUPS = 2
GROUPS = SHARED_GROUPS + E1 * DFF // D
LN_EPS = 1e-5
NORM_EPS = 1e-6
DENOM_EPS = 1e-8
TEMP = 0.7
SHARED_SCALE = 0.25
LO_SCALE = 4096.0

VW = D // 2 + 2
HOTS = 4
TURN_AT, FOLD_AT, QUERY_AT, KEY_AT, VALUE_AT = 1, 3, 12, 15, 17
GNN_AT = VALUE_AT + NT * KT
SLOTS = 4
RAWS = 4

UNSPLIT = 2
V0, GNN0, OUT0, UP0, DOWN0, GNN1, K1, Q1, V1, PROJ1, FFN1 = range(11)
STATIC_AT = K1


def ffn1_blocks():
    order = [("up", 0)]
    for g in range(GROUPS):
        if g + 1 < GROUPS:
            order.append(("up", g + 1))
        order.append(("down", g))
    return order


FFN1_ORDER = ffn1_blocks()
BLOCKS = FFN1 + len(FFN1_ORDER)

STEADY = FFN1_ORDER.index(("up", SHARED_GROUPS))
BODY = 4
LAPS = (len(FFN1_ORDER) - STEADY) // BODY
assert SLOTS == BODY and RAWS == BODY


def at(n, lap, step):
    return n if lap is None else lap * step + n


def raw_index(i):
    return UNSPLIT + i + (1 if i >= STATIC_AT else 0)


RAW_STATIC = UNSPLIT + STATIC_AT
N_RAW = UNSPLIT + BLOCKS + 1

COL_B1_0, COL_LN_G, COL_LN_B, COL_FF_G, COL_FF_B, COL_BK, COL_BQ, COL_B1 = 0, 4, 8, 12, 16, 20, 24, 28
COL_BF1 = COL_B1 + 4 * GROUPS
COLS = COL_BF1 + 1
SM_R, SM_WG = 0, HD
SMALL = HD + KT * E0
ST_FEAT, ST_RF = 0, KT * M1
STATIC = ST_RF + KT * P
ROW_GNN0, ROW_OUT0 = 0, 1
ROW_GNN1, ROW_PROJ1 = 0, 1
ROW_SH, ROW_F2 = 0, 1
ROW_V1 = 2


NORMS = (("ln0", 2), ("z", 2), ("ln1", 2), ("ln2", 2), ("ln4", 2), ("ln3", 2), ("ln5", 2))
LN = (("ln0", 2), ("ln1", 2), ("ln2", 2), ("ln3", 2), ("ln5", 2))
CUTS = (("ln0", 2), ("fold", 4), ("q", 1), ("k", 1), ("v", 2), ("adj", 2), ("pr", 2), ("kv", 1), ("z", 2), ("ln1", 2),
        ("ln2", 2), ("sup", 2), ("k1", 2), ("q1", 2), ("kp", 1), ("v1", 2), ("qp", 1), ("kv1", 2), ("y1", 2),
        ("ln4", 2), ("ln5", 2))
SERIES = {
    "bn": LN, "mv": LN, "var": LN, "rstd": LN, "xn": NORMS,
    "turned": tuple(n for n in NORMS if n[0] != "ln3"), "hi": CUTS, "lo": CUTS, "affine": (("ln4", 4), ("ln5", 4)), "affine2": (("ln4", 4), ("ln5", 4)),
    "f": (("q", 1), ("k", 1), ("kv", 2), ("k1", 4), ("q1", 4), ("v1", 2)),
    "done": (("fold", 4), ("q", 1), ("k", 1), ("v", 2), ("g", 2), ("kv", 1), ("agg0", 2), ("z", 2), ("o", 2),
             ("lg0", 1), ("s", 2), ("k1", 2), ("q1", 2), ("v1", 2), ("ksum1", 1),
             ("kv1", 2), ("p1", 2), ("r", 1), ("lg1", 1)),
}


def series(name):
    stage, _, what = name.rpartition("_")
    before = 0
    for other, times in SERIES.get(what, ()):
        if other == stage:
            return f"all_{what}", before
        before += times
    return name, 0


def nth(name, n):
    return series(name)[1] + n


def last_use(i):
    if i < FFN1:
        return (("v_done", 2), ("g_done", 2), ("o_done", 2), ("ffn0_up", 2),
                ("ffn0_out", 2), ("s_done", 2), ("k1_done", 2), ("q1_done", 2), ("v1_done", 2), ("p1_done", 2))[i]
    kind, g = FFN1_ORDER[i - FFN1]
    return f"ffn1_{kind}", 2 * g + 2


def gnn_kernel(nc, x, src, dst, ew, stream, cols, small, bg, rows0, rows1, codebook, b2_0, b2_1, wf2, out):
    with ExitStack() as ctx:
        def sb(name, shape, dt=F32):
            return ctx.enter_context(nc.sbuf_tensor(name, shape, dt))

        sems = {}

        def sem(name):
            name = series(name)[0]
            if name not in sems:
                sems[name] = ctx.enter_context(nc.semaphore(name))
            return sems[name]

        bank = [ctx.enter_context(nc.psum_tensor(f"bank{i}", [P, 512], F32)) for i in range(8)]

        raw = sb("raw", [P, RAWS, 2048])
        w_hi = [sb(f"w_hi{i}", [P, 2048], F32R) for i in range(SLOTS)]
        w_lo = [sb(f"w_lo{i}", [P, 2048], F32R) for i in range(SLOTS)]
        st_hi = sb("static_hi", [P, STATIC], F32R)
        st_lo = sb("static_lo", [P, STATIC], F32R)
        xs = sb("xs", [P, NT, D])
        base = sb("base", [P, NT, D])
        xn = sb("xn", [P, NT, D])
        xT_hi = sb("xT_hi", [P, 1024], F32R)
        xT_lo = sb("xT_lo", [P, 1024], F32R)
        v_hi = sb("v_hi", [P, NT * 2 * VW], F32R)
        v_lo = sb("v_lo", [P, NT * 2 * VW], F32R)
        pr_hi = sb("proj_hi", [P, 1024], F32R)
        pr_lo = sb("proj_lo", [P, 1024], F32R)
        wide_hi = sb("wide_hi", [P, 2048], F32R)
        wide_lo = sb("wide_lo", [P, 2048], F32R)
        qf_hi = sb("qf_hi", [P, 512], F32R)
        qf_lo = sb("qf_lo", [P, 512], F32R)
        kf_hi = sb("kf_hi", [P, 512], F32R)
        kf_lo = sb("kf_lo", [P, 512], F32R)
        fa = sb("fa", [P, 1024])
        fb = sb("fb", [P, 1024])
        adj_hi = sb("adj_hi", [P, 2, 512], F32R)
        adj_lo = sb("adj_lo", [P, 2, 512], F32R)
        sel = sb("sel", [P, E1 * DFF], F16)
        rows = sb("rows", [P, 3, D])
        colsb = sb("colsb", [P, COLS])
        smr = sb("small_raw", [P, SMALL])
        b2s = sb("b2s", [P, D])
        cbs = sb("cbs", [64, E1])
        bgs = sb("bgs", [P, E0])
        ident = sb("ident", [P, P])
        iota = sb("iota", [P, T])
        blockmask = sb("blockmask", [P, 256])
        edge_i = sb("edge_i", [P, 2, ET], I32)
        edge_f = sb("edge_f", [P, 2, ET])
        ewf = sb("ewf", [P, ET])
        ew_hi = sb("ew_hi", [P, ET], F32R)
        ew_lo = sb("ew_lo", [P, ET])
        ones = sb("ones", [P, P], F32R)
        ones32 = sb("ones32", [P, 2])
        pcol = sb("pcol", [P, 4])
        mhalf = sb("mhalf", [P, 2])
        warm = sb("warm", [P, 2])
        st = sb("bnst", [P, NT, 6])
        mv = sb("mv", [P, NT, 2])
        ve = sb("ve", [P, NT])
        rstd = sb("rstd", [P, NT])
        ve2 = sb("ve2", [P, NT])
        rstd2 = sb("rstd2", [P, NT])
        ksb = sb("ksb", [P, 2, 4])
        ks_hi = sb("ks_hi", [P, 2, 4], F32R)
        ks_lo = sb("ks_lo", [P, 2, 4], F32R)
        nrm = sb("nrm", [P, 2, 8])
        rden = sb("rden", [P, 2, 8])
        lg = sb("logits", [P, NT, E1])
        pe_ = sb("expl", [P, NT, E0])
        top = sb("top", [P, NT, 8])
        topi = sb("topi", [P, NT, 8], U32)
        topf = sb("topf", [P, NT, 8])
        wk = sb("wk", [P, NT, 8])
        comb = sb("comb", [P, NT, P])
        comb2 = xn[:, 1, 0:NT * P].rearrange("p (n e) -> p n e", n=NT)
        combT = blockmask
        combT16 = iota[:, 0:T // 2].bitcast(F16)
        rT = xn[0:64, 0, 0:T]
        iota2 = smr[:, 0:64].bitcast(F16)
        deg = sb("deg", [P, NT])
        degr = sb("degr", [P, NT])

        block = ctx.enter_context(nc.Block())

        hots = (adj_hi[:, :, :].rearrange("p a b -> p (a b)"), adj_lo[:, :, :].rearrange("p a b -> p (a b)"),
                pr_hi[:, :], pr_lo[:, :])

        def flat(t):
            return t[:, :, :].rearrange("p a b -> p (a b)")

        def f32(ap):
            return ap.bitcast(F32)

        def tile_of(t, tt):
            return t[:, 0:KT * T].rearrange("p (k t) -> p k t", k=KT)[:, :, tt * P:(tt + 1) * P]

        def tile_of_bank(b):
            return bank[b][:, :].rearrange("p (k t) -> p k t", k=KT)

        def values(t, tt, at=0, to=D // 2):
            return t[:, 2 * tt * VW:2 * (tt + 1) * VW].rearrange("p (m c) -> p m c", m=2)[:, :, at:to]

        def halves(b):
            return b[:, :].rearrange("p (m c) -> p m c", m=2)

        def folded(t, n, h):
            return t[:, :].rearrange("p (m c) -> p m c", m=KT)[:, 2 * h:2 * h + 2, n * T:(n + 1) * T]

        @block.sync
        def _(sp):
            sp.dma_start(edge_i[:, 0, :], src).then_inc(sem("src_in"), 16)
            for tt in range(NT):
                sp.dma_start(xs[:, tt, :], x[tt * P:(tt + 1) * P, :]).then_inc(sem(f"x{tt}_in"), 16)

            def load(r, lap=None):
                if r >= RAWS + UNSPLIT:
                    sp.wait_ge(sem("raw_used"), at(r - RAWS - UNSPLIT + 1, lap, BODY))
                elif r >= RAWS:
                    sp.wait_ge(sem("fold_done"), nth("fold_done", 2 * (r - RAWS) + 2))
                sp.dma_start(raw[:, r % RAWS, :], stream[at(r, lap, BODY)]).then_inc(sem(f"raw_in{r % RAWS}"), 16)

            sp.dma_start(smr[:, :], small).then_inc(sem("small_in"), 16)
            load(0)
            sp.dma_start(bgs[:, :], bg[0, :].partition_broadcast(P)).then_inc(sem("bg_in"), 16)
            load(1)
            sp.dma_start(colsb[:, :], cols).then_inc(sem("cols_in"), 16)
            sp.dma_start(rows[:, 0:2, :], rows0.partition_broadcast(P)).then_inc(sem("rows0_in"), 16)
            load(2)
            sp.dma_start(b2s[0:E0, :], b2_0).then_inc(sem("b2_0_in"), 16)
            sp.dma_start(b2s[64:P, :], wf2).then_inc(sem("wf2_in"), 16)
            sp.dma_start(cbs[:, :], codebook).then_inc(sem("codebook_in"), 16)
            sp.dma_start(rows[:, ROW_V1, :], rows1[ROW_V1, :].partition_broadcast(P)).then_inc(sem("v1_row_in"), 16)
            steady = N_RAW - LAPS * BODY
            for r in range(3, steady):
                load(r)
                if r == 6:
                    sp.wait_ge(sem("base0"), 2 * NT)
                    sp.dma_start(rows[:, 0:2, :], rows1[0:2, :].partition_broadcast(P)).then_inc(sem("rows1_in"), 16)
                if r == 14:
                    sp.wait_ge(sem("ffn0_out"), 2)
                    sp.dma_start(b2s[0:E1, :], b2_1).then_inc(sem("b2_1_in"), 16)
                    sp.wait_ge(sem("base1"), 2 * NT)
                    sp.dma_start(rows[:, 0:2, :], rows1[3:5, :].partition_broadcast(P)).then_inc(sem("rows2_in"), 16)
            with sp.Fori(0, LAPS) as lap:
                for k in range(BODY):
                    load(steady + k, lap)
            for tt in range(NT):
                sp.wait_ge(sem("y_done"), nth("y_done", tt + 1))
                sp.dma_start(out[tt * P:(tt + 1) * P, :], xs[:, tt, :]).then_inc(sem("stored"), 16)
            sp.wait_ge(sem("stored"), 16 * NT)

        @block.gpsimd
        def _(pool):
            pool.memset(mhalf[:, :], -0.5).then_inc(sem("mhalf_made"), 1)
            pool.memset(ident[:, :], 0.0).then_inc(sem("zeroed"), 1)
            pool.iota(iota[:, :], [[1, T]], 0, 0, allow_small_or_imprecise_dtypes=True).then_inc(sem("iota_made"), 1)
            pool.wait_ge(sem("zeroed"), 1)
            pool.affine_select(out=ident[:, :], in_=ident[:, :], compare_op=ALU.not_equal, fill=1.0, base=0,
                               pattern=[[-1, P]], channel_multiplier=1).then_inc(sem("ident_made"), 1)

            def rsqrt(tag):
                pool.wait_ge(sem("mhalf_made"), 1)
                for tt in range(NT):
                    pool.wait_ge(sem(f"{tag}_var"), nth(f"{tag}_var", tt + 1))
                    pool.tensor_tensor(rstd[:, tt:tt + 1], ve[:, tt:tt + 1], mhalf[:, 0:1],
                                       ALU.pow).then_inc(sem(f"{tag}_rstd"), 1)

            rsqrt("ln0")
            pool.iota(pcol[:, 0:1], [[0, 1]], 0, 1, allow_small_or_imprecise_dtypes=True).then_inc(sem("pidx_made"), 1)
            pool.iota(blockmask[:, :], [[1, 4], [0, HD]], 0, 0,
                      allow_small_or_imprecise_dtypes=True).then_inc(sem("heads_made"), 1)
            pool.iota(sel[:, :], [[1, E1], [0, DFF]], 0, 0,
                      allow_small_or_imprecise_dtypes=True).then_inc(sem("experts_made"), 1)

            pool.wait_ge(sem("rows0_in"), 16)
            for tt in range(NT):
                pool.wait_ge(sem(f"x{tt}_in"), 16)
                pool.tensor_tensor(base[:, tt, :], xs[:, tt, :], rows[:, ROW_OUT0, :],
                                   ALU.add).then_inc(sem("base0"), 1)
            for tt in range(NT):
                pool.wait_ge(sem("base0"), tt + 1)
                pool.tensor_tensor(base[:, tt, :], base[:, tt, :], rows[:, ROW_GNN0, :],
                                   ALU.add).then_inc(sem("base0"), 1)

            def base1():
                pool.wait_ge(sem("rows1_in"), 16)
                for n, row in enumerate((ROW_GNN1, ROW_PROJ1)):
                    for tt in range(NT):
                        if n == 0:
                            pool.wait_ge(sem("x2"), tt + 1)
                        else:
                            pool.wait_ge(sem("base1"), tt + 1)
                        pool.tensor_tensor(base[:, tt, :], (base if n else xs)[:, tt, :], rows[:, row, :],
                                           ALU.add).then_inc(sem("base1"), 1)

            def base2():
                pool.wait_ge(sem("rows2_in"), 16)
                for tt in range(NT):
                    pool.wait_ge(sem("ln3_xn"), nth("ln3_xn", tt + 1))
                    pool.tensor_tensor(base[:, tt, :], xs[:, tt, :], fa[:, tt * D:(tt + 1) * D],
                                       ALU.add).then_inc(sem("base2"), 1)
                for tt in range(NT):
                    pool.wait_ge(sem("base2"), tt + 1)
                    pool.tensor_tensor(base[:, tt, :], base[:, tt, :], rows[:, ROW_F2, :],
                                       ALU.add).then_inc(sem("base2"), 1)

            def low(i, lap=None):
                pool.wait_ge(sem("hi_cut"), at(i + 1, lap, BODY))
                pool.tensor_tensor(w_lo[i % SLOTS][:, :], raw[:, raw_index(i) % RAWS, :],
                                   f32(w_hi[i % SLOTS][:, :]), ALU.subtract).then_inc(sem("raw_used"), 1)

            def low_static():
                pool.wait_ge(sem("static_hi_cut"), 1)
                pool.tensor_tensor(st_lo[:, :], raw[:, RAW_STATIC % RAWS, 0:STATIC], f32(st_hi[:, :]),
                                   ALU.subtract).then_inc(sem("raw_used"), 1)

            for i in range(FFN1 + STEADY):
                if i == 3:
                    pool.wait_ge(sem("fold_done"), nth("fold_done", 4))
                    pool.iota(iota2[:, :], [[0, 2], [1, E1]], 0, 0,
                              allow_small_or_imprecise_dtypes=True).then_inc(sem("iota2_made"), 1)
                if i == 6:
                    rsqrt("ln1")
                if i == STATIC_AT:
                    low_static()
                if i == 7:
                    rsqrt("ln2")
                    base1()
                low(i)
            for tt in range(NT):
                pool.wait_ge(sem("normed_var"), tt + 1)
                pool.tensor_tensor(rstd2[:, tt:tt + 1], ve2[:, tt:tt + 1], mhalf[:, 0:1],
                                   ALU.pow).then_inc(sem("normed_rstd"), 1)
            rsqrt("ln3")
            base2()
            with pool.Fori(0, LAPS) as lap:
                for k in range(BODY):
                    low(FFN1 + STEADY + k, lap)
            for i in range(FFN1 + STEADY + LAPS * BODY, BLOCKS):
                low(i)
            rsqrt("ln5")
            for tt in range(NT):
                pool.wait_ge(sem("hmoe"), tt + 1)
                pool.wait_ge(sem("base2"), 4)
                pool.tensor_tensor(base[:, tt, :], base[:, tt, :], fa[:, tt * D:(tt + 1) * D],
                                   ALU.add).then_inc(sem("base3"), 1)

        def weights_ready(eng, i, lap=None):
            eng.wait_ge(sem("raw_used"), at(raw_index(i) - UNSPLIT + 1, lap, BODY))

        @block.tensor
        def _(pe):
            def mm3(o, a_hi, a_lo, b_hi, b_lo, first, last):
                pe.matmul(o, a_hi, b_hi, start=first, stop=False)
                pe.matmul(o, a_hi, b_lo, start=False, stop=False)
                return pe.matmul(o, a_lo, b_hi, start=False, stop=last)

            def early(o, parts, late):
                for k, (a_hi, a_lo, b_hi, b_lo) in enumerate(parts):
                    pe.matmul(o, a_hi, b_hi, start=(k == 0), stop=False)
                    if late == "a":
                        pe.matmul(o, a_hi, b_lo, start=False, stop=False)
                    else:
                        pe.matmul(o, a_lo, b_hi, start=False, stop=False)

            def after_low(o, parts, late, event, n):
                pe.wait_ge(sem(event), nth(event, n))
                for k, (a_hi, a_lo, b_hi, b_lo) in enumerate(parts):
                    x, y = (a_lo, b_hi) if late == "a" else (a_hi, b_lo)
                    ins = pe.matmul(o, x, y, start=False, stop=(k == len(parts) - 1))
                return ins

            def grouped(o, parts, late, event, n):
                early(o, parts, late)
                return after_low(o, parts, late, event, n)

            def token_parts(t_hi, t_lo, i, tt):
                return [(t_hi[:, kt * T + tt * P:kt * T + (tt + 1) * P], t_lo[:, kt * T + tt * P:kt * T + (tt + 1) * P],
                         w_hi[i % SLOTS][:, kt * D:(kt + 1) * D], w_lo[i % SLOTS][:, kt * D:(kt + 1) * D])
                        for kt in range(KT)]

            def keep_clock(n, b, operand):
                for _ in range(n):
                    pe.matmul(bank[b][:, :], operand[:, 0:P], operand[:, 0:512], start=True, stop=True)

            def turn(tag, tt, halved=False):
                pe.wait_ge(sem(f"{tag}_xn"), nth(f"{tag}_xn", tt + 1))
                for kt in range(KT):
                    b = bank[(4 if halved and kt >= KT // 2 else 6) + tt]
                    ins = pe.transpose(b[:, kt * P:(kt + 1) * P], xn[:, tt, kt * P:(kt + 1) * P], ident[:, :])
                ins.then_inc(sem(f"{tag}_turned"), 1)

            def tokens_out(tag, banks, i, tt, kts=range(KT)):
                weights_ready(pe, i)
                for kt in kts:
                    a = slice(kt * T + tt * P, kt * T + (tt + 1) * P)
                    b = slice(kt * D, (kt + 1) * D)
                    ins = mm3(bank[banks[tt]][:, :], xT_hi[:, a], xT_lo[:, a], w_hi[i % SLOTS][:, b],
                              w_lo[i % SLOTS][:, b], kt == 0, kt == KT - 1)
                    if kt == KT - 1:
                        ins.then_inc(sem(tag), 1)

            pe.wait_ge(sem("ident_made"), 1)

            def edges(j):
                pe.wait_ge(sem("hot"), j + 1)
                pe.wait_ge(sem("hot_w"), j + 1)
                hot = hots[j % HOTS]
                for h in range(2):
                    lhs = hot[:, h * P:(h + 1) * P]
                    if j:
                        pe.matmul(bank[h][:, T:2 * T], lhs, hot[:, 3 * T:4 * T], start=False, stop=False)
                    ins = pe.matmul(bank[h][:, :], lhs, hot[:, T:3 * T], start=(j == 0), stop=(j == ET - 1))
                    if j == 0:
                        ins = pe.matmul(bank[h][:, T:2 * T], lhs, hot[:, 3 * T:4 * T], start=False, stop=False)
                ins.then_inc(sem("hot_used"), 1)

            def fold(n, m):
                pe.wait_ge(sem("small_in"), 16)
                pe.wait_ge(sem(f"raw_in{n}"), 16)
                for kt in range(KT):
                    a = slice(kt * D + m * P, kt * D + (m + 1) * P)
                    o = bank[2 + 2 * n + m // 2][:, (m % 2) * T + kt * HD:(m % 2) * T + (kt + 1) * HD]
                    ins = pe.matmul(o, raw[:, n, a], smr[:, SM_R:SM_R + HD], start=True, stop=True)
                if m % 2 == 1:
                    ins.then_inc(sem("fold_done"), 1)

            def query(m):
                pe.wait_ge(sem("ln0_lo"), nth("ln0_lo", 2))
                pe.wait_ge(sem("fold_lo"), nth("fold_lo", 2))
                for kt in range(KT):
                    a = slice(kt * 512 + m * P, kt * 512 + (m + 1) * P)
                    b = slice(kt * T, (kt + 1) * T)
                    ins = mm3(bank[2][:, m * T:(m + 1) * T], wide_hi[:, a], wide_lo[:, a], xT_hi[:, b], xT_lo[:, b],
                              kt == 0, kt == KT - 1)
                if m == 1:
                    ins.then_inc(sem("q_done"), 1)

            def key(tt):
                pe.wait_ge(sem("fold_lo"), nth("fold_lo", 4))
                for kt in range(KT):
                    a = slice(kt * T + tt * P, kt * T + (tt + 1) * P)
                    b = slice(kt * 512 + T, kt * 512 + 2 * T)
                    ins = mm3(bank[3][:, tt * T:(tt + 1) * T], xT_hi[:, a], xT_lo[:, a], wide_hi[:, b],
                              wide_lo[:, b], kt == 0, kt == KT - 1)
                if tt == 1:
                    ins.then_inc(sem("k_done"), 1)

            for _ in range(12):
                pe.matmul(bank[0][:, 0:P], ident[:, :], ident[:, :], start=True, stop=True)

            for j in range(ET):
                edges(j)
                if j in (TURN_AT, TURN_AT + 1):
                    turn("ln0", j - TURN_AT)
                if FOLD_AT <= j < FOLD_AT + 2 * KT:
                    fold((j - FOLD_AT) // KT, (j - FOLD_AT) % KT)
                if j in (QUERY_AT, QUERY_AT + 1):
                    query(j - QUERY_AT)
                if j in (KEY_AT, KEY_AT + 1):
                    key(j - KEY_AT)
                if VALUE_AT <= j < VALUE_AT + NT * KT:
                    tokens_out("v_done", (4, 5), V0, (j - VALUE_AT) // KT, ((j - VALUE_AT) % KT,))
                if GNN_AT <= j < GNN_AT + KT:
                    tokens_out("g_done", (6, 7), GNN0, 0, (j - GNN_AT,))
            tokens_out("g_done", (6, 7), GNN0, 1)

            pe.wait_ge(sem("k_lo"), nth("k_lo", 1))
            pe.wait_ge(sem("q_lo"), nth("q_lo", 1))
            pe.wait_ge(sem("v_lo"), nth("v_lo", 2))
            pe.wait_ge(sem("ones_made"), 1)
            pe.wait_ge(sem("value_ones"), NT)
            for m in range(2):
                for tt in range(NT):
                    a = slice(tt * T + m * P, tt * T + (m + 1) * P)
                    b = slice((2 * tt + m) * VW, (2 * tt + m + 1) * VW)
                    ins = mm3(bank[2 + m][:, 0:VW], kf_hi[:, a], kf_lo[:, a], v_hi[:, b], v_lo[:, b],
                              tt == 0, tt == NT - 1)
            ins.then_inc(sem("kv_done"), 1)

            def aggregate(tag, part, tt, hs=(0, 1)):
                for h in hs:
                    a = slice(part * T + tt * P, part * T + (tt + 1) * P)
                    b = slice(h * D, (h + 1) * D)
                    ins = mm3(bank[tt][:, :], adj_hi[:, h, a], adj_lo[:, h, a], pr_hi[:, b], pr_lo[:, b],
                              h == 0, h == 1)
                    if h == 1:
                        ins.then_inc(sem(tag), 1)

            pe.wait_ge(sem("pr_lo"), nth("pr_lo", 2))
            for tt in range(NT):
                for h in range(2):
                    a = slice(tt * P, (tt + 1) * P)
                    pe.matmul(bank[7][:, 2 * tt:2 * tt + 2], adj_hi[:, h, a], ones[:, 0:2], start=(h == 0), stop=False)
                    pe.matmul(bank[7][:, 2 * tt:2 * tt + 2], adj_lo[:, h, a], ones[:, 0:2], start=False, stop=(h == 1))
                aggregate("agg0_done", 0, tt)

            pe.wait_ge(sem("kv_lo"), nth("kv_lo", 1))
            for tt in range(NT):
                for m in range(2):
                    a = slice(m * T + tt * P, m * T + (tt + 1) * P)
                    ins = mm3(bank[3][:, 64 + 8 * tt + 4 * m:68 + 8 * tt + 4 * m], qf_hi[:, a], qf_lo[:, a],
                              ks_hi[:, m, :], ks_lo[:, m, :], True, True)
            ins.then_inc(sem("norms_done"), 1)
            for tt in range(NT):
                for m in range(2):
                    a = slice(m * T + tt * P, m * T + (tt + 1) * P)
                    b = slice(m * 256, (m + 1) * 256)
                    ins = mm3(bank[4 + tt][:, b], qf_hi[:, a], qf_lo[:, a], xT_hi[:, b], xT_lo[:, b], True, True)
                ins.then_inc(sem("z_done"), 1)
            weights_ready(pe, OUT0)
            for tt in range(NT):
                turn("z", tt)
            for tt in range(NT):
                pe.wait_ge(sem("z_hi"), nth("z_hi", tt + 1))
                grouped(bank[2 + tt][:, :], token_parts(v_hi, v_lo, OUT0, tt), "a", "z_lo", tt + 1)\
                    .then_inc(sem("o_done"), 1)

            def spread(tag, g, j, m0, lap=None):
                if g:
                    pe.wait_ge(sem(f"{tag}_scaled"), at(nth(f"{tag}_scaled", 2 * g - 1 + j), lap, BODY))
                for mm in range(2):
                    m = m0 + 2 * j + mm
                    units = sel[:, m * P:(m + 1) * P] if lap is None else sel[:, bass.ds(lap * (2 * D) + m * P, P)]
                    ins = pe.matmul(bank[6 + j][:, mm * T:(mm + 1) * T], units, combT16[:, :], start=True, stop=True)
                ins.then_inc(sem(f"{tag}_spread"), 1)

            def up_part(tag, i, g, j, mm):
                for kt in range(KT):
                    a = slice(kt * D + (2 * j + mm) * P, kt * D + (2 * j + mm + 1) * P)
                    b = slice(kt * T, (kt + 1) * T)
                    ins = mm3(bank[2 + j][:, mm * T:(mm + 1) * T], w_hi[i % SLOTS][:, a],
                              w_lo[i % SLOTS][:, a], xT_hi[:, b], xT_lo[:, b], kt == 0, kt == KT - 1)
                if mm == 1:
                    ins.then_inc(sem(f"{tag}_up"), 1)

            def up_half(tag, i, g, j, lap=None):
                weights_ready(pe, i, lap)
                if g:
                    pe.wait_ge(sem(f"{tag}_act"), at(nth(f"{tag}_act", 4 * g - 2 + 2 * j), lap, 2 * BODY))
                for mm in range(2):
                    up_part(tag, i, g, j, mm)

            def up(tag, i, routed, g, m0, lap=None):
                for j in range(2):
                    up_half(tag, i, g, j, lap)
                    if routed:
                        spread(tag, g, j, m0, lap)

            def down_part(i, g, tt, m, first, last=False):
                a = slice((g % 2) * 1024 + m * T + tt * P, (g % 2) * 1024 + m * T + (tt + 1) * P)
                b = slice(m * D, (m + 1) * D)
                return mm3(bank[tt][:, :], wide_hi[:, a], wide_lo[:, a], w_hi[i % SLOTS][:, b],
                           w_lo[i % SLOTS][:, b], first and m == 0, last)

            def down(tag, i, g, lap=None):
                weights_ready(pe, i, lap)
                for j in range(2):
                    pe.wait_ge(sem(f"{tag}_act_lo"), at(nth(f"{tag}_act_lo", 2 * g + j + 1), lap, BODY))
                    for m in (2 * j, 2 * j + 1):
                        for tt in range(NT):
                            ins = down_part(i, g, tt, m, g == 0)
                    ins.then_inc(sem(f"{tag}_down"), 1)

            def last_down(tag, i, g, b2_in, experts):
                weights_ready(pe, i)
                pe.wait_ge(sem(b2_in), 16)
                pe.wait_ge(sem(f"comb{tag[-1]}_T"), 1)

                def biases(tt):
                    pe.matmul(bank[tt][:, :], combT[0:experts, tt * P:(tt + 1) * P], b2s[0:experts, :],
                              start=(g == 0), stop=False)

                biases(0)
                for tt in range(NT):
                    for m in range(KT):
                        if tt == 0 and m % 2 == 0:
                            if m and g == 0:
                                biases(1)
                            pe.wait_ge(sem(f"{tag}_act_lo"), nth(f"{tag}_act_lo", 2 * g + m // 2 + 1))
                        ins = down_part(i, g, tt, m, False, m == KT - 1)
                    ins.then_inc(sem(f"{tag}_out"), 1)
                    if tt == 0 and g:
                        biases(1)

            pe.wait_ge(sem("mixed0"), NT)

            def logits0(tt):
                pe.wait_ge(sem("ln1_full"), tt + 1)
                for kt in range(KT):
                    a = slice(kt * T + tt * P, kt * T + (tt + 1) * P)
                    b = slice(SM_WG + kt * E0, SM_WG + (kt + 1) * E0)
                    ins = pe.matmul(bank[4][:, 8 + tt * 8:16 + tt * 8], fb[:, a], smr[:, b], start=(kt == 0),
                                    stop=(kt == KT - 1))
                return ins

            keep_clock(9, 0, adj_hi[:, 0, :])
            for tt in range(NT):
                turn("ln1", tt)
            keep_clock(3, 0, adj_hi[:, 0, :])
            logits0(0)
            logits0(1).then_inc(sem("lg0_done"), 1)
            weights_ready(pe, UP0)
            pe.wait_ge(sem("x1"), 2)
            pe.wait_ge(sem("ln1_hi"), nth("ln1_hi", 2))
            first = [(w_hi[UP0 % SLOTS][:, kt * D:kt * D + P], w_lo[UP0 % SLOTS][:, kt * D:kt * D + P],
                      xT_hi[:, kt * T:(kt + 1) * T], xT_lo[:, kt * T:(kt + 1) * T]) for kt in range(KT)]
            early(bank[2][:, 0:T], first, "b")
            after_low(bank[2][:, 0:T], first, "b", "ln1_lo", 2)
            up_part("ffn0", UP0, 0, 0, 1)
            for tt in range(NT):
                pe.wait_ge(sem("comb0"), tt + 1)
                ins = pe.transpose(bank[5][:, tt * P:(tt + 1) * P], comb[:, tt, :], ident[:, :])
            ins.then_inc(sem("comb0_turned"), 1)
            up_part("ffn0", UP0, 0, 1, 0)
            pe.wait_ge(sem("comb0_16"), 1)
            pe.wait_ge(sem("sel_made"), 1)
            spread("ffn0", 0, 0, 0)
            up_part("ffn0", UP0, 0, 1, 1)
            spread("ffn0", 0, 1, 0)
            last_down("ffn0", DOWN0, 0, "b2_0_in", E0)

            pe.wait_ge(sem("x2"), 1)
            weights_ready(pe, GNN1)
            first = token_parts(xT_hi, xT_lo, GNN1, 0)
            turn("ln2", 0)
            pe.wait_ge(sem("ln2_hi"), nth("ln2_hi", 1))
            early(bank[0][:, :], first, "a")
            turn("ln2", 1)
            after_low(bank[0][:, :], first, "a", "ln2_lo", 1).then_inc(sem("s_done"), 1)
            pe.wait_ge(sem("ln2_hi"), nth("ln2_hi", 2))
            pe.wait_ge(sem("x2"), 2)
            grouped(bank[1][:, :], token_parts(xT_hi, xT_lo, GNN1, 1), "a", "ln2_lo", 2).then_inc(sem("s_done"), 1)

            def turned_out(tag, banks, i):
                weights_ready(pe, i)
                for m in range(KT):
                    for kt in range(KT):
                        a = slice(kt * D + m * P, kt * D + (m + 1) * P)
                        b = slice(kt * T, (kt + 1) * T)
                        ins = mm3(bank[banks[m // 2]][:, (m % 2) * T:(m % 2 + 1) * T], w_hi[i % SLOTS][:, a],
                                  w_lo[i % SLOTS][:, a], xT_hi[:, b], xT_lo[:, b], kt == 0, kt == KT - 1)
                    if m % 2 == 1:
                        ins.then_inc(sem(tag), 1)

            turned_out("k1_done", (2, 3), K1)
            turned_out("q1_done", (4, 5), Q1)

            def features(n, name, b):
                pe.wait_ge(sem(f"{name}_lo"), nth(f"{name}_lo", 2))
                for tt in range(NT):
                    for kt in range(KT):
                        a = slice(n * 1024 + kt * T + tt * P, n * 1024 + kt * T + (tt + 1) * P)
                        f = slice(ST_FEAT + kt * M1, ST_FEAT + (kt + 1) * M1)
                        ins = mm3(bank[b][:, tt * M1:(tt + 1) * M1], wide_hi[:, a], wide_lo[:, a], st_hi[:, f],
                                  st_lo[:, f], kt == 0, kt == KT - 1)
                ins.then_inc(sem(f"{name}_feat"), 1)

            def norms(name, sq, c):
                pe.wait_ge(sem(f"{name}_sum"), 2)
                for tt in range(NT):
                    ins = pe.matmul(bank[7][:, c + tt:c + tt + 1], sq[:, tt * P:(tt + 1) * P], ones32[:, 0:1],
                                    start=True, stop=True)
                ins.then_inc(sem(f"{name}_norm"), 1)

            pe.wait_ge(sem("raw_used"), RAW_STATIC - UNSPLIT + 1)
            features(0, "k1", 6)
            norms("k1", flat(xn), 0)
            pe.wait_ge(sem("q1_f"), nth("q1_f", 4))
            for tt in range(NT):
                tokens_out("v1_done", (4, 5), V1, tt)
            features(1, "q1", 2)
            pe.wait_ge(sem("k1_nb"), 1)
            norms("q1", fa, 8)
            pe.wait_ge(sem("sup_lo"), nth("sup_lo", 2))
            aggregate("agg1_done", 1, 1, (0,))
            pe.wait_ge(sem("q1_nb"), 1)
            pe.wait_ge(sem("kp_lo"), nth("kp_lo", 1))
            for tt in range(NT):
                a = slice(tt * M1, (tt + 1) * M1)
                pe.matmul(bank[7][:, 0:M1], ones[:, :], kf_hi[:, a], start=(tt == 0), stop=False)
                ins = pe.matmul(bank[7][:, 0:M1], ones[:, :], kf_lo[:, a], start=False, stop=(tt == NT - 1))
            ins.then_inc(sem("ksum1_done"), 1)
            pe.wait_ge(sem("v1_lo"), nth("v1_lo", 2))
            for m in range(2):
                if m == 1:
                    for tt in range(NT):
                        pe.wait_ge(sem("qp"), tt + 1)
                        for c in range(2):
                            ins = pe.transpose(bank[3][:, c * T + tt * P:c * T + (tt + 1) * P],
                                               fb[:, tt * M1 + c * P:tt * M1 + (c + 1) * P], ident[:, :])
                    ins.then_inc(sem("qp_turned"), 1)
                for tt in range(NT):
                    a = slice(tt * M1 + m * P, tt * M1 + (m + 1) * P)
                    b = slice(tt * D, (tt + 1) * D)
                    ins = mm3(bank[(6, 2)[m]][:, :], kf_hi[:, a], kf_lo[:, a], v_hi[:, b], v_lo[:, b], tt == 0,
                              tt == NT - 1)
                ins.then_inc(sem("kv1_done"), 1)
            aggregate("agg1_done", 1, 0)
            pe.wait_ge(sem("qp_lo"), nth("qp_lo", 1))
            pe.wait_ge(sem("kv1_lo"), nth("kv1_lo", 2))
            for kt in range(KT):
                for m in range(2):
                    a = slice(m * D + kt * P, m * D + (kt + 1) * P)
                    b = slice(m * T, (m + 1) * T)
                    ins = mm3(bank[4 + kt // 2][:, (kt % 2) * T:(kt % 2 + 1) * T], xT_hi[:, a], xT_lo[:, a],
                              qf_hi[:, b], qf_lo[:, b], m == 0, m == 1)
                if kt % 2 == 1:
                    ins.then_inc(sem("y1_turned"), 1)
            aggregate("agg1_done", 1, 1, (1,))
            weights_ready(pe, PROJ1)
            pe.wait_ge(sem("y1_hi"), nth("y1_hi", 2))
            for tt in range(NT):
                grouped(bank[2 + tt][:, :], token_parts(v_hi, v_lo, PROJ1, tt), "a", "y1_lo", 2).then_inc(sem("p1_done"), 1)

            def router_and_f(tag, b, t0, t1, split, n):
                pe.wait_ge(sem(f"{split}_hi"), nth(f"{split}_hi", n))
                parts = [(st_hi[:, ST_RF + kt * P:ST_RF + (kt + 1) * P], st_lo[:, ST_RF + kt * P:ST_RF + (kt + 1) * P],
                          xT_hi[:, kt * T + t0:kt * T + t1], xT_lo[:, kt * T + t0:kt * T + t1]) for kt in range(KT)]
                grouped(bank[b][:, t0:t1], parts, "b", f"{split}_lo", n).then_inc(sem(tag), 1)

            for tt in range(NT):
                turn("ln4", tt, True)
                keep_clock((10, 8)[tt], 0, st_hi[:, :])
            router_and_f("r_done", 4, 0, T, "ln4", 2)
            weights_ready(pe, FFN1)
            up_part("ffn1", FFN1, 0, 0, 0)
            pe.wait_ge(sem("codebook_in"), 16)
            pe.wait_ge(sem("rT"), 1)
            for tt in range(NT):
                ins = pe.matmul(bank[5][:, tt * E1:(tt + 1) * E1], rT[:, tt * P:(tt + 1) * P], cbs[:, :], start=True,
                                stop=True)
            ins.then_inc(sem("lg1_done"), 1)
            up_part("ffn1", FFN1, 0, 0, 1)
            up_half("ffn1", FFN1, 0, 1)
            up("ffn1", FFN1 + 1, False, 1, 0)
            for tt in range(NT):
                pe.wait_ge(sem("comb1"), tt + 1)
                ins = pe.transpose(bank[4][:, tt * P:(tt + 1) * P], comb[:, tt, :], ident[:, :])
            ins.then_inc(sem("comb1_turned"), 1)
            down("ffn1", FFN1 + 2, 0)
            pe.wait_ge(sem("comb1_16"), 1)
            with pe.Fori(0, LAPS) as lap:
                for n in range(STEADY, STEADY + BODY):
                    kind, g = FFN1_ORDER[n]
                    if kind == "up":
                        up("ffn1", FFN1 + n, True, g, 4 * (g - SHARED_GROUPS), lap)
                    else:
                        down("ffn1", FFN1 + n, g, lap)
            last_down("ffn1", BLOCKS - 1, GROUPS - 1, "b2_1_in", E1)
            turn("ln5", 0, True)
            keep_clock(10, 0, st_hi[:, :])
            turn("ln5", 1, True)
            for tt in range(NT):
                router_and_f("f1_done", 2 + tt, tt * P, (tt + 1) * P, "ln5", tt + 1)
            pe.wait_ge(sem("wf2_in"), 16)
            for tt in range(NT):
                pe.wait_ge(sem("f1_silu"), tt + 1)
                pe.matmul(bank[6 + tt][:, :], fb[64:P, tt * P:(tt + 1) * P], b2s[64:P, :], start=True,
                          stop=True).then_inc(sem("f2_done"), 1)

        @block.scalar
        def _(act):
            act.dma_start(edge_i[:, 1, :], dst).then_inc(sem("dst_in"), 16)
            act.dma_start(ewf[:, :], ew).then_inc(sem("ew_in"), 16)
            act.wait_ge(sem("mhalf_made"), 1)
            act.activation(warm[:, :], mhalf[:, :], ACT.Exp)

            def high_block(i, lap=None):
                r = raw_index(i)
                act.wait_ge(sem(f"raw_in{r % RAWS}"), at(nth(f"raw_in{r % RAWS}", 16 * (r // RAWS + 1)), lap, 16))
                if i >= SLOTS:
                    event, n = last_use(i - SLOTS)
                    act.wait_ge(sem(event), at(nth(event, n), lap, BODY))
                act.activation(w_hi[i % SLOTS][:, :], raw[:, r % RAWS, :], ACT.Copy).then_inc(sem("hi_cut"), 1)

            def high_static():
                r = RAW_STATIC
                act.wait_ge(sem(f"raw_in{r % RAWS}"), nth(f"raw_in{r % RAWS}", 16 * (r // RAWS + 1)))
                act.activation(st_hi[:, :], raw[:, r % RAWS, 0:STATIC], ACT.Copy).then_inc(sem("static_hi_cut"), 1)

            def high(tag, o, i, wait, n, scale=1.0):
                act.wait_ge(sem(wait), nth(wait, n))
                act.activation(o, i, ACT.Copy, scale=scale).then_inc(sem(f"{tag}_hi"), 1)

            def high_turned(tag, o, tt):
                high(tag, tile_of(o, tt), tile_of_bank(6 + tt), f"{tag}_turned", tt + 1)

            def affine_high(tag, g, b, tt):
                act.wait_ge(sem(f"{tag}_turned"), nth(f"{tag}_turned", tt + 1))
                for kt in range(KT // 2, KT):
                    act.activation(fb[:, kt * T + tt * P:kt * T + (tt + 1) * P],
                                   bank[4 + tt][:, kt * P:(kt + 1) * P], ACT.Identity, scale=colsb[:, g + kt:g + kt + 1],
                                   bias=colsb[:, b + kt:b + kt + 1]).then_inc(sem(f"{tag}_affine2"), 1)
                act.wait_ge(sem(f"{tag}_affine2"), nth(f"{tag}_affine2", 2 * tt + 2))
                high(tag, tile_of(xT_hi, tt), tile_of(fb, tt), f"{tag}_affine", 2 * tt + 2)

            def high_fold(n, h):
                high("fold", folded(wide_hi, n, h), bank[2 + 2 * n + h][:, :].rearrange("p (m c) -> p m c", m=2),
                     "fold_done", 2 * n + h + 1)

            def elu_exp(name, i, o):
                act.wait_ge(sem(f"{name}_min"), nth(f"{name}_min", 1))
                act.activation(o, i, ACT.Exp).then_inc(sem(f"{name}_exp"), 1)

            act.wait_ge(sem("ew_cut"), 1)
            for j in range(ET):
                act.wait_ge(sem("hot_src"), j + 1)
                hot = hots[j % HOTS]
                act.activation(hot[:, 2 * T:3 * T], f32(hot[:, T:2 * T]), ACT.Copy,
                               scale=f32(ew_hi[:, j:j + 1])).then_inc(sem("hot_w"), 1)
                if j in (4, 5):
                    high_turned("ln0", xT_hi, j - 4)
                if j in (8, 10, 12, 14):
                    high_fold((j - 8) // 4, (j - 8) // 2 % 2)
                if j in (9, 15, 21, 26):
                    high_block((9, 15, 21, 26).index(j))
                if j == 17:
                    elu_exp("q", fa[:, 0:512], fa[:, 512:1024])
                if j == 19:
                    high("q", qf_hi[:, :], fb[:, 0:512], "q_f", 1)
                if j == 20:
                    elu_exp("k", fb[:, 512:1024], xn[:, 0, :])
                if j == 22:
                    high("k", kf_hi[:, :], xn[:, 1, :], "k_f", 1)
                if j in (24, 28):
                    tt = (j - 24) // 4
                    high("v", values(v_hi, tt), halves(bank[4 + tt]), "v_done", tt + 1)
                if j == 30:
                    high_block(4)
            for h in range(2):
                high("adj", adj_hi[:, h, :], bank[h][:, :], "hot_used", ET)
            for tt in range(NT):
                high("pr", pr_hi[:, tt * D:(tt + 1) * D], bank[6 + tt][:, :], "g_done", tt + 1)
            high("kv", xT_hi[:, 0:512], fb[:, 0:512], "kv_f", 2)
            high_block(5)
            high_static()
            for tt in range(NT):
                high_turned("z", v_hi, tt)
            high_block(6)
            for tt in range(NT):
                act.wait_ge(sem("ln1_turned"), nth("ln1_turned", tt + 1))
                act.activation(tile_of(fb, tt), tile_of_bank(6 + tt), ACT.Copy).then_inc(sem("ln1_full"), 1)
                high_turned("ln1", xT_hi, tt)

            for tt in range(NT):
                act.wait_ge(sem("negmax0"), tt + 1)
                act.activation(pe_[:, tt, 0:E0], lg[:, tt, 0:E0], ACT.Exp, bias=wk[:, tt, 0:1],
                               accum_out=wk[:, tt, 1:2]).then_inc(sem("sum0"), 1)

            def hidden(tag, func, g, col, lap=None):
                for j in range(2):
                    act.wait_ge(sem(f"{tag}_up"), at(nth(f"{tag}_up", 2 * g + j + 1), lap, BODY))
                    if g:
                        act.wait_ge(sem(f"{tag}_scaled"), at(nth(f"{tag}_scaled", 2 * g - 1 + j), lap, BODY))
                    for mm in range(2):
                        c = col + 4 * g + 2 * j + mm
                        bias = colsb[:, c:c + 1] if lap is None else colsb[:, bass.ds(lap * 8 + c, 1)]
                        act.activation(fa[:, j * 512 + mm * T:j * 512 + (mm + 1) * T],
                                       bank[2 + j][:, mm * T:(mm + 1) * T], func,
                                       bias=bias).then_inc(sem(f"{tag}_act"), 1)

            act.wait_ge(sem("cols_in"), 16)
            hidden("ffn0", ACT.Relu, 0, COL_B1_0)
            for tt in range(NT):
                high_turned("ln2", xT_hi, tt)
            high_block(7)
            high_block(8)
            for tt in range(NT):
                high("sup", pr_hi[:, tt * D:(tt + 1) * D], bank[tt][:, :], "s_done", tt + 1)
            for name, n, f, sq in (("k1", 0, fa, flat(xn)), ("q1", 1, fb, fa)):
                for h in range(2):
                    a = slice(h * 512, (h + 1) * 512)
                    high(name, wide_hi[:, n * 1024 + h * 512:n * 1024 + (h + 1) * 512], f[:, a], f"{name}_f",
                         2 * h + 2)
                    if n:
                        act.wait_ge(sem("k1_sq"), 2)
                        act.wait_ge(sem("k1_lo"), nth("k1_lo", 2))
                    act.activation(sq[:, a], f[:, a], ACT.Square).then_inc(sem(f"{name}_sq"), 1)
                high_block(9 + n)
            act.wait_ge(sem("k1_nb"), 1)
            act.wait_ge(sem("q1_lo"), nth("q1_lo", 2))
            act.wait_ge(sem("q1_sq"), 2)
            for tt in range(NT):
                act.wait_ge(sem("k1_feat"), 1)
                act.activation(fb[:, 512 + tt * M1:512 + (tt + 1) * M1], bank[6][:, tt * M1:(tt + 1) * M1], ACT.Exp,
                               bias=nrm[:, 0, tt:tt + 1]).then_inc(sem("kp"), 1)
            high("kp", kf_hi[:, :], fb[:, 512:1024], "kp", 2, M1 ** -0.5)
            high_block(11)
            for tt in range(NT):
                high("v1", v_hi[:, tt * D:(tt + 1) * D], xn[:, tt, :], "v1_f", tt + 1)
            act.wait_ge(sem("q1_nb"), 1)
            act.wait_ge(sem("q1_feat"), 1)
            for tt in range(NT):
                act.activation(fb[:, tt * M1:(tt + 1) * M1], bank[2][:, tt * M1:(tt + 1) * M1], ACT.Exp,
                               bias=nrm[:, 1, tt:tt + 1]).then_inc(sem("qp"), 1)
            high_block(12)
            high("qp", qf_hi[:, :], bank[3][:, :], "qp_turned", 1, M1 ** -0.5)
            for m in range(2):
                high("kv1", xT_hi[:, m * D:(m + 1) * D], bank[(6, 2)[m]][:, :], "kv1_done", m + 1)
            for h in range(2):
                high("y1", v_hi[:, h * 512:(h + 1) * 512], bank[4 + h][:, :], "y1_turned", h + 1)
            high_block(13)
            for tt in range(NT):
                affine_high("ln4", COL_LN_G, COL_LN_B, tt)
            act.wait_ge(sem("r_done"), nth("r_done", 1))
            act.activation(rT[:, :], bank[4][0:64, 0:T], ACT.Copy).then_inc(sem("rT"), 1)
            for tt in range(NT):
                act.wait_ge(sem("negmax1"), tt + 1)
                act.activation(wk[:, tt, 2:4], top[:, tt, 0:2], ACT.Exp, bias=wk[:, tt, 0:1],
                               accum_out=wk[:, tt, 1:2]).then_inc(sem("sum1"), 1)
            act.wait_ge(sem("base2"), 2)

            def ffn1_step(n, lap=None, cut=True):
                kind, g = FFN1_ORDER[n]
                if kind == "up":
                    hidden("ffn1", ACT.Silu, g, COL_B1, lap)
                if cut:
                    high_block(FFN1 + n + SLOTS, lap)

            for n in range(STEADY):
                ffn1_step(n)
            with act.Fori(0, LAPS - 1) as lap:
                for n in range(STEADY, STEADY + BODY):
                    ffn1_step(n, lap)
            for n in range(STEADY + (LAPS - 1) * BODY, len(FFN1_ORDER)):
                ffn1_step(n, None, FFN1 + n + SLOTS < BLOCKS)
            for tt in range(NT):
                affine_high("ln5", COL_FF_G, COL_FF_B, tt)
            for tt in range(NT):
                a = slice(tt * P, (tt + 1) * P)
                act.wait_ge(sem("f1_done"), tt + 1)
                act.activation(fb[64:P, a], bank[2 + tt][64:P, a], ACT.Silu,
                               bias=colsb[64:P, COL_BF1:COL_BF1 + 1]).then_inc(sem("f1_silu"), 1)

        @block.vector
        def _(dve):
            def stats(tag, tile, tt, event, n):
                dve.wait_ge(sem(event), nth(event, n))
                dve.bn_stats(st[:, tt, :], tile).then_inc(sem(f"{tag}_bn"), 1)
                dve.wait_ge(sem(f"{tag}_bn"), nth(f"{tag}_bn", tt + 1))
                dve.bn_aggr(mv[:, tt, :], st[:, tt, :]).then_inc(sem(f"{tag}_mv"), 1)
                dve.wait_ge(sem(f"{tag}_mv"), nth(f"{tag}_mv", tt + 1))
                if tag == "ln3":
                    dve.tensor_scalar(ve2[:, tt:tt + 1], mv[:, tt, 1:2], 1.0 + LN_EPS, LN_EPS * LN_EPS, ALU.mult,
                                      ALU.add).then_inc(sem("normed_var"), 1)
                dve.tensor_scalar(ve[:, tt:tt + 1], mv[:, tt, 1:2], LN_EPS, None, ALU.add)\
                   .then_inc(sem(f"{tag}_var"), 1)

            def normalize(tag, tile, tt, out):
                dve.wait_ge(sem(f"{tag}_rstd"), nth(f"{tag}_rstd", tt + 1))
                dve.tensor_scalar(out, tile, mv[:, tt, 0:1], rstd[:, tt:tt + 1], ALU.subtract,
                                  ALU.mult).then_inc(sem(f"{tag}_xn"), 1)

            def low(tag, o, i, hi, n=1):
                dve.wait_ge(sem(f"{tag}_hi"), nth(f"{tag}_hi", n))
                dve.tensor_tensor(o, i, f32(hi), ALU.subtract).then_inc(sem(f"{tag}_lo"), 1)

            def low_turned(tag, lo, hi, tt):
                low(tag, tile_of(lo, tt), tile_of_bank(6 + tt), tile_of(hi, tt), tt + 1)

            x_tiles = [xs[:, tt, :] for tt in range(NT)]
            xn_tiles = [xn[:, tt, :] for tt in range(NT)]
            fa_tiles = [fa[:, tt * D:(tt + 1) * D] for tt in range(NT)]

            dve.memset(ones32[:, :], 1.0).then_inc(sem("ones32_made"), 1)
            dve.wait_ge(sem("ones32_made"), 1)
            dve.tensor_copy(ones[:, :], ones32[:, 0:1].to_broadcast([P, P])).then_inc(sem("ones_made"), 1)
            for tt in range(NT):
                dve.tensor_copy(values(v_hi, tt, D // 2, VW), ones32[:, 0:1].unsqueeze(2).to_broadcast([P, 2, 2]))
                dve.tensor_scalar(values(v_lo, tt, D // 2, VW), ones32[:, 0:1].unsqueeze(2).to_broadcast([P, 2, 2]),
                                  0.0, None, ALU.mult).then_inc(sem("value_ones"), 1)
            for q in range(4):
                dve.memset(pcol[32 * q:32 * q + 32, 1:2], float(q))
            dve.memset(pcol[0:64, 3:4], 1.0)
            dve.memset(pcol[64:P, 3:4], 1.0 / LO_SCALE).then_inc(sem("pcol_made"), 1)
            dve.wait_ge(sem("src_in"), 16)
            dve.wait_ge(sem("dst_in"), 16)
            dve.tensor_copy(edge_f[:, :, :], edge_i[:, :, :]).then_inc(sem("edges"), 1)
            dve.wait_ge(sem("ew_in"), 16)
            dve.tensor_copy(ew_hi[:, :], ewf[:, :]).then_inc(sem("ew_cut"), 1)
            dve.wait_ge(sem("ew_cut"), 1)
            dve.tensor_tensor(ew_lo[:, :], ewf[:, :], f32(ew_hi[:, :]), ALU.subtract).then_inc(sem("ew_cut"), 1)
            dve.wait_ge(sem("edges"), 1)
            dve.wait_ge(sem("ew_cut"), 2)
            dve.wait_ge(sem("iota_made"), 1)

            def low_fold(n, h):
                low("fold", folded(wide_lo, n, h), bank[2 + 2 * n + h][:, :].rearrange("p (m c) -> p m c", m=2),
                    folded(wide_hi, n, h), 2 * n + h + 1)

            for j in range(ET):
                if j >= HOTS:
                    dve.wait_ge(sem("hot_used"), j - HOTS + 1)
                hot = hots[j % HOTS]
                s, d = edge_f[:, 0, j:j + 1], edge_f[:, 1, j:j + 1]
                dve.tensor_scalar(hot[:, T:2 * T], iota[:, :], s, None, ALU.is_equal).then_inc(sem("hot_src"), 1)
                dve.tensor_scalar(hot[:, 0:T], iota[:, :], d, None, ALU.is_equal)
                dve.tensor_scalar(hot[:, 3 * T:4 * T], iota[:, :], s, ew_lo[:, j:j + 1], ALU.is_equal,
                                  ALU.mult).then_inc(sem("hot"), 1)
                if j in (0, 1):
                    stats("ln0", x_tiles[j], j, f"x{j}_in", 16)
                if j in (1, 2):
                    normalize("ln0", x_tiles[j - 1], j - 1, xn_tiles[j - 1])
                if j in (5, 6):
                    low_turned("ln0", xT_lo, xT_hi, j - 5)
                if j in (8, 10, 12, 14):
                    low_fold((j - 8) // 4, (j - 8) // 2 % 2)
                if j == 16:
                    dve.wait_ge(sem("q_done"), nth("q_done", 1))
                    dve.tensor_scalar(fa[:, 0:512], bank[2][:, :], 0.0, None, ALU.min).then_inc(sem("q_min"), 1)
                if j == 18:
                    dve.wait_ge(sem("q_exp"), 1)
                    dve.scalar_tensor_tensor(out=fb[:, 0:512], in0=bank[2][:, :], scalar=0.0, in1=fa[:, 512:1024],
                                             op0=ALU.max, op1=ALU.add).then_inc(sem("q_f"), 1)
                if j == 19:
                    dve.wait_ge(sem("k_done"), nth("k_done", 1))
                    dve.tensor_scalar(fb[:, 512:1024], bank[3][:, :], 0.0, None, ALU.min).then_inc(sem("k_min"), 1)
                if j == 20:
                    low("q", qf_lo[:, :], fb[:, 0:512], qf_hi[:, :])
                if j == 21:
                    dve.wait_ge(sem("k_exp"), 1)
                    dve.scalar_tensor_tensor(out=xn[:, 1, :], in0=bank[3][:, :], scalar=0.0, in1=xn[:, 0, :],
                                             op0=ALU.max, op1=ALU.add).then_inc(sem("k_f"), 1)
                if j == 23:
                    low("k", kf_lo[:, :], xn[:, 1, :], kf_hi[:, :])
                if j in (25, 29):
                    tt = (j - 25) // 4
                    low("v", values(v_lo, tt), halves(bank[4 + tt]), values(v_hi, tt), tt + 1)
                if j == 26:
                    dve.wait_ge(sem("heads_made"), 1)
                    dve.wait_ge(sem("pcol_made"), 1)
                    dve.tensor_scalar(blockmask[:, :], blockmask[:, :], pcol[:, 1:2], None,
                                      ALU.is_equal).then_inc(sem("blockmask"), 1)
                if j == 30:
                    dve.wait_ge(sem("pidx_made"), 1)
                    dve.tensor_copy(pcol[0:64, 2:3], pcol[0:64, 0:1])
                    dve.wait_ge(sem("experts_made"), 1)
                    dve.tensor_scalar(pcol[64:P, 2:3], pcol[64:P, 0:1], -64.0, None, ALU.add).then_inc(sem("pmod"), 1)
                    dve.wait_ge(sem("pmod"), 1)
                    dve.tensor_scalar(sel[:, :], sel[:, :], pcol[:, 2:3], pcol[:, 3:4], ALU.is_equal,
                                      ALU.mult).then_inc(sem("sel_made"), 1)
            for h in range(2):
                low("adj", adj_lo[:, h, :], bank[h][:, :], adj_hi[:, h, :], h + 1)
            for tt in range(NT):
                low("pr", pr_lo[:, tt * D:(tt + 1) * D], bank[6 + tt][:, :], pr_hi[:, tt * D:(tt + 1) * D], tt + 1)
            dve.wait_ge(sem("kv_done"), nth("kv_done", 1))
            dve.wait_ge(sem("blockmask"), 1)
            dve.wait_ge(sem("q_lo"), nth("q_lo", 1))
            for m in range(2):
                dve.tensor_tensor(fb[:, m * 256:(m + 1) * 256], bank[2 + m][:, 0:256], blockmask[:, :],
                                  ALU.mult).then_inc(sem("kv_f"), 1)
            for m in range(2):
                dve.tensor_tensor(ksb[:, m, :], blockmask[:, 0:256:HD], bank[2 + m][:, 256:257].to_broadcast([P, 4]),
                                  ALU.mult).then_inc(sem("ksb"), 1)
            dve.wait_ge(sem("ksb"), 2)
            dve.tensor_copy(ks_hi[:, :, :], ksb[:, :, :]).then_inc(sem("ks_hi"), 1)
            dve.wait_ge(sem("ks_hi"), nth("ks_hi", 1))
            dve.tensor_tensor(ks_lo[:, :, :], ksb[:, :, :], f32(ks_hi[:, :, :]), ALU.subtract)
            low("kv", xT_lo[:, 0:512], fb[:, 0:512], xT_hi[:, 0:512])
            dve.wait_ge(sem("k_lo"), nth("k_lo", 1))
            dve.wait_ge(sem("agg0_done"), nth("agg0_done", 2))
            dve.tensor_copy(deg[:, :], bank[7][:, 0:4:2]).then_inc(sem("deg"), 1)
            dve.wait_ge(sem("deg"), 1)
            dve.reciprocal(degr[:, :], deg[:, :]).then_inc(sem("degr"), 1)
            dve.wait_ge(sem("norms_done"), 1)
            dve.tensor_scalar(nrm[:, :, :], bank[3][:, 64:80].rearrange("p (t h) -> p t h", t=NT), NORM_EPS, None,
                              ALU.add).then_inc(sem("nrm"), 1)
            dve.wait_ge(sem("nrm"), 1)
            dve.reciprocal(rden[:, :, :], nrm[:, :, :]).then_inc(sem("rden"), 1)
            dve.wait_ge(sem("rden"), 1)
            for tt in range(NT):
                dve.wait_ge(sem("z_done"), nth("z_done", tt + 1))
                dve.tensor_tensor(xn[:, tt, :].rearrange("p (h f) -> p h f", h=HEADS),
                                  bank[4 + tt][:, :].rearrange("p (h f) -> p h f", h=HEADS),
                                  rden[:, tt, :].unsqueeze(2).to_broadcast([P, HEADS, HD]),
                                  ALU.mult).then_inc(sem("z_xn"), 1)
            for tt in range(NT):
                low_turned("z", v_lo, v_hi, tt)
            dve.wait_ge(sem("degr"), 1)
            for tt in range(NT):
                dve.wait_ge(sem("agg0_done"), nth("agg0_done", tt + 1))
                dve.wait_ge(sem("base0"), NT + tt + 1)
                dve.scalar_tensor_tensor(out=base[:, tt, :], in0=bank[tt][:, :], scalar=degr[:, tt:tt + 1],
                                         in1=base[:, tt, :], op0=ALU.mult, op1=ALU.add).then_inc(sem("mixed0"), 1)
            for tt in range(NT):
                dve.wait_ge(sem("o_done"), nth("o_done", tt + 1))
                dve.wait_ge(sem("mixed0"), tt + 1)
                dve.tensor_tensor(xs[:, tt, :], bank[2 + tt][:, :], base[:, tt, :], ALU.add).then_inc(sem("x1"), 1)
                stats("ln1", x_tiles[tt], tt, "x1", tt + 1)
            for tt in range(NT):
                normalize("ln1", x_tiles[tt], tt, xn_tiles[tt])
            for tt in range(NT):
                dve.wait_ge(sem("ln1_full"), tt + 1)
                low("ln1", tile_of(xT_lo, tt), tile_of(fb, tt), tile_of(xT_hi, tt), tt + 1)

            def select(n, tt, k):
                w = (E0, E1)[n]
                dve.max(top[:, tt, :], lg[:, tt, 0:w]).then_inc(sem(f"top{n}"), 1)
                dve.wait_ge(sem(f"top{n}"), nth(f"top{n}", tt + 1))
                dve.tensor_scalar(wk[:, tt, 0:1], top[:, tt, 0:1], -1.0, None, ALU.mult).then_inc(sem(f"negmax{n}"), 1)
                dve.max_index(topi[:, tt, :], top[:, tt, :], lg[:, tt, 0:w]).then_inc(sem(f"topi{n}"), 1)
                dve.wait_ge(sem(f"topi{n}"), nth(f"topi{n}", tt + 1))
                dve.tensor_copy(topf[:, tt, 0:k], topi[:, tt, 0:k]).then_inc(sem(f"topf{n}"), 1)

            def spread_halves(n, b):
                dve.wait_ge(sem(f"comb{n}_turned"), nth(f"comb{n}_turned", 1))
                dve.tensor_scalar(combT16[64:P, :], b[64:P, 0:T], LO_SCALE, None, ALU.mult)\
                   .then_inc(sem(f"comb{n}_hi"), 1)
                dve.tensor_copy(combT16[0:64, :], b[0:64, 0:T])
                dve.wait_ge(sem(f"comb{n}_hi"), nth(f"comb{n}_hi", 1))
                dve.scalar_tensor_tensor(out=combT16[64:P, :], in0=b[64:P, 0:T], scalar=LO_SCALE,
                                         in1=combT16[64:P, :], op0=ALU.mult, op1=ALU.subtract)\
                   .then_inc(sem(f"comb{n}_16"), 1)
                dve.tensor_copy(combT[0:64, :], b[0:64, 0:T]).then_inc(sem(f"comb{n}_T"), 1)

            dve.wait_ge(sem("bg_in"), 16)
            dve.wait_ge(sem("lg0_done"), nth("lg0_done", 1))
            dve.tensor_tensor(lg[:, :, 0:E0], bank[4][:, 8:24].rearrange("p (t e) -> p t e", t=NT),
                              bgs[:, :].unsqueeze(1).to_broadcast([P, NT, E0]), ALU.add).then_inc(sem("lg0"), 1)
            dve.wait_ge(sem("lg0"), 1)
            dve.wait_ge(sem("iota2_made"), 1)
            for tt in range(NT):
                select(0, tt, 1)
            for tt in range(NT):
                dve.wait_ge(sem("sum0"), tt + 1)
                dve.reciprocal(wk[:, tt, 2:3], wk[:, tt, 1:2]).then_inc(sem("score0"), 1)
                dve.wait_ge(sem("score0"), tt + 1)
                dve.wait_ge(sem("topf0"), tt + 1)
                dve.tensor_scalar(comb[:, tt, :], iota2[:, :], topf[:, tt, 0:1], wk[:, tt, 2:3], ALU.is_equal,
                                  ALU.mult).then_inc(sem("comb0"), 1)
            spread_halves(0, bank[5])

            def hidden(tag, g, routed, lap=None):
                for j in range(2):
                    a = slice(j * 512, (j + 1) * 512)
                    o = slice((g % 2) * 1024 + j * 512, (g % 2) * 1024 + (j + 1) * 512)
                    dve.wait_ge(sem(f"{tag}_act"), at(nth(f"{tag}_act", 4 * g + 2 * j + 2), lap, 2 * BODY))
                    if g:
                        dve.wait_ge(sem(f"{tag}_act_lo"), at(nth(f"{tag}_act_lo", 2 * g - 1 + j), lap, BODY))
                    if routed:
                        n = g - (SHARED_GROUPS if tag == "ffn1" else 0)
                        dve.wait_ge(sem(f"{tag}_spread"), at(nth(f"{tag}_spread", 2 * n + j + 1), lap, BODY))
                        dve.tensor_tensor(fb[:, a], fa[:, a], bank[6 + j][:, :], ALU.mult)\
                           .then_inc(sem(f"{tag}_scaled"), 1)
                    else:
                        dve.tensor_scalar(fb[:, a], fa[:, a], SHARED_SCALE, None, ALU.mult)\
                           .then_inc(sem(f"{tag}_scaled"), 1)
                    dve.wait_ge(sem(f"{tag}_scaled"), at(nth(f"{tag}_scaled", 2 * g + j + 1), lap, BODY))
                    if g >= 2:
                        dve.wait_ge(sem(f"{tag}_down"), at(nth(f"{tag}_down", 2 * (g - 2) + j + 1), lap, BODY))
                    dve.tensor_copy(wide_hi[:, o], fb[:, a]).then_inc(sem(f"{tag}_act_hi"), 1)
                    dve.wait_ge(sem(f"{tag}_act_hi"), at(nth(f"{tag}_act_hi", 2 * g + j + 1), lap, BODY))
                    dve.tensor_tensor(wide_lo[:, o], fb[:, a], f32(wide_hi[:, o]), ALU.subtract)\
                       .then_inc(sem(f"{tag}_act_lo"), 1)

            hidden("ffn0", 0, True)
            for tt in range(NT):
                dve.wait_ge(sem("ffn0_out"), tt + 1)
                dve.tensor_tensor(xs[:, tt, :], bank[tt][:, :], xs[:, tt, :], ALU.add).then_inc(sem("x2"), 1)
                stats("ln2", x_tiles[tt], tt, "x2", tt + 1)
                if tt == 1:
                    low_turned("ln2", xT_lo, xT_hi, 0)
                normalize("ln2", x_tiles[tt], tt, xn_tiles[tt])
            low_turned("ln2", xT_lo, xT_hi, 1)
            for tt in range(NT):
                low("sup", pr_lo[:, tt * D:(tt + 1) * D], bank[tt][:, :], pr_hi[:, tt * D:(tt + 1) * D], tt + 1)
            dve.wait_ge(sem("cols_in"), 16)
            def negative_norms(n, name):
                dve.wait_ge(sem(f"{name}_norm"), 1)
                dve.tensor_scalar(nrm[:, n, 0:2], bank[7][:, 8 * n:8 * n + 2], -0.5, None,
                                  ALU.mult).then_inc(sem(f"{name}_nb"), 1)

            for name, n, f, sq, col in (("k1", 0, fa, flat(xn), COL_BK), ("q1", 1, fb, fa, COL_BQ)):
                for h in range(2):
                    dve.wait_ge(sem(f"{name}_done"), nth(f"{name}_done", h + 1))
                    for mm in range(2):
                        m = 2 * h + mm
                        dve.tensor_scalar(f[:, m * T:(m + 1) * T], bank[2 + 2 * n + h][:, mm * T:(mm + 1) * T],
                                          colsb[:, col + m:col + m + 1], None, ALU.add).then_inc(sem(f"{name}_f"), 1)
                for h in range(2):
                    a = slice(h * 512, (h + 1) * 512)
                    o = slice(n * 1024 + h * 512, n * 1024 + (h + 1) * 512)
                    low(name, wide_lo[:, o], f[:, a], wide_hi[:, o], h + 1)
                dve.wait_ge(sem(f"{name}_sq"), 2)
                dve.tensor_tensor(sq[:, 0:512], sq[:, 0:512], sq[:, 512:1024], ALU.add).then_inc(sem(f"{name}_sum"), 1)
                dve.wait_ge(sem(f"{name}_sum"), 1)
                dve.tensor_tensor(sq[:, 0:T], sq[:, 0:T], sq[:, T:2 * T], ALU.add).then_inc(sem(f"{name}_sum"), 1)
                if n:
                    negative_norms(0, "k1")

            def low_scaled(tag, lo, i, hi):
                dve.wait_ge(sem(f"{tag}_hi"), nth(f"{tag}_hi", 1))
                dve.scalar_tensor_tensor(out=lo, in0=i, scalar=M1 ** -0.5, in1=f32(hi), op0=ALU.mult,
                                         op1=ALU.subtract).then_inc(sem(f"{tag}_lo"), 1)

            low_scaled("kp", kf_lo[:, :], fb[:, 512:1024], kf_hi[:, :])
            dve.wait_ge(sem("v1_row_in"), 16)
            for tt in range(NT):
                dve.wait_ge(sem("v1_done"), nth("v1_done", tt + 1))
                dve.tensor_tensor(xn[:, tt, :], bank[4 + tt][:, :], rows[:, ROW_V1, :], ALU.add)\
                   .then_inc(sem("v1_f"), 1)
            for tt in range(NT):
                a = slice(tt * D, (tt + 1) * D)
                low("v1", v_lo[:, a], xn[:, tt, :], v_hi[:, a], tt + 1)
            negative_norms(1, "q1")
            low_scaled("qp", qf_lo[:, :], bank[3][:, :], qf_hi[:, :])
            for m in range(2):
                a = slice(m * D, (m + 1) * D)
                low("kv1", xT_lo[:, a], bank[(6, 2)[m]][:, :], xT_hi[:, a], m + 1)
            dve.wait_ge(sem("ksum1_done"), nth("ksum1_done", 1))
            for tt in range(NT):
                q = fb[:, tt * M1:(tt + 1) * M1]
                dve.tensor_tensor_reduce(q, q, bank[7][:, 0:M1], M1 ** -0.5, DENOM_EPS, ALU.mult, ALU.add,
                                         deg[:, tt:tt + 1]).then_inc(sem("den1"), 1)
            dve.wait_ge(sem("den1"), 2)
            dve.reciprocal(degr[:, :], deg[:, :]).then_inc(sem("denr1"), 1)
            for h in range(2):
                a = slice(h * 512, (h + 1) * 512)
                low("y1", v_lo[:, a], bank[4 + h][:, :], v_hi[:, a], h + 1)
            for tt in range(NT):
                dve.wait_ge(sem("agg1_done"), nth("agg1_done", tt + 1))
                dve.wait_ge(sem("base1"), 4)
                dve.tensor_tensor(base[:, tt, :], bank[tt][:, :], base[:, tt, :], ALU.add).then_inc(sem("mixed1"), 1)
            dve.wait_ge(sem("denr1"), 1)

            def affine(tag, g, b, tt):
                dve.wait_ge(sem(f"{tag}_turned"), nth(f"{tag}_turned", tt + 1))
                for kt in range(KT // 2):
                    dve.tensor_scalar(fb[:, kt * T + tt * P:kt * T + (tt + 1) * P],
                                      bank[6 + tt][:, kt * P:(kt + 1) * P], colsb[:, g + kt:g + kt + 1],
                                      colsb[:, b + kt:b + kt + 1], ALU.mult, ALU.add).then_inc(sem(f"{tag}_affine"), 1)

            for tt in range(NT):
                dve.wait_ge(sem("p1_done"), nth("p1_done", tt + 1))
                dve.wait_ge(sem("mixed1"), tt + 1)
                dve.scalar_tensor_tensor(out=xs[:, tt, :], in0=bank[2 + tt][:, :], scalar=degr[:, tt:tt + 1],
                                         in1=base[:, tt, :], op0=ALU.mult, op1=ALU.add).then_inc(sem("x3"), 1)
                stats("ln3", x_tiles[tt], tt, "x3", tt + 1)
                if tt == 1:
                    affine("ln4", COL_LN_G, COL_LN_B, 0)
                dve.wait_ge(sem("normed_rstd"), tt + 1)
                dve.tensor_scalar(xn[:, tt, :], xs[:, tt, :], mv[:, tt, 0:1], rstd2[:, tt:tt + 1], ALU.subtract,
                                  ALU.mult).then_inc(sem("ln4_xn"), 1)
            affine("ln4", COL_LN_G, COL_LN_B, 1)
            for tt in range(NT):
                low("ln4", tile_of(xT_lo, tt), tile_of(fb, tt), tile_of(xT_hi, tt), tt + 1)
            for tt in range(NT):
                normalize("ln3", x_tiles[tt], tt, fa_tiles[tt])
            dve.wait_ge(sem("lg1_done"), nth("lg1_done", 1))
            dve.tensor_scalar(lg[:, :, :], bank[5][:, 0:NT * E1].rearrange("p (t e) -> p t e", t=NT), 1.0 / TEMP,
                              None, ALU.mult).then_inc(sem("lg1"), 1)
            dve.wait_ge(sem("lg1"), 1)
            for tt in range(NT):
                select(1, tt, 2)
            for tt in range(NT):
                dve.wait_ge(sem("sum1"), tt + 1)
                dve.reciprocal(wk[:, tt, 4:5], wk[:, tt, 1:2]).then_inc(sem("score1"), 1)
                dve.wait_ge(sem("score1"), tt + 1)
                dve.tensor_scalar(wk[:, tt, 5:7], wk[:, tt, 2:4], wk[:, tt, 4:5], None, ALU.mult)\
                   .then_inc(sem("weights1"), 1)
                dve.wait_ge(sem("weights1"), tt + 1)
                dve.wait_ge(sem("topf1"), tt + 1)
                for k, c in enumerate((comb, comb2)):
                    dve.tensor_scalar(c[:, tt, :], iota2[:, :], topf[:, tt, k:k + 1], wk[:, tt, 5 + k:6 + k],
                                      ALU.is_equal, ALU.mult).then_inc(sem("picked"), 1)
                dve.wait_ge(sem("picked"), 2 * tt + 2)
                dve.tensor_tensor(comb[:, tt, :], comb[:, tt, :], comb2[:, tt, :], ALU.add).then_inc(sem("comb1"), 1)
            hidden("ffn1", 0, False)
            hidden("ffn1", 1, False)
            spread_halves(1, bank[4])
            with dve.Fori(0, LAPS) as lap:
                for g in (SHARED_GROUPS, SHARED_GROUPS + 1):
                    hidden("ffn1", g, True, lap)
            for tt in range(NT):
                dve.wait_ge(sem("ffn1_out"), tt + 1)
                dve.scalar_tensor_tensor(out=fa_tiles[tt], in0=rows[:, ROW_SH, :], scalar=SHARED_SCALE,
                                         in1=bank[tt][:, :], op0=ALU.mult, op1=ALU.add).then_inc(sem("hmoe"), 1)
                stats("ln5", fa_tiles[tt], tt, "hmoe", tt + 1)
                if tt == 1:
                    affine("ln5", COL_FF_G, COL_FF_B, 0)
                normalize("ln5", fa_tiles[tt], tt, xn_tiles[tt])
            low("ln5", tile_of(xT_lo, 0), tile_of(fb, 0), tile_of(xT_hi, 0), 1)
            affine("ln5", COL_FF_G, COL_FF_B, 1)
            low("ln5", tile_of(xT_lo, 1), tile_of(fb, 1), tile_of(xT_hi, 1), 2)
            for tt in range(NT):
                dve.wait_ge(sem("f2_done"), tt + 1)
                dve.wait_ge(sem("base3"), tt + 1)
                dve.tensor_tensor(xs[:, tt, :], bank[6 + tt][:, :], base[:, tt, :], ALU.add).then_inc(sem("y_done"), 1)


def blocks_of(m):
    return m.reshape(KT, P, -1).transpose(1, 0, 2).reshape(P, -1)


def kernel(**inputs):
    import concourse.bacc as bacc
    from concourse.bass_utils import run_bass_kernel_spmd

    w = {k: np.asarray(v) for k, v in inputs.items()}
    qkv0, qkv1 = w["L0_mix_W_qkv"], w["L1_mix_w_qkv"]
    blocks = [
        qkv0[:, 0:D].T, qkv0[:, D:2 * D].T, qkv0[:, 2 * D:], w["L0_gnn_W"].T, w["L0_mix_W_out"],
        w["L0_ffn_W1"].transpose(1, 0, 2).reshape(D, D), w["L0_ffn_W2"].reshape(D, D), w["L1_gnn_weight"],
        qkv1[0:D].T, qkv1[D:2 * D].T, qkv1[2 * D:].T, w["L1_mix_w_proj"].T,
    ]
    ws1, ws2, w1, w2 = w["L1_ffn_Ws1"], w["L1_ffn_Ws2"], w["L1_ffn_W1"], w["L1_ffn_W2"]
    for kind, g in FFN1_ORDER:
        if g < SHARED_GROUPS:
            blocks.append(ws1[:, g * D:(g + 1) * D] if kind == "up" else ws2[g * D:(g + 1) * D])
        else:
            e = slice((g - SHARED_GROUPS) * D // DFF, (g - SHARED_GROUPS + 1) * D // DFF)
            blocks.append(w1[e].transpose(1, 0, 2).reshape(D, D) if kind == "up" else w2[e].reshape(D, D))
    static = np.zeros((P, 2048), np.float32)
    static[:, ST_FEAT:ST_RF] = blocks_of(w["L1_mix_w_feat"].T)
    static[:, ST_RF:ST_RF + KT * P] = blocks_of(np.concatenate([w["L1_ffn_Wr"], w["L1_ffn_Wf1"]], 1))
    packed = [blocks_of(b) for b in blocks]
    packed.insert(RAW_STATIC, static)
    cols = np.zeros((P, COLS), np.float32)
    for at, v in ((COL_B1_0, w["L0_ffn_b1"]), (COL_LN_G, w["L1_ffn_ln1_g"]), (COL_LN_B, w["L1_ffn_ln1_b"]),
                  (COL_FF_G, w["L1_ffn_ffln_g"]), (COL_FF_B, w["L1_ffn_ffln_b"]), (COL_BK, w["L1_mix_b_qkv"][0:D]),
                  (COL_BQ, w["L1_mix_b_qkv"][D:2 * D]), (COL_B1, w["L1_ffn_bs1"]), (COL_B1 + 8, w["L1_ffn_b1"])):
        v = v.reshape(-1, P).T
        cols[:, at:at + v.shape[1]] = v
    cols[64:P, COL_BF1] = w["L1_ffn_bf1"]
    small = np.zeros((P, SMALL), np.float32)
    small[0:HD, 0:FD] = small[HD:P, FD:HD] = w["L0_mix_random_matrix"]
    small[:, SM_WG:] = blocks_of(w["L0_ffn_Wg"])
    arrays = {
        "x": w["x"], "src": w["src"].reshape(P, ET), "dst": w["dst"].reshape(P, ET),
        "ew": w["edge_weight"].reshape(P, ET), "stream": np.stack(packed), "cols": cols, "small": small,
        "bg": w["L0_ffn_bg"].reshape(1, E0),
        "rows0": np.stack([w["L0_gnn_b"], w["L0_mix_b_out"]]),
        "rows1": np.stack([w["L1_gnn_bias"], w["L1_mix_b_proj"], w["L1_mix_b_qkv"][2 * D:], w["L1_ffn_bs2"],
                           w["L1_ffn_bf2"]]),
        "codebook": w["L1_ffn_codebook"].T, "b2_0": w["L0_ffn_b2"], "b2_1": w["L1_ffn_b2"],
        "wf2": w["L1_ffn_Wf2"],
    }
    arrays = {k: np.ascontiguousarray(v) for k, v in arrays.items()}
    nc = bacc.Bacc("TRN2", target_bir_lowering=False, num_devices=1)
    aps = {k: nc.dram_tensor(k, v.shape, mybir.dt.from_np(v.dtype), kind="ExternalInput").ap()
           for k, v in arrays.items()}
    out = nc.dram_tensor("out", (T, D), F32, kind="ExternalOutput").ap()
    gnn_kernel(nc, out=out, **aps)
    r = run_bass_kernel_spmd(nc, [arrays], core_ids=[0])
    return r.results[0]["out"]
```
